# Optimizing a Trainium2 kernel written in Bass

```python
import numpy as np
import jax
import jax.numpy as jnp

def _softmax(x, axis=-1):
    return jax.nn.softmax(x, axis=axis)

def _gelu(x):
    return jax.nn.gelu(x, approximate=True)

def _silu(x):
    return jax.nn.silu(x)

def _sigmoid(x):
    return jax.nn.sigmoid(x)

def _layernorm(x, axis=-1, eps=1e-05):
    m = jnp.mean(x, axis=axis, keepdims=True)
    v = jnp.var(x, axis=axis, keepdims=True)
    return (x - m) / jnp.sqrt(v + eps)

def _scatter_add(tgt, idx, src, axis=0):
    return tgt.at[idx].add(src)

def _segment_sum(src, seg, n):
    return jax.ops.segment_sum(src, seg, n)
kernel_name = 'mk_perceiver_d1_seqx_r4_063c63'

def setup_inputs(seed: int=0):
    np.random.seed(seed)
    _w = jnp.asarray

    def _rec_inputs():
        import jax
        import jax.numpy as jnp
        _rk = jax.random.key(seed)
        x = -0.0002928 + 1 * jax.random.normal(jax.random.fold_in(_rk, 1), (4, 256, 256), jnp.float32)
        _lenS = 256 - jax.random.randint(jax.random.fold_in(_rk, 7), (4,), 0, max(1, 256 // 4) + 1, jnp.int32)
        _lenS2 = 4096 - jax.random.randint(jax.random.fold_in(_rk, 8), (4,), 0, max(1, 4096 // 4) + 1, jnp.int32)
        _ctx_1024P = jax.random.normal(jax.random.fold_in(_rk, 11), (4, 16, 256), jnp.float32)
        _ctx_1024c = jax.random.dirichlet(jax.random.fold_in(_rk, 511), 0.3 * jnp.ones((16,), jnp.float32), (4, 4096))
        _ctx_1024t = jnp.einsum('bsk,bkd->bsd', _ctx_1024c, _ctx_1024P)
        _ctx_1024t = _ctx_1024t * jax.lax.rsqrt(jnp.mean(jnp.square(_ctx_1024t)) + 1e-12) * 0.953939
        ctx_1024 = -1.39393e-06 + 0.999914 * (_ctx_1024t + 0.3 * jax.random.normal(jax.random.fold_in(_rk, 611), (4, 4096, 256), jnp.float32))
        _validS = jnp.arange(256)[None, :] < _lenS[:, None]
        _validS2 = jnp.arange(4096)[None, :] < _lenS2[:, None]
        _causal = jnp.tril(jnp.ones((256, 256), dtype=bool))
        mask_BxS2_bf0 = jnp.logical_not(jnp.ones((4, 4096), dtype=bool))
        return (x, ctx_1024, mask_BxS2_bf0)
    x, ctx_1024, mask_BxS2_bf0 = _rec_inputs()

    def _L0_xattn_setup():
        import jax, jax.numpy as jnp
        import numpy as np
        B, SQ, SKV, D, H = (2, 512, 512, 256, 16)
        HD = D // H

        def cross_attention(query, context, mask, Wq, bq, Wkv, bkv, Wout, bout, num_heads):
            b, sq, d = query.shape
            skv = context.shape[1]
            hd = d // num_heads
            scale = hd ** (-0.5)
            q = query @ Wq + bq
            kv = context @ Wkv + bkv
            kv = kv.reshape(b, skv, 2, num_heads, hd).transpose(2, 0, 3, 1, 4)
            k, v = (kv[0], kv[1])
            q = q.reshape(b, sq, num_heads, hd).transpose(0, 2, 1, 3)
            scores = jnp.einsum('bhid,bhjd->bhij', q, k) * scale
            scores = jnp.where(mask[:, None, None, :], -jnp.inf, scores)
            attn = jax.nn.softmax(scores, axis=-1)
            out = jnp.einsum('bhij,bhjd->bhid', attn, v)
            out = out.transpose(0, 2, 1, 3).reshape(b, sq, d)
            return out @ Wout + bout
        key = jax.random.key(seed)
        ks = jax.random.split(key, 6)
        scale = 1.0 / np.sqrt(D)
        return {'query': jax.random.normal(ks[0], (B, SQ, D), dtype=jnp.float32), 'context': jax.random.normal(ks[1], (B, SKV, D), dtype=jnp.float32), 'mask': jnp.zeros((B, SKV), dtype=bool), 'Wq': jax.random.normal(ks[2], (D, D), dtype=jnp.float32) * scale, 'bq': jnp.zeros((D,), dtype=jnp.float32), 'Wkv': jax.random.normal(ks[3], (D, 2 * D), dtype=jnp.float32) * scale, 'bkv': jnp.zeros((2 * D,), dtype=jnp.float32), 'Wout': jax.random.normal(ks[4], (D, D), dtype=jnp.float32) * scale, 'bout': jnp.zeros((D,), dtype=jnp.float32), 'num_heads': H}
    _L0_xattn_all = _L0_xattn_setup()
    _L0_xattn_in = {k: v for k, v in _L0_xattn_all.items() if k in ('Wq', 'bq', 'Wkv', 'bkv', 'Wout', 'bout')}
    del _L0_xattn_all

    def _L0_attn_setup():
        import jax, jax.numpy as jnp
        import numpy as np
        import math
        B, T, D, H = (4, 256, 256, 16)
        DK = D // H
        EPS = 1e-12
        key = jax.random.key(seed)
        ks = jax.random.split(key, 6)
        xav = math.sqrt(6.0 / (D + D))
        x = jax.random.normal(ks[0], (B, T, D), dtype=jnp.float32)
        Wq = jax.random.uniform(ks[1], (D, D), jnp.float32, -xav, xav)
        Wk = jax.random.uniform(ks[2], (D, D), jnp.float32, -xav, xav)
        Wv = jax.random.uniform(ks[3], (D, D), jnp.float32, -xav, xav)
        Wo = jax.random.uniform(ks[4], (D, D), jnp.float32, -xav, xav)
        logit_g = math.log(0.9 / 0.1)
        logit_l = math.log(0.1 / 0.9)
        W_gamma = jnp.zeros((H,), jnp.float32)
        b_gamma = jnp.full((H,), logit_g, jnp.float32)
        W_lambda = jnp.zeros((H,), jnp.float32)
        b_lambda = jnp.full((H,), logit_l, jnp.float32)
        return {'x': x, 'Wq': Wq, 'Wk': Wk, 'Wv': Wv, 'Wo': Wo, 'W_gamma': W_gamma, 'b_gamma': b_gamma, 'W_lambda': W_lambda, 'b_lambda': b_lambda}
    _L0_attn_all = _L0_attn_setup()
    _L0_attn_in = {k: v for k, v in _L0_attn_all.items() if k in ('Wq', 'Wk', 'Wv', 'Wo', 'W_gamma', 'b_gamma', 'W_lambda', 'b_lambda')}
    del _L0_attn_all

    def _L0_ffn_setup():
        import jax, jax.numpy as jnp
        import numpy as np
        DIM = 256
        INTER = 128
        E = 8
        TOP_K = 2
        ROUTE_SCALE = 1.0
        key = jax.random.key(seed)
        ks = jax.random.split(key, 8)
        s_d = 1.0 / np.sqrt(DIM)
        s_f = 1.0 / np.sqrt(INTER)
        x = jax.random.normal(ks[0], (2, 512, DIM), dtype=jnp.float32)
        gate_w = jax.random.uniform(ks[1], (E, DIM), jnp.float32, -s_d, s_d)
        wg = jax.random.uniform(ks[2], (E, INTER, DIM), jnp.float32, -s_d, s_d)
        wu = jax.random.uniform(ks[3], (E, INTER, DIM), jnp.float32, -s_d, s_d)
        wd = jax.random.uniform(ks[4], (E, DIM, INTER), jnp.float32, -s_f, s_f)
        sg = jax.random.uniform(ks[5], (INTER, DIM), jnp.float32, -s_d, s_d)
        su = jax.random.uniform(ks[6], (INTER, DIM), jnp.float32, -s_d, s_d)
        sd = jax.random.uniform(ks[7], (DIM, INTER), jnp.float32, -s_f, s_f)
        return {'x': x, 'gate_w': gate_w, 'wg': wg, 'wu': wu, 'wd': wd, 'sg': sg, 'su': su, 'sd': sd}
    _L0_ffn_all = _L0_ffn_setup()
    _L0_ffn_in = {k: v for k, v in _L0_ffn_all.items() if k in ('gate_w', 'wg', 'wu', 'wd', 'sg', 'su', 'sd')}
    del _L0_ffn_all
    return {'x': x, 'ctx_1024': ctx_1024, 'mask_BxS2_bf0': mask_BxS2_bf0, 'L0_xattn_Wq': _L0_xattn_in['Wq'], 'L0_xattn_bq': _L0_xattn_in['bq'], 'L0_xattn_Wkv': _L0_xattn_in['Wkv'], 'L0_xattn_bkv': _L0_xattn_in['bkv'], 'L0_xattn_Wout': _L0_xattn_in['Wout'], 'L0_xattn_bout': _L0_xattn_in['bout'], 'L0_attn_Wq': _L0_attn_in['Wq'], 'L0_attn_Wk': _L0_attn_in['Wk'], 'L0_attn_Wv': _L0_attn_in['Wv'], 'L0_attn_Wo': _L0_attn_in['Wo'], 'L0_attn_W_gamma': _L0_attn_in['W_gamma'], 'L0_attn_b_gamma': _L0_attn_in['b_gamma'], 'L0_attn_W_lambda': _L0_attn_in['W_lambda'], 'L0_attn_b_lambda': _L0_attn_in['b_lambda'], 'L0_ffn_gate_w': _L0_ffn_in['gate_w'], 'L0_ffn_wg': _L0_ffn_in['wg'], 'L0_ffn_wu': _L0_ffn_in['wu'], 'L0_ffn_wd': _L0_ffn_in['wd'], 'L0_ffn_sg': _L0_ffn_in['sg'], 'L0_ffn_su': _L0_ffn_in['su'], 'L0_ffn_sd': _L0_ffn_in['sd']}

def reference(x, ctx_1024, mask_BxS2_bf0, L0_xattn_Wq, L0_xattn_bq, L0_xattn_Wkv, L0_xattn_bkv, L0_xattn_Wout, L0_xattn_bout, L0_attn_Wq, L0_attn_Wk, L0_attn_Wv, L0_attn_Wo, L0_attn_W_gamma, L0_attn_b_gamma, L0_attn_W_lambda, L0_attn_b_lambda, L0_ffn_gate_w, L0_ffn_wg, L0_ffn_wu, L0_ffn_wd, L0_ffn_sg, L0_ffn_su, L0_ffn_sd):
    import jax
    import jax.numpy as jnp

    def _L0_xattn_ref(query, context, mask, Wq, bq, Wkv, bkv, Wout, bout, num_heads):
        import jax, jax.numpy as jnp
        import numpy as np
        B, SQ, SKV, D, H = (2, 512, 512, 256, 16)
        HD = D // H

        def cross_attention(query, context, mask, Wq, bq, Wkv, bkv, Wout, bout, num_heads):
            b, sq, d = query.shape
            skv = context.shape[1]
            hd = d // num_heads
            scale = hd ** (-0.5)
            q = query @ Wq + bq
            kv = context @ Wkv + bkv
            kv = kv.reshape(b, skv, 2, num_heads, hd).transpose(2, 0, 3, 1, 4)
            k, v = (kv[0], kv[1])
            q = q.reshape(b, sq, num_heads, hd).transpose(0, 2, 1, 3)
            scores = jnp.einsum('bhid,bhjd->bhij', q, k) * scale
            scores = jnp.where(mask[:, None, None, :], -jnp.inf, scores)
            attn = jax.nn.softmax(scores, axis=-1)
            out = jnp.einsum('bhij,bhjd->bhid', attn, v)
            out = out.transpose(0, 2, 1, 3).reshape(b, sq, d)
            return out @ Wout + bout
        return cross_attention(query, context, mask, Wq, bq, Wkv, bkv, Wout, bout, num_heads)

    def _L0_attn_ref(x, Wq, Wk, Wv, Wo, W_gamma, b_gamma, W_lambda, b_lambda):
        import jax, jax.numpy as jnp
        import numpy as np
        import math
        B, T, D, H = (4, 256, 256, 16)
        DK = D // H
        EPS = 1e-12
        b, t, d = x.shape

        def proj(W):
            return jnp.einsum('btd,ed->bte', x, W).reshape(b, t, H, DK).transpose(1, 0, 2, 3)
        q = proj(Wq)
        k = proj(Wk)
        v = proj(Wv)
        k = k / jnp.maximum(jnp.linalg.norm(k, axis=-1, keepdims=True), EPS)
        k_bar = k.mean(axis=-1)
        gamma = jax.nn.sigmoid(W_gamma * k_bar + b_gamma)
        lam = jax.nn.sigmoid(W_lambda * k_bar + b_lambda)
        rho = (1.0 - lam) * gamma
        S0 = jnp.zeros((b, H, DK, DK), x.dtype)

        def step(S, inp):
            q_t, k_t, v_t, rho_t = inp
            r = rho_t[..., None, None]
            S = r * S + (1.0 - r) * jnp.einsum('bhv,bhk->bhvk', v_t, k_t)
            y_t = jnp.einsum('bhv,bhvk->bhk', q_t, S)
            return (S, y_t)
        _, ys = jax.lax.scan(step, S0, (q, k, v, rho))
        out = ys.transpose(1, 0, 2, 3).reshape(b, t, d)
        return jnp.einsum('btd,ed->bte', out, Wo)

    def _L0_ffn_ref(x, gate_w, wg, wu, wd, sg, su, sd):
        import jax, jax.numpy as jnp
        import numpy as np
        DIM = 256
        INTER = 128
        E = 8
        TOP_K = 2
        ROUTE_SCALE = 1.0
        B, S, D = x.shape
        xf = x.reshape(-1, D)
        N = xf.shape[0]
        scores = jax.nn.softmax(xf @ gate_w.T, axis=-1)
        _, idx = jax.lax.top_k(scores, TOP_K)
        weights = jnp.take_along_axis(scores, idx, axis=-1) * ROUTE_SCALE
        cw = jnp.zeros((N, E), dtype=xf.dtype)
        cw = cw.at[jnp.arange(N)[:, None], idx].add(weights)
        g = jnp.einsum('nd,efd->nef', xf, wg)
        u = jnp.einsum('nd,efd->nef', xf, wu)
        h = jax.nn.silu(g) * u
        y = jnp.einsum('nef,edf->ned', h, wd)
        routed = jnp.einsum('ned,ne->nd', y, cw)
        shared = jax.nn.silu(xf @ sg.T) * (xf @ su.T) @ sd.T
        return (routed + shared).reshape(B, S, D)
    x = x + _L0_xattn_ref(_layernorm(x, axis=-1), ctx_1024, mask_BxS2_bf0, L0_xattn_Wq, L0_xattn_bq, L0_xattn_Wkv, L0_xattn_bkv, L0_xattn_Wout, L0_xattn_bout, 16)
    x = x + _L0_attn_ref(_layernorm(x, axis=-1), L0_attn_Wq, L0_attn_Wk, L0_attn_Wv, L0_attn_Wo, L0_attn_W_gamma, L0_attn_b_gamma, L0_attn_W_lambda, L0_attn_b_lambda)
    x = x + _L0_ffn_ref(_layernorm(x, axis=-1), L0_ffn_gate_w, L0_ffn_wg, L0_ffn_wu, L0_ffn_wd, L0_ffn_sg, L0_ffn_su, L0_ffn_sd)
    return x

_drawn_inputs = setup_inputs


def setup_inputs(seed=0):
    import zlib

    import numpy as np

    out = dict(_drawn_inputs(seed))
    spreads = {'L0_xattn_bq': (0.0, 0.351),
     'L0_xattn_bkv': (0.0, 0.1),
     'L0_xattn_bout': (0.0, 0.1),
     'L0_attn_W_gamma': (0.0, 0.8),
     'L0_attn_b_gamma': (2.1972246170043945, 0.2),
     'L0_attn_W_lambda': (0.0, 0.8),
     'L0_attn_b_lambda': (-2.1972246170043945, 0.2)}
    factors = {}
    for name, (base, spread) in spreads.items():
        noise = np.random.default_rng([zlib.crc32(name.encode()), seed]).standard_normal(out[name].shape)
        drawn = base * np.exp(spread * noise) if base else spread * noise
        out[name] = jnp.asarray(drawn.astype(out[name].dtype))
    for name, factor in factors.items():
        out[name] = (out[name] * factor).astype(out[name].dtype)
    return out
```

```python
from contextlib import ExitStack

import concourse.bass as bass
import concourse.mybir as mybir
from concourse.bass import ds

F32 = mybir.dt.float32
BF16 = mybir.dt.bfloat16
U8 = mybir.dt.uint8
ALU = mybir.AluOpType
ACT = mybir.ActivationFunctionType
AX = mybir.AxisListType

P = 128
B, T, D = 4, 256, 256
S = 4096
H, HD = 16, 16
NC = D // P
NQ = T // P
NT = B * NQ
CH = 512
NCH = S // CH
KT = S // P
ROWS = 6 * HD
UNITS = 8
TASKS = 16
HPB = 4
LEAD = 22
SCALE = HD ** -0.5
LN_EPS = 1e-5
NORM_EPS2 = 1e-24
E, F = 8, 128
WEIGHTS_LOADED = 16 * 16
KEY_STATS = 10
K_PARTS = (0, 0, 0, 1, 1, 2)
Q_PARTS = (2, 1, 0, 1, 0, 0)
LOADS = 12 * 16


def build(nc, x, ctx_, mask, Wq, bq, Wkv, bkv, Wout, bout, Aq, Ak, Av, Ao, W_g, b_g, W_l, b_l,
          gate_w, wg, wu, wd, sg, su, sd, out):
    with ExitStack() as top:
        sems = {}

        def sem(name):
            if name not in sems:
                sems[name] = top.enter_context(nc.semaphore(name))
            return sems[name]

        def sb(name, shape, dt=F32, scope=top):
            return scope.enter_context(nc.sbuf_tensor(name, shape, dt))

        ps = top.enter_context(nc.psum_tensor("ps", [P, 8, 512], F32))
        rho_dram = nc.dram_tensor("rho_scratch", [H, T], F32)

        x_sb = sb("x_sb", [P, NT, D])
        ident = sb("ident", [P, P])
        identb = sb("identb", [P, P], BF16)
        stats = sb("stats", [P, NT, 6])
        mv = sb("mv", [P, NT, 2])
        veps = sb("veps", [P, NT])
        rstd = sb("rstd", [P, NT])
        newt = sb("newt", [P, NT])
        mhalf = sb("mhalf", [P, 32])

        loop = ExitStack()
        wq_sb = sb("wq_sb", [P, NC, D], scope=loop)
        wkv_sb = sb("wkv_sb", [P, NC, 2 * D], scope=loop)
        wout_sb = sb("wout_sb", [P, NC, D], scope=loop)
        aqT = sb("aqT", [P, NC, H, 32], scope=loop)
        avT = sb("avT", [P, NC, H, 32], scope=loop)
        akT = sb("akT", [P, NC, D], scope=loop)
        aoT = sb("aoT", [P, NC, D], scope=loop)
        bq_col = sb("bq_col", [P, 2], scope=loop)
        bk_col = sb("bk_col", [P, 2], scope=loop)
        bv_bc = sb("bv_bc", [P, D], scope=loop)
        mrow = sb("mrow", [KT, B, P], BF16, scope=loop)
        gl_bc = sb("gl_bc", [P, 4, H], scope=loop)
        qp = sb("qp", [P, 2, 3, B * T], BF16, scope=loop)
        kslot = [sb(f"kslot{i}", [100, S], BF16, scope=loop) for i in range(4)]
        qslot = [sb(f"qslot{i}", [100, T], BF16, scope=loop) for i in range(4)]
        vslot = [sb(f"vslot{i}", [P, KT, HD + 1], scope=loop) for i in range(2)]
        pT = [sb(f"pT{i}", [P, 4, T], scope=loop) for i in range(2)]
        accS = sb("accS", [P, T], scope=loop)
        o_un = sb("o_un", [P, H * NQ * (HD + 1)], scope=loop)
        pm = sb("pm", [P, 2, NQ, UNITS], scope=loop)
        nm = sb("nm", [P, 2, NQ], scope=loop)
        nmr = sb("nmr", [P, NQ], scope=loop)
        mt = sb("mt", [P, 2, NQ, 4], BF16, scope=loop)
        o_un4 = o_un[:, :].rearrange("p (h q c) -> p q h c", h=H, q=NQ)

        starts = sb("starts", [P, HPB, T + P], scope=loop)
        ctx_raw = [sb(f"ctx_raw{i}", [P, 4, D], scope=loop) for i in range(2)]
        ctxT = [sb(f"ctxT{i}", [P, NC, CH], scope=loop) for i in range(2)]
        r1 = [sb(f"r1_{i}", [P, CH], scope=loop) for i in range(2)]

        setup = ExitStack()
        sxn = sb("sxn", [P, NT, D], scope=setup)
        sxnT = sb("sxnT", [P, NC, B * T], scope=setup)
        araw = sb("araw", [P, 4, NC, D], scope=setup)
        mask_u8 = sb("mask_u8", [KT, B, P], U8, scope=setup)
        bout_bc = sb("bout_bc", [P, D], scope=setup)
        setup.close()
        rec = ExitStack()
        dec = [sb(f"dec{i}", [P, HPB, T + P], scope=rec) for i in range(2)]
        on = sb("on", [P, NQ, D], scope=rec)
        oT = sb("oT", [P, NC, T], scope=rec)
        x1 = sb("x1", [P, NQ, D], scope=rec)
        xn = sb("xn", [P, NQ, D], scope=rec)
        xnT = sb("xnT", [P, NC, T], scope=rec)
        k_sb = sb("k_sb", [P, NQ, D], scope=rec)
        ksq = sb("ksq", [P, NQ, D], scope=rec)
        kk = sb("kk", [P, NQ, D], scope=rec)
        qv = sb("qv", [P, 4, 2, T], scope=rec)
        rden = sb("rden", [P, NQ, H], scope=rec)
        sm = {n: sb("sm_" + n, [P, NQ * H], scope=rec)
              for n in ("ss", "ks", "rn", "t", "kbar", "ug", "ul", "eg", "el", "den", "rho", "kscale")}
        rhoT = sb("rhoT", [NQ * H, P], scope=rec)
        y_sb = on
        yT = oT
        rows = sb("rows", [P, H, T + P], scope=rec)
        rec.close()
        kp = sb("kp", [P, 2, 3, S], BF16, scope=loop)
        vall = sb("vall", [P, H, KT, HD + 1], scope=loop)
        loop.close()

        moe = ExitStack()
        xn3 = sb("xn3", [P, NT, D], scope=moe)
        xn3T = sb("xn3T", [P, NC, B * T], scope=moe)
        g_raw = sb("g_raw", [E, D], scope=moe)
        gT = sb("gT", [P, NC, E], scope=moe)
        lower = sb("lower", [P, E, E], scope=moe)
        lg = sb("lg", [P, NT, E], scope=moe)
        pr = sb("pr", [P, NT, E], scope=moe)
        mx8 = sb("mx8", [P, NT], scope=moe)
        sum8 = sb("sum8", [P, NT], scope=moe)
        ahead = sb("ahead", [P, NT, E, E], scope=moe)
        tie = sb("tie", [P, NT, E, E], scope=moe)
        rank = sb("rank", [P, NT, E], scope=moe)
        cw = sb("cw", [P, E, NT], scope=moe)
        cwe = [sb(f"cwe{i}", [P, NT], scope=moe) for i in range(2)]
        wraw = [sb(f"wraw{i}", [P, 3, D], scope=moe) for i in range(2)]
        wT = [sb(f"wT{i}", [P, 3, D], scope=moe) for i in range(2)]
        silu = [sb(f"silu{i}", [P, 512], scope=moe) for i in range(2)]
        hT = [sb(f"hT{i}", [P, B * T], scope=moe) for i in range(2)]
        moe.close()

        block = top.enter_context(nc.Block())
        NCK = 2 * NCH

        @block.sync
        def _(sp):
            sp.dma_start(x_sb[:, :, :], x.rearrange("b (q p) d -> p (b q) d", p=P)).then_inc(sem("x_loaded"), 16)
            loads = [
                (wq_sb[:, :, :], Wq.rearrange("(c p) n -> p c n", p=P)),
                (wkv_sb[:, :, :], Wkv.rearrange("(c p) n -> p c n", p=P)),
                (wout_sb[:, :, :], Wout.rearrange("(c p) n -> p c n", p=P)),
                (bq_col[:, :], bq.rearrange("(g p) -> p g", p=P)),
                (bk_col[:, :], bkv[0:D].rearrange("(g p) -> p g", p=P)),
                (bv_bc[:, :], bkv[D:2 * D].partition_broadcast(P)),
                (bout_bc[:, :], bout.partition_broadcast(P)),
                (mask_u8[:, :, :], mask.rearrange("b (c k) -> c b k", k=P)),
            ] + [(gl_bc[:, i, :], w.partition_broadcast(P)) for i, w in enumerate((W_g, b_g, W_l, b_l))] \
              + [(araw[:, i, :, :], w.rearrange("(c p) n -> p c n", p=P)) for i, w in enumerate((Aq, Ak, Av, Ao))]
            for dst, src in loads:
                sp.dma_start(dst, src, allow_slow_non_contiguous=dst.shape[-1] == 2).then_inc(sem("weights_loaded"), 16)
            assert len(loads) * 16 == WEIGHTS_LOADED

            ctx_v = ctx_.rearrange("b (c t p) d -> p (b c) t d", p=P, t=4)
            with sp.Fori(0, B) as b:
                for c in range(NCH):
                    sp.wait_ge(sem("ctx_transposed"), b * NCH + (c + 1))
                    sp.dma_start(ctx_raw[c % 2][:, :, :], ctx_v[:, ds(b * NCH + c, 1), :, :].rearrange(
                        "p o t d -> p (o t) d")).then_inc(sem(f"ctx_loaded{c % 2}"), 16)
                sp.wait_ge(sem("k_low"), b * NCK + NCK)
                sp.wait_ge(sem("mask_ready"), 1)
                for s in range(4):
                    sp.dma_start(kslot[s][96:97, :].rearrange("o (c k) -> o c k", k=P),
                                 mrow[:, ds(b, 1), :].rearrange("c o k -> c (o k)")).then_inc(sem(f"k_loaded{s}"), 16)

                def load_keys(h):
                    slot, g, p0 = h % 4, h // 8, HD * (h % 8)
                    if h >= 4:
                        sp.wait_ge(sem("s2_done"), b * (H * UNITS) + (h - 3) * UNITS)
                    done = sem(f"k_loaded{slot}")
                    kd, qd = kslot[slot], qslot[slot]
                    for r, part in enumerate(K_PARTS):
                        sp.dma_start(kd[r * HD:(r + 1) * HD, :], kp[p0:p0 + HD, g, part, :]).then_inc(done, 16)
                    for r, part in enumerate(Q_PARTS):
                        sp.dma_start(qd[r * HD:(r + 1) * HD, :], qp[p0:p0 + HD, g, part, ds(b * T, T)]).then_inc(done, 16)

                def load_values(h):
                    if h < 2:
                        sp.wait_ge(sem("v_evacuated"), b * NCK + NCK)
                    else:
                        sp.wait_ge(sem("pv_done"), b * (H * UNITS) + (h - 1) * UNITS + 2)
                    sp.dma_start(vslot[h % 2][:, :, :], vall[:, h, :, :]).then_inc(sem(f"v_loaded{h % 2}"), 16)

                for h in range(4):
                    load_keys(h)
                load_values(0)
                load_values(1)
                for t in range(1, H - 1):
                    if t + 3 < H:
                        load_keys(t + 3)
                    load_values(t + 1)
                sp.wait_ge(sem("rhoT_ready"), b + 1)
                sp.dma_start(rho_dram[:, :].rearrange("h (q t) -> q h t", q=NQ),
                             rhoT[:, :]).then_inc(sem("rho_stored"), 16)
                sp.wait_ge(sem("rho_stored"), b * 16 + 16)
                for hg in range(4):
                    src = rho_dram[4 * hg:4 * hg + 4, :]
                    for dst, row in ((rows[:, 4 * hg:4 * hg + 4, 0:T], src), (rows[:, 4 * hg:4 * hg + 4, T:T + P], src[:, P:T])):
                        sp.dma_start(dst, row.partition_broadcast(P)).then_inc(sem(f"rows_loaded{hg}"), 16)

            sp.wait_ge(sem("x2_ready"), B)
            sp.dma_start(g_raw[:, :], gate_w).then_inc(sem("gate_loaded"), 16)

            def load_expert(i, buf, g3, u3, d3):
                sp.wait_ge(sem("w_transposed"), i + 1)
                done = sem(f"w_loaded{buf}")
                sp.dma_start(wraw[buf][:, 0, :], g3).then_inc(done, 16)
                sp.dma_start(wraw[buf][:, 1, :], u3).then_inc(done, 16)
                sp.dma_start(wraw[buf][:, 2, :].rearrange("p (c f) -> p c f", c=NC),
                             d3.rearrange("(c p) f -> p c f", p=P)).then_inc(done, 16)
            with sp.Fori(0, E // 2) as e2:
                for k in range(2):
                    e = e2 * 2 + k
                    load_expert(e, k, wg[ds(e, 1), :, :].rearrange("o f d -> (o f) d"),
                                wu[ds(e, 1), :, :].rearrange("o f d -> (o f) d"),
                                wd[ds(e, 1), :, :].rearrange("o d f -> (o d) f"))
            load_expert(E, 0, sg, su, sd)
            out_v = out.rearrange("b (q p) d -> p (b q) d", p=P)
            for q in range(4):
                sp.wait_ge(sem("down_read"), E * NT + 2 + (2 * q + 2))
                sp.dma_start(out_v[:, 2 * q:2 * q + 2, :], x_sb[:, 2 * q:2 * q + 2, :]).then_inc(sem("out_stored"), 16)
            sp.wait_ge(sem("out_stored"), 64)

        @block.gpsimd
        def _(pool):
            pool.sem_inc(sem("mt_parts"), 8)
            pool.memset(ident[:, :], 0.0).then_inc(sem("pool_const"), 1)
            pool.memset(identb[:, :], 0.0).then_inc(sem("pool_const"), 1)
            pool.memset(starts[:, :, :], 0.0).then_inc(sem("pool_const"), 1)
            pool.memset(mhalf[:, :], -0.5).then_inc(sem("pool_const"), 1)
            pool.memset(mt[:, :, :, :], 1.0).then_inc(sem("pool_const"), 1)
            pool.wait_ge(sem("pool_const"), 5)
            for m, pattern in ((ident[:, :], [[-1, P]]), (identb[:, :], [[-1, P]]),
                               (starts[:, :, 0:T], [[0, HPB], [-1, T]]), (starts[:, :, T:T + P], [[0, HPB], [-1, P]])):
                pool.affine_select(out=m, in_=m, compare_op=ALU.not_equal, fill=1.0, base=0, pattern=pattern,
                                   channel_multiplier=1).then_inc(sem("ident_ready"), 1)
            pool.wait_ge(sem("ident_ready"), 4)
            for s in range(4):
                pool.memset(kslot[s][96:100, :], 1.0).then_inc(sem("slot_ones"), 1)
                pool.wait_ge(sem("slot_ones"), 2 * s + 1)
                pool.memset(qslot[s][96:100, :], 1.0).then_inc(sem("slot_ones"), 1)
                pool.wait_ge(sem("slot_ones"), 2 * s + 2)
            pool.memset(vall[:, :, :, HD], 1.0).then_inc(sem("slot_ones"), 1)

            def inverse_root(name, dst, src, need, w):
                pool.wait_ge(sem(name + "_var"), need)
                pool.tensor_tensor(dst, src, mhalf[:, 0:w], ALU.pow).then_inc(sem(name + "_root"), 1)

            inverse_root("ln1", rstd[:, :], veps[:, :], 1, NT)
            with pool.Fori(0, B) as b:
                def split_max(Hn, par):
                    pool.wait_ge(sem("nm_ready"), Hn + 3)
                    pool.wait_ge(sem("mt_transposed"), Hn + 1)
                    pool.sem_inc(sem("pool_past"), 1)
                    part = sem("mt_parts")
                    pool.tensor_copy(mt[:, par, :, 1], nm[:, par, :]).then_inc(part, 1)
                    pool.wait_ge(part, Hn * 4 + 9)
                    pool.tensor_tensor(nmr[:, :], nm[:, par, :], mt[:, par, :, 1], ALU.subtract).then_inc(part, 1)
                    pool.wait_ge(part, Hn * 4 + 10)
                    pool.sem_inc(sem("pool_past"), 1)
                    pool.tensor_copy(mt[:, par, :, 2], nmr[:, :]).then_inc(part, 1)
                    pool.wait_ge(part, Hn * 4 + 11)
                    pool.tensor_tensor(mt[:, par, :, 3], nmr[:, :], mt[:, par, :, 2], ALU.subtract).then_inc(part, 1)
                with pool.Fori(0, H // 2) as g:
                    for k in range(2):
                        split_max(b * H + (g * 2 + k), k)
                inverse_root("ln2", rstd[:, 0:NQ], veps[:, 0:NQ], b + 1, NQ)
                inverse_root("kn", sm["rn"][:, :], sm["ss"][:, :], b + 1, NQ * H)
                pool.wait_ge(sem("scan_done"), b * 4 + 4)
                pool.sem_inc(sem("pool_past"), 1)
                pool.memset(vall[:, :, :, HD], 1.0).then_inc(sem("slot_ones"), 1)
            inverse_root("ln3", rstd[:, :], veps[:, :], 1, NT)
            pool.wait_ge(sem("x2_ready"), B)
            pool.memset(lower[:, :, :], 1.0).then_inc(sem("lower0"), 1)
            pool.wait_ge(sem("lower0"), 1)
            pool.affine_select(out=lower[:, :, :], in_=lower[:, :, :], compare_op=ALU.is_gt, fill=0.0, base=0,
                               pattern=[[1, E], [-1, E]], channel_multiplier=0).then_inc(sem("lower_ready"), 1)

        @block.tensor
        def _(pe):
            def transpose(dst, src, idt, **k):
                return pe.matmul(dst, src, idt, start=True, stop=True, is_transpose=True, **k)

            def transpose_all(name, src):
                for c in range(NC):
                    for half in range(2):
                        for i in range(4):
                            t = half * 4 + i
                            pe.wait_ge(sem(name + "_normed"), t + 1)
                            m = transpose(ps[:, 2 * c + half, i * P:(i + 1) * P], src[:, t, c * P:(c + 1) * P], ident[:, :])
                        m.then_inc(sem(name + "_turned"), 1)

            pe.sem_inc(sem("ctx_transposed"), 2)
            pe.sem_inc(sem("pv_done"), 2)
            pe.sem_inc(sem("accT_done"), 1)
            pe.sem_inc(sem("mt_transposed"), 2)
            pe.sem_inc(sem("w_transposed"), 2)
            pe.sem_inc(sem("down_done"), NT)
            pe.wait_ge(sem("ident_ready"), 4)
            transpose_all("ln1", sxn)
            pe.wait_ge(sem("weights_loaded"), WEIGHTS_LOADED)
            for i in range(4):
                for dc in range(NC):
                    for ec in range(NC):
                        m = transpose(ps[:, 4 + i, dc * D + ec * P:dc * D + (ec + 1) * P],
                                      araw[:, i, ec, dc * P:(dc + 1) * P], ident[:, :])
                m.then_inc(sem("a_turned"), 1)
            pe.wait_ge(sem("ln1T_ready"), 4)
            pe.wait_ge(sem("a_ready"), 4)
            for g in range(2):
                for half in range(2):
                    i = 2 * g + half
                    for c in range(NC):
                        m = pe.matmul(ps[:, 4 + i, :], wq_sb[:, c, g * P:(g + 1) * P],
                                      sxnT[:, c, half * 512:(half + 1) * 512], start=c == 0, stop=c == NC - 1)
                    m.then_inc(sem("q_proj"), 1)
            pe.wait_ge(sem("q_low"), 4)
            pe.wait_ge(sem("acc_zero"), 1)

            with pe.Fori(0, B) as b:
                def turn(c):
                    pe.wait_ge(sem(f"ctx_loaded{c % 2}"), b * (8 * NCH) + 16 * (c // 2 + 1))
                    if c:
                        pe.wait_ge(sem("ctxT_ready"), b * NCH + c)
                    for dc in range(NC):
                        for t in range(4):
                            m = transpose(ps[:, dc, t * P:(t + 1) * P], ctx_raw[c % 2][:, t, dc * P:(dc + 1) * P], ident[:, :])
                    m.then_inc(sem("ctx_transposed"), 1)

                def project(c):
                    pe.wait_ge(sem("ctxT_ready"), b * NCH + (c + 1))
                    for g in range(2):
                        if c:
                            pe.wait_ge(sem("k_rest"), b * NCK + (2 * c - 1 + g))
                        for dc in range(NC):
                            m = pe.matmul(ps[:, 2 + g, :], wkv_sb[:, dc, g * P:(g + 1) * P], ctxT[c % 2][:, dc, :],
                                          start=dc == 0, stop=dc == NC - 1)
                        m.then_inc(sem("k_proj"), 1)
                    for pair in range(2):
                        if c:
                            pe.wait_ge(sem("v_evacuated"), b * NCK + (2 * c - 1 + pair))
                        for j in range(2):
                            t = 2 * pair + j
                            for dc in range(NC):
                                m = pe.matmul(ps[:, 4 + pair, j * D:(j + 1) * D], ctxT[c % 2][:, dc, t * P:(t + 1) * P],
                                              wkv_sb[:, dc, D:2 * D], start=dc == 0, stop=dc == NC - 1)
                        m.then_inc(sem("v_proj"), 1)

                turn(0)
                for c in range(NCH):
                    if c + 1 < NCH:
                        turn(c + 1)
                    project(c)

                pe.wait_ge(sem("v_evacuated"), b * NCK + NCK)
                pe.wait_ge(sem("k_rest"), b * NCK + NCK)
                pe.wait_ge(sem("slot_ones"), b + 9)

                def max_task(H0, i, hh0):
                    hh, k = divmod(i, TASKS)
                    kc, qt = divmod(k, NQ)
                    slot = hh % 4
                    if k == 0:
                        pe.wait_ge(sem(f"k_loaded{slot}"), b * (4 * LOADS + 16) + hh0 * (LOADS // 4) + (16 + LOADS * (hh // 4 + 1)))
                    pe.wait_ge(sem("max_read"), H0 * TASKS + (i + 1))
                    pe.matmul(ps[:, 4 + i % 2, :], qslot[slot][0:ROWS + 1, qt * P:(qt + 1) * P],
                              kslot[slot][0:ROWS + 1, kc * 512:(kc + 1) * 512], start=True, stop=True
                              ).then_inc(sem("s1_done"), 1)

                def turn_max(H0, hh):
                    pe.wait_ge(sem("mt_parts"), H0 * 4 + (4 * hh + 12))
                    pe.wait_ge(sem("o_reduced"), H0 + (hh + 1))
                    bank = ps[96:100, 6 + hh % 2, 0:P].bitcast(BF16)
                    for qt in range(NQ):
                        m = transpose(bank[:, qt * P:(qt + 1) * P], mt[:, hh % 2, qt, :], identb[:, :], tile_position=(0, 96))
                    m.then_inc(sem("mt_transposed"), 1)

                def steps(H0, hh0, lo, hi, first=False, last=False):
                    for s in range(lo, hi):
                        hh, u = divmod(s, UNITS)
                        slot = hh % 4
                        live = not (last and s >= HPB * UNITS)
                        if live:
                            if u == 0:
                                pe.wait_ge(sem("qrow_ready"), H0 + (hh + 1))
                            pe.wait_ge(sem("exp_done"), H0 * UNITS + (s + 1))
                            for j in range(4):
                                kt = 4 * u + j
                                m = pe.matmul(ps[:, 2 * (s % 2) + j // 2, (j % 2) * T:(j % 2 + 1) * T],
                                              kslot[slot][:, kt * P:(kt + 1) * P], qslot[slot][:, :], start=True, stop=True)
                            m.then_inc(sem("s2_done"), 1)
                        tasks = [i for i in (LEAD + 2 * s, LEAD + 2 * s + 1) if not (last and i >= HPB * TASKS)]
                        if tasks:
                            max_task(H0, tasks[0], hh0)
                        if not (first and s == 0) and s <= (HPB * UNITS if last else hi):
                            weigh(H0, hh0, s - 1)
                        if tasks:
                            max_task(H0, tasks[1], hh0)
                        if u == 2 and not (first and hh == 0):
                            pe.wait_ge(sem("acc_copied"), H0 + hh)
                            for qt in range(NQ):
                                m = transpose(ps[:, 6 + (hh - 1) % 2, T + qt * P:T + (qt + 1) * P], accS[:, qt * P:(qt + 1) * P], ident[:, :])
                            m.then_inc(sem("accT_done"), 1)
                        if u == 6 and live and not (last and hh == HPB - 1):
                            turn_max(H0, hh + 1)

                def weigh(H0, hh0, s):
                    hh, u = divmod(s, UNITS)
                    pe.wait_ge(sem("exp_done"), H0 * UNITS + (s + 3))
                    if u == 0:
                        pe.wait_ge(sem("o_reduced"), H0 + (hh + 1))
                        pe.wait_ge(sem(f"v_loaded{hh % 2}"), b * (H * 8) + hh0 * 8 + 16 * (hh // 2 + 1))
                    for j in range(4):
                        m = pe.matmul(ps[32 * j:32 * j + HD + 1, 6 + hh % 2, 0:T], vslot[hh % 2][:, 4 * u + j, :],
                                      pT[s % 2][:, j, :], start=u == 0, stop=u == UNITS - 1, tile_position=(0, 32 * j))
                    m.then_inc(sem("pv_done"), 1)

                Hb = b * H
                for i in range(TASKS):
                    max_task(Hb, i, 0)
                for i in range(TASKS, LEAD):
                    max_task(Hb, i, 0)
                turn_max(Hb, 0)
                steps(Hb, 0, 0, 4, first=True)
                with pe.Fori(0, H // HPB - 1) as g:
                    steps(Hb + g * HPB, g * HPB, 4, 36)
                steps(Hb + (H - HPB), H - HPB, 4, 36, last=True)

                pe.wait_ge(sem("on_ready"), b + 1)
                for c in range(NC):
                    for qt in range(NQ):
                        m = transpose(ps[:, 0, c * T + qt * P:c * T + (qt + 1) * P], on[:, qt, c * P:(c + 1) * P], ident[:, :])
                m.then_inc(sem("on_turned"), 1)
                pe.wait_ge(sem("oT_ready"), b * 2 + 1)
                for qt in range(NQ):
                    for c in range(NC):
                        m = pe.matmul(ps[:, 1, qt * D:(qt + 1) * D], oT[:, c, qt * P:(qt + 1) * P], wout_sb[:, c, :],
                                      start=c == 0, stop=c == NC - 1)
                m.then_inc(sem("x_proj"), 1)
                pe.wait_ge(sem("ln2_normed"), b * NQ + NQ)
                for c in range(NC):
                    for qt in range(NQ):
                        m = transpose(ps[:, 2, c * T + qt * P:c * T + (qt + 1) * P], xn[:, qt, c * P:(c + 1) * P], ident[:, :])
                m.then_inc(sem("xn_turned"), 1)
                pe.wait_ge(sem("xnT_ready"), b + 1)
                for qt in range(NQ):
                    for c in range(NC):
                        m = pe.matmul(ps[:, 3, qt * D:(qt + 1) * D], xnT[:, c, qt * P:(qt + 1) * P], akT[:, c, :],
                                      start=c == 0, stop=c == NC - 1)
                m.then_inc(sem("rk_proj"), 1)
                for hg in range(4):
                    for i, w in enumerate((aqT, avT)):
                        for c in range(NC):
                            m = pe.matmul(ps[:, 4 + hg, i * T:(i + 1) * T],
                                          w[:, c, 4 * hg:4 * hg + 4, :].rearrange("p h e -> p (h e)"), xnT[:, c, :],
                                          start=c == 0, stop=c == NC - 1)
                    m.then_inc(sem("qv_proj"), 1)
                pe.wait_ge(sem("rho_ready"), b + 1)
                transpose(ps[0:NQ * H, 0, 0:P], sm["rho"][:, :], ident[:, :]).then_inc(sem("rho_turned"), 1)

                def affinity(m):
                    hg = m // 2
                    if m == 0:
                        pe.wait_ge(sem("qv_ready"), b * 4 + 4)
                    if m >= 3:
                        pe.wait_ge(sem("weighted"), b * 8 + (m - 2))
                    for j in range(2):
                        h = 2 * (m % 2) + j
                        r = slice(32 * h, 32 * h + HD)
                        bank = 1 + 2 * (m % 3) + j
                        pe.matmul(ps[:, bank, 0:T], qv[r, hg, 1, 0:P], qv[r, hg, 0, :],
                                  start=True, stop=True, tile_position=(32 * h, 0))
                        mm = pe.matmul(ps[:, bank, T:T + P], qv[r, hg, 1, P:T], qv[r, hg, 0, P:T],
                                       start=True, stop=True, tile_position=(32 * h, 0))
                        mm.then_inc(sem("affinity"), 1)

                def mix(m):
                    hg = m // 2
                    pe.wait_ge(sem("weighted"), b * 8 + (m + 1))
                    pe.wait_ge(sem("kk_ready"), b + 1)
                    for j in range(2):
                        h = 2 * (m % 2) + j
                        col = slice((4 * hg + h) * HD, (4 * hg + h + 1) * HD)
                        c1 = slice(D + col.start, D + col.stop)
                        w = dec[hg % 2]
                        pe.matmul(ps[:, 7, col], w[:, h, 0:P], kk[:, 0, col], start=True, stop=True)
                        pe.matmul(ps[:, 7, c1], w[:, h, P:T], kk[:, 0, col], start=True, stop=False)
                        mm = pe.matmul(ps[:, 7, c1], w[:, h, T:T + P], kk[:, 1, col], start=False, stop=True)
                    mm.then_inc(sem("mixed"), 1)

                affinity(0)
                affinity(1)
                for m in range(8):
                    if m + 2 < 8:
                        affinity(m + 2)
                    mix(m)
                pe.wait_ge(sem("y_ready"), b + 1)
                for c in range(NC):
                    for qt in range(NQ):
                        m = transpose(ps[:, 0, c * T + qt * P:c * T + (qt + 1) * P], y_sb[:, qt, c * P:(c + 1) * P], ident[:, :])
                m.then_inc(sem("y_turned"), 1)
                pe.wait_ge(sem("oT_ready"), b * 2 + 2)
                for qt in range(NQ):
                    for c in range(NC):
                        m = pe.matmul(ps[:, 1, qt * D:(qt + 1) * D], yT[:, c, qt * P:(qt + 1) * P], aoT[:, c, :],
                                      start=c == 0, stop=c == NC - 1)
                m.then_inc(sem("y_proj"), 1)
                pe.wait_ge(sem("x2_ready"), b + 1)

            transpose_all("ln3", xn3)
            pe.wait_ge(sem("gate_loaded"), 16)
            for c in range(NC):
                m = transpose(ps[:, 4, c * E:(c + 1) * E], g_raw[:, c * P:(c + 1) * P], ident[0:E, 0:E])
            m.then_inc(sem("gate_turned"), 1)
            pe.wait_ge(sem("gate_ready"), 1)
            pe.wait_ge(sem("ln3T_ready"), 4)
            for t in range(NT):
                for c in range(NC):
                    m = pe.matmul(ps[:, 5, t * E:(t + 1) * E], xn3T[:, c, t * P:(t + 1) * P], gT[:, c, :],
                                  start=c == 0, stop=c == NC - 1)
            m.then_inc(sem("logits"), 1)
            pe.wait_ge(sem("logits_read"), 1)

            def expert(e, k, nth):
                pe.wait_ge(sem(f"w_loaded{k}"), nth)
                pe.wait_ge(sem("wT_ready"), e * 2 + 2)
                for i in range(2):
                    for c in range(NC):
                        transpose(ps[:, 0, (2 * i + c) * P:(2 * i + c + 1) * P], wraw[k][:, i, c * P:(c + 1) * P], ident[:, :])
                for c in range(NC):
                    m = transpose(ps[:, 1, c * P:(c + 1) * P], wraw[k][:, 2, c * P:(c + 1) * P], ident[:, :])
                m.then_inc(sem("w_transposed"), 1)
                pe.wait_ge(sem("wT_ready"), e * 2 + 4)
                for half in range(2):
                    pe.wait_ge(sem("h_ready"), e * 2 + (half + 1))
                    for i in range(2):
                        for c in range(NC):
                            m = pe.matmul(ps[:, 2 + 2 * half + i, :], wT[k][:, i, c * P:(c + 1) * P],
                                          xn3T[:, c, half * 512:(half + 1) * 512], start=c == 0, stop=c == NC - 1)
                    m.then_inc(sem("gu_done"), 1)
                for t in range(NT):
                    pe.wait_ge(sem("h_ready"), e * 2 + (t // 4 + 3))
                    pe.wait_ge(sem("down_read"), e * NT + (t + 1))
                    pe.matmul(ps[:, 6 + t % 2, 0:D], hT[k][:, t * P:(t + 1) * P], wT[k][:, 2, :],
                              start=True, stop=True).then_inc(sem("down_done"), 1)

            with pe.Fori(0, E // 2) as e2:
                for k in range(2):
                    expert(e2 * 2 + k, k, e2 * 48 + 48)
            expert(E, 0, 48 * (E // 2 + 1))

        @block.scalar
        def _(act):
            def copy(dst, src):
                return act.activation(dst, src, ACT.Copy)

            act.sem_inc(sem("exp_done"), 2)
            act.sem_inc(sem("wT_ready"), 2)
            for i in range(4):
                act.wait_ge(sem("ln1_turned"), i + 1)
                copy(sxnT[:, i // 2, (i % 2) * 512:(i % 2 + 1) * 512], ps[:, i, :]).then_inc(sem("ln1T_ready"), 1)
            for i, dst in enumerate((aqT, akT, avT, aoT)):
                act.wait_ge(sem("a_turned"), i + 1)
                if i % 2 == 0:
                    act.wait_ge(sem("a_zero"), 2)
                    for dc in range(NC):
                        m = copy(dst[:, dc, :, 0:HD], ps[:, 4 + i, dc * D:(dc + 1) * D].rearrange("p (h e) -> p h e", e=HD))
                else:
                    m = copy(dst[:, :, :], ps[:, 4 + i, :].rearrange("p (c e) -> p c e", c=NC))
                m.then_inc(sem("a_ready"), 1)
            for i in range(4):
                g, half = divmod(i, 2)
                cols = slice(half * 512, (half + 1) * 512)
                act.wait_ge(sem("q_proj"), i + 1)
                act.activation(qp[:, g, 0, cols], ps[:, 4 + i, :], ACT.Identity, bias=bq_col[:, g:g + 1]).then_inc(sem("q_high"), 1)
                act.wait_ge(sem("q_rest"), i + 1)
                copy(qp[:, g, 1, cols], r1[i % 2][:, :]).then_inc(sem("q_mid"), 1)
            act.wait_ge(sem("a_ready"), 4)

            with act.Fori(0, B) as b:
                def evacuate(c):
                    act.wait_ge(sem("ctx_transposed"), b * NCH + (c + 3))
                    if c >= 2:
                        act.wait_ge(sem("v_proj"), b * NCK + 2 * (c - 1))
                    copy(ctxT[c % 2][:, :, :], ps[:, 0:2, :]).then_inc(sem("ctxT_ready"), 1)

                evacuate(0)
                for c in range(NCH):
                    cols = slice(c * CH, (c + 1) * CH)
                    if c + 1 < NCH:
                        evacuate(c + 1)
                    for g in range(2):
                        act.wait_ge(sem("k_proj"), b * NCK + (2 * c + g + 1))
                        act.activation(kp[:, g, 0, cols], ps[:, 2 + g, :], ACT.Identity, bias=bk_col[:, g:g + 1]).then_inc(sem("k_high"), 1)
                    for g in range(2):
                        act.wait_ge(sem("k_rest"), b * NCK + (2 * c + g + 1))
                        copy(kp[:, g, 1, cols], r1[g][:, :]).then_inc(sem("k_mid"), 1)

                def qrow(H0, hh):
                    act.wait_ge(sem("mt_transposed"), H0 + (hh + 3))
                    copy(qslot[hh % 4][96:100, :], ps[96:100, 6 + hh % 2, 0:P].bitcast(BF16)).then_inc(sem("qrow_ready"), 1)

                def steps(H0, lo, hi, first=False, last=False):
                    for s in range(lo, hi):
                        hh, u = divmod(s, UNITS)
                        live = not (last and s >= HPB * UNITS)
                        if live:
                            act.wait_ge(sem("s2_done"), H0 * UNITS + (s + 1))
                            act.wait_ge(sem("pv_done"), H0 * UNITS + (s + 1))
                            act.activation(pT[s % 2][:, :, :], ps[:, 2 * (s % 2):2 * (s % 2) + 2, :].rearrange(
                                "p a (j t) -> p (a j) t", j=2), ACT.Exp, scale=SCALE).then_inc(sem("exp_done"), 1)
                        if u == 0 and not (first and hh == 0):
                            act.wait_ge(sem("pv_done"), H0 * UNITS + (s + 2))
                            act.wait_ge(sem("accT_done"), H0 + hh)
                            copy(accS[:, :], ps[:, 6 + (hh - 1) % 2, 0:T]).then_inc(sem("acc_copied"), 1)
                        if u == 6 and live and not (last and hh == HPB - 1):
                            qrow(H0, hh + 1)

                Hb = b * H
                qrow(Hb, 0)
                steps(Hb, 0, 4, first=True)
                with act.Fori(0, H // HPB - 1) as g:
                    steps(Hb + g * HPB, 4, 36)
                steps(Hb + (H - HPB), 4, 36, last=True)

                act.wait_ge(sem("on_turned"), b + 1)
                copy(oT[:, :, :], ps[:, 0, :].rearrange("p (c t) -> p c t", c=NC)).then_inc(sem("oT_ready"), 1)
                act.wait_ge(sem("xn_turned"), b + 1)
                copy(xnT[:, :, :], ps[:, 2, :].rearrange("p (c t) -> p c t", c=NC)).then_inc(sem("xnT_ready"), 1)
                act.wait_ge(sem("rk_proj"), b + 1)
                copy(k_sb[:, :, :], ps[:, 3, :].rearrange("p (q e) -> p q e", q=NQ)).then_inc(sem("rk_ready"), 1)
                for hg in range(4):
                    act.wait_ge(sem("qv_proj"), b * 4 + (hg + 1))
                    copy(qv[:, hg, :, :], ps[:, 4 + hg, :].rearrange("p (i t) -> p i t", i=2)).then_inc(sem("qv_ready"), 1)
                act.wait_ge(sem("gates"), b * 2 + 2)
                act.activation(sm["eg"][:, :], sm["ug"][:, :], ACT.Exp, scale=-1.0).then_inc(sem("gate_exp"), 1)
                act.activation(sm["el"][:, :], sm["ul"][:, :], ACT.Exp).then_inc(sem("gate_exp"), 1)
                act.wait_ge(sem("rho_turned"), b + 1)
                copy(rhoT[:, :], ps[0:NQ * H, 0, 0:P]).then_inc(sem("rhoT_ready"), 1)
                act.wait_ge(sem("mixed"), b * 8 + 8)
                copy(y_sb[:, :, :], ps[:, 7, :].rearrange("p (q e) -> p q e", q=NQ)).then_inc(sem("y_ready"), 1)
                act.wait_ge(sem("y_turned"), b + 1)
                copy(yT[:, :, :], ps[:, 0, :].rearrange("p (c t) -> p c t", c=NC)).then_inc(sem("oT_ready"), 1)

            for i in range(4):
                act.wait_ge(sem("ln3_turned"), i + 1)
                copy(xn3T[:, i // 2, (i % 2) * 512:(i % 2 + 1) * 512], ps[:, i, :]).then_inc(sem("ln3T_ready"), 1)
            act.wait_ge(sem("gate_turned"), 1)
            copy(gT[:, :, :], ps[:, 4, 0:NC * E].rearrange("p (c e) -> p c e", c=NC)).then_inc(sem("gate_ready"), 1)
            act.wait_ge(sem("lg_shifted"), 1)
            act.activation(pr[:, :, :], lg[:, :, :], ACT.Exp).then_inc(sem("lg_exp"), 1)

            def expert(e, k):
                act.wait_ge(sem("w_transposed"), e + 3)
                act.wait_ge(sem("down_done"), e * NT + NT)
                copy(wT[k][:, 0:2, :], ps[:, 0, :].rearrange("p (i f) -> p i f", i=2)).then_inc(sem("wT_ready"), 1)
                copy(wT[k][:, 2, :], ps[:, 1, 0:D]).then_inc(sem("wT_ready"), 1)
                for half in range(2):
                    act.wait_ge(sem("gu_done"), e * 2 + (half + 1))
                    act.wait_ge(sem("h_ready"), e * 2 + (half + 1))
                    act.activation(silu[half][:, :], ps[:, 2 + 2 * half, :], ACT.Silu).then_inc(sem("silu_done"), 1)

            with act.Fori(0, E // 2) as e2:
                for k in range(2):
                    expert(e2 * 2 + k, k)
            expert(E, 0)

        @block.vector
        def _(dve):
            def normalise(name, n, src, dst, base, lane):
                for t in range(n):
                    dve.bn_stats(stats[:, t, :], src[:, t, :]).then_inc(sem(name + "_stats"), 1)
                dve.wait_ge(sem(name + "_stats"), base * n + n)
                dve.sem_inc(sem("dve_past"), 1)
                for t in range(n):
                    dve.bn_aggr(mv[:, t, :], stats[:, t, :]).then_inc(sem(name + "_aggr"), 1)
                dve.wait_ge(sem(name + "_aggr"), base * n + n)
                dve.tensor_scalar(veps[:, 0:n], mv[:, 0:n, 1], LN_EPS, None, ALU.add).then_inc(sem(name + "_var"), 1)
                refine(name, rstd[:, 0:n], veps[:, 0:n], newt[:, 0:n], base)
                for t in range(n):
                    dve.tensor_scalar(dst[:, t, :], src[:, t, :], mv[:, t, 0:1], rstd[:, t:t + 1], ALU.subtract,
                                      ALU.mult).then_inc(sem(name + "_normed"), 1)

            def refine(name, y, v, tmp, base):
                step = sem(name + "_newton")
                dve.wait_ge(sem(name + "_root"), base + 1)
                dve.tensor_tensor(tmp, y, y, ALU.mult).then_inc(step, 1)
                dve.wait_ge(step, base * 4 + 1)
                dve.tensor_tensor(tmp, tmp, v, ALU.mult).then_inc(step, 1)
                dve.wait_ge(step, base * 4 + 2)
                dve.tensor_scalar(tmp, tmp, -0.5, 1.5, ALU.mult, ALU.add).then_inc(step, 1)
                dve.wait_ge(step, base * 4 + 3)
                dve.tensor_tensor(y, y, tmp, ALU.mult).then_inc(step, 1)
                dve.wait_ge(step, base * 4 + 4)

            dve.sem_inc(sem("max_read"), 2)
            dve.sem_inc(sem("nm_ready"), 2)
            dve.sem_inc(sem("o_reduced"), 2)
            dve.sem_inc(sem("h_ready"), 2)
            dve.sem_inc(sem("down_read"), 2)
            for w in (aqT, avT):
                dve.memset(w[:, :, :, :], 0.0).then_inc(sem("a_zero"), 1)
            dve.wait_ge(sem("x_loaded"), 16)
            normalise("ln1", NT, x_sb, sxn, 0, 0)
            dve.wait_ge(sem("weights_loaded"), WEIGHTS_LOADED)
            dve.wait_ge(sem("ln1_normed"), NT)
            dve.tensor_tensor(x_sb[:, :, :], x_sb[:, :, :], bout_bc[:, :].unsqueeze(1).broadcast_to([P, NT, D]),
                              ALU.add).then_inc(sem("xb_ready"), 1)
            dve.tensor_scalar(mrow[:, :, :], mask_u8[:, :, :], -3e38, 10.0, ALU.mult, ALU.mult).then_inc(sem("mask_ready"), 1)
            for i in range(4):
                g, half = divmod(i, 2)
                cols = slice(half * 512, (half + 1) * 512)
                dve.wait_ge(sem("q_high"), i + 1)
                dve.scalar_tensor_tensor(out=r1[i % 2][:, :], in0=ps[:, 4 + i, :], scalar=bq_col[:, g:g + 1],
                                         in1=qp[:, g, 0, cols], op0=ALU.add, op1=ALU.subtract).then_inc(sem("q_rest"), 1)
                dve.wait_ge(sem("q_mid"), i + 1)
                dve.wait_ge(sem("q_rest"), i + 1)
                dve.tensor_tensor(qp[:, g, 2, cols], r1[i % 2][:, :], qp[:, g, 1, cols], ALU.subtract).then_inc(sem("q_low"), 1)
            dve.wait_ge(sem("q_rest"), 4)
            dve.wait_ge(sem("q_low"), 4)
            dve.memset(ps[:, 6:8, :], 0.0).then_inc(sem("acc_zero"), 1)

            with dve.Fori(0, B) as b:
                dve.wait_ge(sem("slot_ones"), b + 9)

                def values(c, pair):
                    dve.wait_ge(sem("v_proj"), b * NCK + (2 * c + pair + 1))
                    kt = 4 * c + 2 * pair
                    dve.tensor_tensor(vall[:, :, kt:kt + 2, 0:HD].rearrange("p h k e -> p k h e"),
                                      ps[:, 4 + pair, :].rearrange("p (k h e) -> p k h e", k=2, h=H),
                                      bv_bc[:, :].rearrange("p (h e) -> p h e", h=H).unsqueeze(1).broadcast_to([P, 2, H, HD]),
                                      ALU.add).then_inc(sem("v_evacuated"), 1)

                for c in range(NCH):
                    cols = slice(c * CH, (c + 1) * CH)
                    for g in range(2):
                        dve.wait_ge(sem("k_high"), b * NCK + (2 * c + g + 1))
                        if c:
                            dve.wait_ge(sem("k_low"), b * NCK + (2 * c - 1 + g))
                        dve.scalar_tensor_tensor(out=r1[g][:, :], in0=ps[:, 2 + g, :], scalar=bk_col[:, g:g + 1],
                                                 in1=kp[:, g, 0, cols], op0=ALU.add, op1=ALU.subtract).then_inc(sem("k_rest"), 1)
                    values(c, 0)
                    for g in range(2):
                        dve.wait_ge(sem("k_mid"), b * NCK + (2 * c + g + 1))
                        dve.wait_ge(sem("k_rest"), b * NCK + (2 * c + g + 1))
                        dve.tensor_tensor(kp[:, g, 2, cols], r1[g][:, :], kp[:, g, 1, cols], ALU.subtract).then_inc(sem("k_low"), 1)
                    values(c, 1)

                def max_task(H0, i):
                    hh, k = divmod(i, TASKS)
                    kc, qt = divmod(k, NQ)
                    par = hh % 2
                    if k == 0:
                        dve.wait_ge(sem("nm_ready"), H0 + (hh + 1))
                    dve.wait_ge(sem("s1_done"), H0 * TASKS + (i + 1))
                    dve.tensor_reduce(pm[:, par, qt, kc:kc + 1], ps[:, 4 + i % 2, :], AX.X, ALU.max).then_inc(sem("max_read"), 1)
                    if k == TASKS - 1:
                        dve.wait_ge(sem("max_read"), H0 * TASKS + (i + 3))
                        dve.wait_ge(sem("mt_parts"), H0 * 4 + (hh * 4 + 4))
                        dve.tensor_reduce(nm[:, par, :], pm[:, par, :, :], AX.X, ALU.max, negate=True).then_inc(sem("nm_ready"), 1)

                def steps(H0, g0, lo, hi, first=False, last=False):
                    for s in range(lo, hi):
                        hh, u = divmod(s, UNITS)
                        for i in (LEAD + 2 * s, LEAD + 2 * s + 1):
                            if not (last and i >= HPB * TASKS):
                                max_task(H0, i)
                        if u == 3 and not (first and hh == 0):
                            dve.wait_ge(sem("accT_done"), H0 + (hh + 1))
                            dst = o_un[:, ds(g0 * (NQ * (HD + 1)) + (hh - 1) * NQ * (HD + 1), NQ * (HD + 1))]
                            dve.tensor_reduce(dst.rearrange("p (q c) -> p q c", q=NQ),
                                              ps[:, 6 + (hh - 1) % 2, T:2 * T].rearrange("p (q j c) -> p q c j", q=NQ, j=4)[:, :, 0:HD + 1, :],
                                              AX.X, ALU.add).then_inc(sem("o_reduced"), 1)

                Hb = b * H
                for i in range(LEAD):
                    max_task(Hb, i)
                steps(Hb, 0, 0, 4, first=True)
                with dve.Fori(0, H // HPB - 1) as g:
                    steps(Hb + g * HPB, g * HPB, 4, 36)
                steps(Hb + (H - HPB), H - HPB, 4, 36, last=True)

                dve.wait_ge(sem("o_reduced"), b * H + (H + 2))
                dve.reciprocal(rden[:, :, :], o_un4[:, :, :, HD]).then_inc(sem("rden_ready"), 1)
                dve.wait_ge(sem("rden_ready"), b + 1)
                dve.tensor_tensor(on[:, :, :].rearrange("p q (h e) -> p q h e", h=H), o_un4[:, :, :, 0:HD],
                                  rden[:, :, :].unsqueeze(3).broadcast_to([P, NQ, H, HD]), ALU.mult).then_inc(sem("on_ready"), 1)
                dve.wait_ge(sem("x_proj"), b + 1)
                xs = x_sb[:, ds(b * NQ, NQ), :]
                dve.tensor_tensor(x1[:, :, :], ps[:, 1, :].rearrange("p (q e) -> p q e", q=NQ), xs, ALU.add).then_inc(sem("x1_ready"), 1)
                dve.wait_ge(sem("x1_ready"), b + 1)
                normalise("ln2", NQ, x1, xn, b, 0)

                dve.wait_ge(sem("rk_ready"), b + 1)
                st = sem("key_stat")
                n = [0]

                def chain(ins):
                    n[0] += 1
                    ins.then_inc(st, 1)
                    dve.wait_ge(st, b * KEY_STATS + n[0])

                hv = lambda t: t[:, :].rearrange("p (q h) -> p q h", q=NQ)
                bc = lambda i: gl_bc[:, i, :].unsqueeze(1).broadcast_to([P, NQ, H])
                kv_ = lambda t: t[:, :, :].rearrange("p q (h e) -> p (q h) e", h=H)
                chain(dve.tensor_tensor(ksq[:, :, :], k_sb[:, :, :], k_sb[:, :, :], ALU.mult))
                chain(dve.tensor_reduce(sm["ss"][:, :], kv_(ksq), AX.X, ALU.add))
                chain(dve.tensor_reduce(sm["ks"][:, :], kv_(k_sb), AX.X, ALU.add))
                dve.tensor_scalar(sm["ss"][:, :], sm["ss"][:, :], NORM_EPS2, None, ALU.max).then_inc(sem("kn_var"), 1)
                refine("kn", sm["rn"][:, :], sm["ss"][:, :], sm["t"][:, :], b)
                chain(dve.scalar_tensor_tensor(out=sm["kbar"][:, :], in0=sm["ks"][:, :], scalar=1.0 / HD, in1=sm["rn"][:, :],
                                               op0=ALU.mult, op1=ALU.mult))
                chain(dve.tensor_tensor(hv(sm["ug"]), hv(sm["kbar"]), bc(0), ALU.mult))
                chain(dve.tensor_tensor(hv(sm["ul"]), hv(sm["kbar"]), bc(2), ALU.mult))
                dve.tensor_tensor(hv(sm["ug"]), hv(sm["ug"]), bc(1), ALU.add).then_inc(sem("gates"), 1)
                dve.tensor_tensor(hv(sm["ul"]), hv(sm["ul"]), bc(3), ALU.add).then_inc(sem("gates"), 1)
                dve.wait_ge(sem("gate_exp"), b * 2 + 2)
                chain(dve.tensor_scalar(sm["den"][:, :], sm["eg"][:, :], 1.0, None, ALU.add))
                chain(dve.scalar_tensor_tensor(out=sm["den"][:, :], in0=sm["el"][:, :], scalar=1.0, in1=sm["den"][:, :],
                                               op0=ALU.add, op1=ALU.mult))
                dve.reciprocal(sm["rho"][:, :], sm["den"][:, :]).then_inc(sem("rho_ready"), 1)
                dve.wait_ge(sem("rho_ready"), b + 1)
                chain(dve.tensor_scalar(sm["t"][:, :], sm["rho"][:, :], -1.0, 1.0, ALU.mult, ALU.add))
                chain(dve.tensor_tensor(sm["kscale"][:, :], sm["t"][:, :], sm["rn"][:, :], ALU.mult))
                dve.tensor_tensor(kv_(kk), kv_(k_sb), sm["kscale"][:, :].unsqueeze(2).broadcast_to([P, NQ * H, HD]),
                                  ALU.mult).then_inc(sem("kk_ready"), 1)
                assert n[0] == KEY_STATS

                def scan(hg):
                    dve.wait_ge(sem(f"rows_loaded{hg}"), b * 32 + 32)
                    if hg >= 2:
                        dve.wait_ge(sem("mixed"), b * 8 + 2 * (hg - 1))
                    r = rows[:, 4 * hg:4 * hg + 4, :]
                    dve.memset(r[:, :, 0:T + 1:T], 0.0).then_inc(sem("rows_cut"), 1)
                    dve.wait_ge(sem("rows_cut"), b * 4 + (hg + 1))
                    flat = lambda t: t.rearrange("p h t -> p (h t)")
                    dve.tensor_tensor_scan(flat(dec[hg % 2][:, :, :]), flat(r), flat(starts[:, :, :]), 0.0,
                                           ALU.mult, ALU.add).then_inc(sem("scan_done"), 1)

                def weight(m):
                    hg, bank = m // 2, 1 + 2 * (m % 3)
                    dve.wait_ge(sem("affinity"), b * 16 + 2 * (m + 1))
                    dve.wait_ge(sem("scan_done"), b * 4 + (hg + 1))
                    w = dec[hg % 2][:, 2 * (m % 2):2 * (m % 2) + 2, :]
                    dve.tensor_tensor(w, w, ps[:, bank:bank + 2, 0:T + P], ALU.mult).then_inc(sem("weighted"), 1)

                for hg in range(4):
                    scan(hg)
                    weight(2 * hg)
                    weight(2 * hg + 1)
                dve.wait_ge(sem("y_proj"), b + 1)
                dve.tensor_tensor(xs, ps[:, 1, :].rearrange("p (q e) -> p q e", q=NQ), x1[:, :, :], ALU.add).then_inc(sem("x2_ready"), 1)

            dve.wait_ge(sem("x2_ready"), B)
            normalise("ln3", NT, x_sb, xn3, 0, 0)
            st = sem("route")
            n = [0]

            def chain(ins):
                n[0] += 1
                ins.then_inc(st, 1)
                dve.wait_ge(st, n[0])

            dve.wait_ge(sem("logits"), 1)
            dve.tensor_copy(lg[:, :, :], ps[:, 5, 0:NT * E].rearrange("p (t e) -> p t e", e=E)).then_inc(sem("logits_read"), 1)
            dve.wait_ge(sem("logits_read"), 1)
            over_e = lambda t: t[:, :].unsqueeze(2).broadcast_to([P, NT, E])
            chain(dve.tensor_reduce(mx8[:, :], lg[:, :, :], AX.X, ALU.max))
            dve.tensor_tensor(lg[:, :, :], lg[:, :, :], over_e(mx8), ALU.subtract).then_inc(sem("lg_shifted"), 1)
            dve.wait_ge(sem("lg_exp"), 1)
            chain(dve.tensor_reduce(sum8[:, :], pr[:, :, :], AX.X, ALU.add))
            chain(dve.reciprocal(sum8[:, :], sum8[:, :]))
            chain(dve.tensor_tensor(pr[:, :, :], pr[:, :, :], over_e(sum8), ALU.mult))
            other = lambda t: pr[:, t, :].unsqueeze(1).broadcast_to([P, E, E])
            own = lambda t: pr[:, t, :].unsqueeze(2).broadcast_to([P, E, E])
            dve.wait_ge(sem("lower_ready"), 1)
            for t in range(NT):
                dve.tensor_tensor(ahead[:, t, :, :], other(t), own(t), ALU.is_gt).then_inc(sem("ahead"), 1)
                dve.tensor_tensor(tie[:, t, :, :], other(t), own(t), ALU.is_equal).then_inc(sem("ahead"), 1)
            dve.wait_ge(sem("ahead"), 2 * NT)
            flat2 = lambda t: t[:, :, :, :].rearrange("p t e f -> p t (e f)")
            chain(dve.tensor_tensor(flat2(tie), flat2(tie), lower[:, :, :].rearrange("p e f -> p (e f)").unsqueeze(1).broadcast_to([P, NT, E * E]), ALU.mult))
            chain(dve.tensor_tensor(flat2(ahead), flat2(ahead), flat2(tie), ALU.add))
            chain(dve.tensor_reduce(rank[:, :, :], ahead[:, :, :, :], AX.X, ALU.add))
            chain(dve.scalar_tensor_tensor(out=cw[:, :, :].rearrange("p e t -> p t e"), in0=rank[:, :, :], scalar=1.5,
                                           in1=pr[:, :, :], op0=ALU.is_lt, op1=ALU.mult))

            def expert(e, k, shared=False):
                if not shared:
                    dve.wait_ge(sem("down_read"), e * NT + 2)
                    dve.tensor_copy(cwe[k][:, :], cw[:, ds(e, 1), :].rearrange("p o t -> p (o t)")).then_inc(sem("cwe_ready"), 1)
                for half in range(2):
                    dve.wait_ge(sem("silu_done"), e * 2 + (half + 1))
                    dve.wait_ge(sem("down_done"), e * NT + NT)
                    dve.tensor_tensor(hT[k][:, half * 512:(half + 1) * 512], silu[half][:, :], ps[:, 3 + 2 * half, :],
                                      ALU.mult).then_inc(sem("h_ready"), 1)
                for t in range(NT):
                    dve.wait_ge(sem("down_done"), e * NT + (NT + t + 1))
                    if not shared:
                        if t == 0:
                            dve.wait_ge(sem("cwe_ready"), e + 1)
                        dve.scalar_tensor_tensor(out=x_sb[:, t, :], in0=ps[:, 6 + t % 2, 0:D], scalar=cwe[k][:, t:t + 1],
                                                 in1=x_sb[:, t, :], op0=ALU.mult, op1=ALU.add).then_inc(sem("down_read"), 1)
                    else:
                        dve.tensor_tensor(x_sb[:, t, :], x_sb[:, t, :], ps[:, 6 + t % 2, 0:D], ALU.add).then_inc(sem("down_read"), 1)

            with dve.Fori(0, E // 2) as e2:
                for k in range(2):
                    expert(e2 * 2 + k, k)
            expert(E, 0, shared=True)


_INS = ['x', 'ctx_1024', 'mask_BxS2_bf0', 'L0_xattn_Wq', 'L0_xattn_bq', 'L0_xattn_Wkv', 'L0_xattn_bkv', 'L0_xattn_Wout',
        'L0_xattn_bout', 'L0_attn_Wq', 'L0_attn_Wk', 'L0_attn_Wv', 'L0_attn_Wo', 'L0_attn_W_gamma', 'L0_attn_b_gamma',
        'L0_attn_W_lambda', 'L0_attn_b_lambda', 'L0_ffn_gate_w', 'L0_ffn_wg', 'L0_ffn_wu', 'L0_ffn_wd', 'L0_ffn_sg',
        'L0_ffn_su', 'L0_ffn_sd']


def kernel(**inputs):
    import numpy as np
    import concourse.bacc as bacc
    from concourse.bass_utils import run_bass_kernel_spmd

    nc = bacc.Bacc("TRN2", target_bir_lowering=False, num_devices=1)
    arrays, args = {}, []
    for name in _INS:
        a = np.ascontiguousarray(inputs[name])
        arrays[f"in_{name}_dram"] = a
        args.append(nc.dram_tensor(f"in_{name}_dram", a.shape, mybir.dt.from_np(a.dtype), kind="ExternalInput").ap())
    o = nc.dram_tensor("out_0_dram", (B, T, D), F32, kind="ExternalOutput").ap()
    build(nc, *args, o)
    r = run_bass_kernel_spmd(nc, [arrays], core_ids=[0])
    return r.results[0]["out_0_dram"]
```

```python
from contextlib import ExitStack

import concourse.bass as bass
import concourse.mybir as mybir
from concourse.bass import ds

F32 = mybir.dt.float32
BF16 = mybir.dt.bfloat16
U8 = mybir.dt.uint8
ALU = mybir.AluOpType
ACT = mybir.ActivationFunctionType
AX = mybir.AxisListType

P = 128
B, T, D = 4, 256, 256
S = 4096
H, HD = 16, 16
NC = D // P
NQ = T // P
NT = B * NQ
CH = 512
NCH = S // CH
KT = S // P
ROWS = 6 * HD
UNITS = 8
TASKS = 16
HPB = 4
LEAD = 22
SCALE = HD ** -0.5
LN_EPS = 1e-5
NORM_EPS2 = 1e-24
E, F = 8, 128
WEIGHTS_LOADED = 12 * 16
KEY_STATS = 10
K_PARTS = (0, 0, 0, 1, 1, 2)
Q_PARTS = (2, 1, 0, 1, 0, 0)
CTXT = 3
HALF = S // 2
FIRST = list(range(8)) + list(range(16, 22)) + list(range(8, 16))
EARLY_TASKS = {5: (0, 5), 6: (5, 10), 7: (10, 14)}
EARLY = 14
FIRST_LOADS = (1 + 6 + 6) * 16
LOADS = 12 * 16


def build(nc, x, ctx_, mask, Wq, bq, Wkv, bkv, Wout, bout, Aq, Ak, Av, Ao, W_g, b_g, W_l, b_l,
          gate_w, wg, wu, wd, sg, su, sd, out):
    with ExitStack() as top:
        sems = {}

        def sem(name):
            if name not in sems:
                sems[name] = top.enter_context(nc.semaphore(name))
            return sems[name]

        def sb(name, shape, dt=F32, scope=top):
            return scope.enter_context(nc.sbuf_tensor(name, shape, dt))

        ps = top.enter_context(nc.psum_tensor("ps", [P, 8, 512], F32))
        rho_dram = nc.dram_tensor("rho_scratch", [B, H, T], F32)

        x_sb = sb("x_sb", [P, NT, D])
        on = sb("on", [P, NT, D])
        ident = sb("ident", [P, P])
        identb = sb("identb", [P, P], BF16)
        stats = sb("stats", [P, NT, 6])
        mv = sb("mv", [P, NT, 2])
        veps = sb("veps", [P, NT])
        rstd = sb("rstd", [P, NT])
        newt = sb("newt", [P, NT])
        mhalf = sb("mhalf", [P, NT * H])
        gl_bc = sb("gl_bc", [P, 4, H])
        wout_sb = sb("wout_sb", [P, NC, D])

        loop = ExitStack()
        wq_sb = sb("wq_sb", [P, NC, D], scope=loop)
        wkv_sb = sb("wkv_sb", [P, NC, 2 * D], scope=loop)
        bq_col = sb("bq_col", [P, 2], scope=loop)
        bk_col = sb("bk_col", [P, 2], scope=loop)
        bv_bc = sb("bv_bc", [P, D], scope=loop)
        mrow = sb("mrow", [KT, B, P], BF16, scope=loop)
        qp = sb("qp", [P, 2, 3, B * T], BF16, scope=loop)
        kslot = [sb(f"kslot{i}", [100, S], BF16, scope=loop) for i in range(4)]
        qslot = [sb(f"qslot{i}", [100, T], BF16, scope=loop) for i in range(4)]
        vslot = [sb(f"vslot{i}", [P, KT, HD + 1], scope=loop) for i in range(2)]
        pT = [sb(f"pT{i}", [P, 4, T], scope=loop) for i in range(2)]
        accS = sb("accS", [P, T], scope=loop)
        o_un = sb("o_un", [P, H * NQ * (HD + 1)], scope=loop)
        rden = sb("rden", [P, NQ, H], scope=loop)
        pm = sb("pm", [P, 2, NQ, UNITS], scope=loop)
        nm = sb("nm", [P, 2, NQ], scope=loop)
        nmr = sb("nmr", [P, NQ], scope=loop)
        mt = sb("mt", [P, 2, NQ, 4], BF16, scope=loop)
        o_un4 = o_un[:, :].rearrange("p (h q c) -> p q h c", h=H, q=NQ)
        ctx_raw = [sb(f"ctx_raw{i}", [P, 4, D], scope=loop) for i in range(2)]
        ctxT = [sb(f"ctxT{i}", [P, NC, CH], scope=loop) for i in range(CTXT)]
        r1 = [sb(f"r1_{i}", [P, CH], scope=loop) for i in range(2)]
        setup = ExitStack()
        sxn = sb("sxn", [P, NT, D], scope=setup)
        sxnT = sb("sxnT", [P, NC, B * T], scope=setup)
        mask_u8 = sb("mask_u8", [KT, B, P], U8, scope=setup)
        bout_bc = sb("bout_bc", [P, D], scope=setup)
        setup.close()
        kp = sb("kp", [P, 2, 3, S], BF16, scope=loop)
        vall = sb("vall", [P, H, KT, HD + 1], scope=loop)
        loop.close()

        rec = ExitStack()
        araw = sb("araw", [P, 4, NC, D], scope=rec)
        aqT = sb("aqT", [P, NC, H, 32], scope=rec)
        avT = sb("avT", [P, NC, H, 32], scope=rec)
        akT = sb("akT", [P, NC, D], scope=rec)
        aoT = sb("aoT", [P, NC, D], scope=rec)
        onT = sb("onT", [P, NC, B * T], scope=rec)
        xn2 = sb("xn2", [P, NT, D], scope=rec)
        xn2T = sb("xn2T", [P, NC, B * T], scope=rec)
        k_sb = sb("k_sb", [P, NT, D], scope=rec)
        kk = sb("kk", [P, NT, D], scope=rec)
        kkb = [sb(f"kkb{i}", [P, NQ, D], scope=rec) for i in range(2)]
        ksq = xn2
        sm = {n: sb("sm_" + n, [P, NT * H], scope=rec)
              for n in ("ss", "ks", "rn", "t", "kbar", "ug", "ul", "eg", "el", "den", "rho", "kscale")}
        rhoT = sb("rhoT", [NT * H, P], scope=rec)
        starts = sb("starts", [P, HPB, T + P], scope=rec)
        rows = [sb(f"rows{i}", [P, H, T + P], scope=rec) for i in range(2)]
        dec = [sb(f"dec{i}", [P, HPB, T + P], scope=rec) for i in range(4)]
        qd = [sb(f"qd{i}", [P, HPB, T], scope=rec) for i in range(4)]
        vT = [sb(f"vT{i}", [P, T], scope=rec) for i in range(4)]
        y_sb = sb("y_sb", [P, NT, D], scope=rec)
        yT = onT
        rec.close()

        moe = ExitStack()
        xn3 = sb("xn3", [P, NT, D], scope=moe)
        xn3T = sb("xn3T", [P, NC, B * T], scope=moe)
        g_raw = sb("g_raw", [E, D], scope=moe)
        gT = sb("gT", [P, NC, E], scope=moe)
        lower = sb("lower", [P, E, E], scope=moe)
        lg = sb("lg", [P, NT, E], scope=moe)
        pr = sb("pr", [P, NT, E], scope=moe)
        mx8 = sb("mx8", [P, NT], scope=moe)
        sum8 = sb("sum8", [P, NT], scope=moe)
        ahead = sb("ahead", [P, NT, E, E], scope=moe)
        tie = sb("tie", [P, NT, E, E], scope=moe)
        rank = sb("rank", [P, NT, E], scope=moe)
        cw = sb("cw", [P, E, NT], scope=moe)
        cwe = [sb(f"cwe{i}", [P, NT], scope=moe) for i in range(2)]
        wraw = [sb(f"wraw{i}", [P, 3, D], scope=moe) for i in range(2)]
        wT = [sb(f"wT{i}", [P, 3, D], scope=moe) for i in range(2)]
        silu = [sb(f"silu{i}", [P, 512], scope=moe) for i in range(2)]
        hT = [sb(f"hT{i}", [P, B * T], scope=moe) for i in range(2)]
        moe.close()

        K_LOADED = [3 * LOADS + LOADS // 2] * 2 + [4 * LOADS] * 2

        def value_bank(c, pair):
            return (0 if c == NCH - 1 else 4) + pair

        block = top.enter_context(nc.Block())
        NCK = 2 * NCH

        @block.sync
        def _(sp):
            sp.dma_start(x_sb[:, :, :], x.rearrange("b (q p) d -> p (b q) d", p=P)).then_inc(sem("x_loaded"), 16)
            loads = [
                (wq_sb[:, :, :], Wq.rearrange("(c p) n -> p c n", p=P)),
                (wkv_sb[:, :, :], Wkv.rearrange("(c p) n -> p c n", p=P)),
                (wout_sb[:, :, :], Wout.rearrange("(c p) n -> p c n", p=P)),
                (bq_col[:, :], bq.rearrange("(g p) -> p g", p=P)),
                (bk_col[:, :], bkv[0:D].rearrange("(g p) -> p g", p=P)),
                (bv_bc[:, :], bkv[D:2 * D].partition_broadcast(P)),
                (bout_bc[:, :], bout.partition_broadcast(P)),
                (mask_u8[:, :, :], mask.rearrange("b (c k) -> c b k", k=P)),
            ] + [(gl_bc[:, i, :], w.partition_broadcast(P)) for i, w in enumerate((W_g, b_g, W_l, b_l))]
            for dst, src in loads:
                sp.dma_start(dst, src, allow_slow_non_contiguous=dst.shape[-1] == 2).then_inc(sem("weights_loaded"), 16)
            assert len(loads) * 16 == WEIGHTS_LOADED

            ctx_v = ctx_.rearrange("b (c t p) d -> p (b c) t d", p=P, t=4)
            with sp.Fori(0, B) as b:
                def key_rows(h, lo, hi, done):
                    slot, g, p0 = h % 4, h // 8, HD * (h % 8)
                    for r, part in enumerate(K_PARTS):
                        sp.dma_start(kslot[slot][r * HD:(r + 1) * HD, lo:hi], kp[p0:p0 + HD, g, part, lo:hi]).then_inc(done, 16)

                def query_rows(h, done):
                    slot, g, p0 = h % 4, h // 8, HD * (h % 8)
                    for r, part in enumerate(Q_PARTS):
                        sp.dma_start(qslot[slot][r * HD:(r + 1) * HD, :], qp[p0:p0 + HD, g, part, ds(b * T, T)]).then_inc(done, 16)

                def load_values(h):
                    if h < 2:
                        sp.wait_ge(sem("v_evacuated"), b * NCK + NCK)
                    else:
                        sp.wait_ge(sem("pv_done"), b * (H * UNITS) + (h - 1) * UNITS + 2)
                    sp.dma_start(vslot[h % 2][:, :, :], vall[:, h, :, :]).then_inc(sem(f"v_loaded{h % 2}"), 16)

                for c in range(NCH):
                    sp.wait_ge(sem("ctx_transposed"), b * NCH + (c + 1))
                    sp.dma_start(ctx_raw[c % 2][:, :, :], ctx_v[:, ds(b * NCH + c, 1), :, :].rearrange(
                        "p o t d -> p (o t) d")).then_inc(sem(f"ctx_loaded{c % 2}"), 16)
                    if c == 2:
                        sp.wait_ge(sem("mask_ready"), 1)
                        for s in range(4):
                            sp.dma_start(kslot[s][96:97, :].rearrange("o (c k) -> o c k", k=P),
                                         mrow[:, ds(b, 1), :].rearrange("c o k -> c (o k)")).then_inc(sem(f"k_first{s}"), 16)
                        for h in range(2):
                            query_rows(h, sem(f"k_first{h}"))
                for h in range(2):
                    sp.wait_ge(sem("k_low"), b * NCK + NCK // 2)
                    key_rows(h, 0, HALF, sem(f"k_first{h}"))
                sp.wait_ge(sem("k_low"), b * NCK + NCK)
                for h in range(2):
                    key_rows(h, HALF, S, sem(f"k_loaded{h}"))
                load_values(0)
                load_values(1)
                for h in range(2, 4):
                    key_rows(h, 0, S, sem(f"k_loaded{h}"))
                    query_rows(h, sem(f"k_loaded{h}"))
                for t in range(1, H - 1):
                    if t + 3 < H:
                        h = t + 3
                        sp.wait_ge(sem("s2_done"), b * (H * UNITS) + (h - 3) * UNITS)
                        key_rows(h, 0, S, sem(f"k_loaded{h % 4}"))
                        query_rows(h, sem(f"k_loaded{h % 4}"))
                    load_values(t + 1)

            sp.wait_ge(sem("loop_done"), 1)
            for i, w in enumerate((Aq, Ak, Av, Ao)):
                sp.dma_start(araw[:, i, :, :], w.rearrange("(c p) n -> p c n", p=P)).then_inc(sem("a_loaded"), 16)
            sp.wait_ge(sem("rhoT_ready"), 1)
            for b in range(B):
                sp.dma_start(rho_dram[b].rearrange("h (q t) -> q h t", q=NQ),
                             rhoT[b * NQ * H:(b + 1) * NQ * H, :]).then_inc(sem("rho_stored"), 16)
            sp.wait_ge(sem("rho_stored"), B * 16)
            for b in range(B):
                if b >= 2:
                    sp.wait_ge(sem("scan_done"), 4 * (b - 1))
                for hg in range(4):
                    src = rho_dram[b, 4 * hg:4 * hg + 4, :]
                    dst = rows[b % 2][:, 4 * hg:4 * hg + 4, :]
                    sp.dma_start(dst[:, :, 0:T], src.partition_broadcast(P)).then_inc(sem(f"rows_loaded{hg}_{b % 2}"), 16)
                    sp.dma_start(dst[:, :, T:T + P], src[:, P:T].partition_broadcast(P)).then_inc(sem(f"rows_loaded{hg}_{b % 2}"), 16)

            sp.wait_ge(sem("x2_ready"), 4)
            sp.dma_start(g_raw[:, :], gate_w).then_inc(sem("gate_loaded"), 16)

            def load_expert(i, buf, g3, u3, d3):
                sp.wait_ge(sem("w_transposed"), i + 1)
                done = sem(f"w_loaded{buf}")
                sp.dma_start(wraw[buf][:, 0, :], g3).then_inc(done, 16)
                sp.dma_start(wraw[buf][:, 1, :], u3).then_inc(done, 16)
                sp.dma_start(wraw[buf][:, 2, :].rearrange("p (c f) -> p c f", c=NC),
                             d3.rearrange("(c p) f -> p c f", p=P)).then_inc(done, 16)
            with sp.Fori(0, E // 2) as e2:
                for k in range(2):
                    e = e2 * 2 + k
                    load_expert(e, k, wg[ds(e, 1), :, :].rearrange("o f d -> (o f) d"),
                                wu[ds(e, 1), :, :].rearrange("o f d -> (o f) d"),
                                wd[ds(e, 1), :, :].rearrange("o d f -> (o d) f"))
            load_expert(E, 0, sg, su, sd)
            out_v = out.rearrange("b (q p) d -> p (b q) d", p=P)
            for q in range(4):
                sp.wait_ge(sem("down_read"), E * NT + 2 + (2 * q + 2))
                sp.dma_start(out_v[:, 2 * q:2 * q + 2, :], x_sb[:, 2 * q:2 * q + 2, :]).then_inc(sem("out_stored"), 16)
            sp.wait_ge(sem("out_stored"), 64)

        @block.gpsimd
        def _(pool):
            pool.sem_inc(sem("mt_parts"), 8)
            pool.memset(ident[:, :], 0.0).then_inc(sem("pool_const"), 1)
            pool.memset(identb[:, :], 0.0).then_inc(sem("pool_const"), 1)
            pool.memset(mhalf[:, :], -0.5).then_inc(sem("pool_const"), 1)
            pool.memset(mt[:, :, :, :], 1.0).then_inc(sem("pool_const"), 1)
            pool.wait_ge(sem("pool_const"), 4)
            for m in (ident, identb):
                pool.affine_select(out=m[:, :], in_=m[:, :], compare_op=ALU.not_equal, fill=1.0, base=0, pattern=[[-1, P]],
                                   channel_multiplier=1).then_inc(sem("ident_ready"), 1)
            pool.wait_ge(sem("ident_ready"), 2)
            for s in range(4):
                pool.memset(kslot[s][96:100, :], 1.0).then_inc(sem("slot_ones"), 1)
                pool.wait_ge(sem("slot_ones"), 2 * s + 1)
                pool.memset(qslot[s][96:100, :], 1.0).then_inc(sem("slot_ones"), 1)
                pool.wait_ge(sem("slot_ones"), 2 * s + 2)
            pool.memset(vall[:, :, :, HD], 1.0).then_inc(sem("slot_ones"), 1)

            def inverse_root(name, dst, src, need, w):
                pool.wait_ge(sem(name + "_var"), need)
                pool.tensor_tensor(dst, src, mhalf[:, 0:w], ALU.pow).then_inc(sem(name + "_root"), 1)

            inverse_root("ln1", rstd[:, :], veps[:, :], 1, NT)
            with pool.Fori(0, B) as b:
                def split_max(Hn, par):
                    pool.wait_ge(sem("nm_ready"), Hn + 3)
                    pool.wait_ge(sem("mt_transposed"), Hn + 1)
                    pool.sem_inc(sem("pool_past"), 1)
                    part = sem("mt_parts")
                    pool.tensor_copy(mt[:, par, :, 1], nm[:, par, :]).then_inc(part, 1)
                    pool.wait_ge(part, Hn * 4 + 9)
                    pool.tensor_tensor(nmr[:, :], nm[:, par, :], mt[:, par, :, 1], ALU.subtract).then_inc(part, 1)
                    pool.wait_ge(part, Hn * 4 + 10)
                    pool.sem_inc(sem("pool_past"), 1)
                    pool.tensor_copy(mt[:, par, :, 2], nmr[:, :]).then_inc(part, 1)
                    pool.wait_ge(part, Hn * 4 + 11)
                    pool.tensor_tensor(mt[:, par, :, 3], nmr[:, :], mt[:, par, :, 2], ALU.subtract).then_inc(part, 1)
                with pool.Fori(0, H // 2) as g:
                    for k in range(2):
                        split_max(b * H + (g * 2 + k), k)
            pool.wait_ge(sem("loop_done"), 1)
            pool.memset(starts[:, :, :], 0.0).then_inc(sem("starts0"), 1)
            pool.wait_ge(sem("starts0"), 1)
            for part, w in ((starts[:, :, 0:T], T), (starts[:, :, T:T + P], P)):
                pool.affine_select(out=part, in_=part, compare_op=ALU.not_equal, fill=1.0, base=0,
                                   pattern=[[0, HPB], [-1, w]], channel_multiplier=1).then_inc(sem("starts_ready"), 1)
            inverse_root("ln2", rstd[:, :], veps[:, :], 1, NT)
            inverse_root("kn", sm["rn"][:, :], sm["ss"][:, :], 1, NT * H)
            inverse_root("ln3", rstd[:, :], veps[:, :], 1, NT)
            pool.wait_ge(sem("x2_ready"), 4)
            pool.memset(lower[:, :, :], 1.0).then_inc(sem("lower0"), 1)
            pool.wait_ge(sem("lower0"), 1)
            pool.affine_select(out=lower[:, :, :], in_=lower[:, :, :], compare_op=ALU.is_gt, fill=0.0, base=0,
                               pattern=[[1, E], [-1, E]], channel_multiplier=0).then_inc(sem("lower_ready"), 1)

        @block.tensor
        def _(pe):
            def transpose(dst, src, idt, **k):
                return pe.matmul(dst, src, idt, start=True, stop=True, is_transpose=True, **k)

            def transpose_all(name, src):
                if name == "on":
                    pe.wait_ge(sem("on_ready"), B)
                if name == "ln3":
                    pe.wait_ge(sem("yT_ready"), 4)
                for c in range(NC):
                    for half in range(2):
                        for i in range(4):
                            t = half * 4 + i
                            if name not in ("on", "y"):
                                pe.wait_ge(sem(name + "_normed"), t + 1)
                            m = transpose(ps[:, 2 * c + half, i * P:(i + 1) * P], src[:, t, c * P:(c + 1) * P], ident[:, :])
                        m.then_inc(sem(name + "_turned"), 1)

            pe.sem_inc(sem("ctx_transposed"), 2)
            pe.sem_inc(sem("affinity"), 4)
            pe.sem_inc(sem("mixed"), 4)
            pe.sem_inc(sem("pv_done"), 2)
            pe.sem_inc(sem("accT_done"), 1)
            pe.sem_inc(sem("mt_transposed"), 2)
            pe.sem_inc(sem("w_transposed"), 2)
            pe.sem_inc(sem("down_done"), NT)
            pe.wait_ge(sem("ident_ready"), 2)
            transpose_all("ln1", sxn)
            pe.wait_ge(sem("ln1T_ready"), 4)
            pe.wait_ge(sem("weights_loaded"), WEIGHTS_LOADED)
            for g in range(2):
                for half in range(2):
                    i = 2 * g + half
                    for c in range(NC):
                        m = pe.matmul(ps[:, 4 + i, :], wq_sb[:, c, g * P:(g + 1) * P],
                                      sxnT[:, c, half * 512:(half + 1) * 512], start=c == 0, stop=c == NC - 1)
                    m.then_inc(sem("q_proj"), 1)
            pe.wait_ge(sem("q_low"), 4)
            pe.wait_ge(sem("acc_zero"), 1)

            with pe.Fori(0, B) as b:
                def turn(c):
                    pe.wait_ge(sem(f"ctx_loaded{c % 2}"), b * (8 * NCH) + 16 * (c // 2 + 1))
                    if c:
                        pe.wait_ge(sem("ctxT_ready"), b * NCH + c)
                    for dc in range(NC):
                        for t in range(4):
                            m = transpose(ps[:, dc, t * P:(t + 1) * P], ctx_raw[c % 2][:, t, dc * P:(dc + 1) * P], ident[:, :])
                    m.then_inc(sem("ctx_transposed"), 1)

                def project_keys(c):
                    pe.wait_ge(sem("ctxT_ready"), b * NCH + (c + 1))
                    for g in range(2):
                        if c:
                            pe.wait_ge(sem("k_rest"), b * NCK + (2 * c - 1 + g))
                        for dc in range(NC):
                            m = pe.matmul(ps[:, 2 + g, :], wkv_sb[:, dc, g * P:(g + 1) * P], ctxT[c % CTXT][:, dc, :],
                                          start=dc == 0, stop=dc == NC - 1)
                        m.then_inc(sem("k_proj"), 1)

                def project_values(c):
                    for pair in range(2):
                        if c:
                            pe.wait_ge(sem("v_evacuated"), b * NCK + (2 * c - 1 + pair))
                        for j in range(2):
                            t = 2 * pair + j
                            for dc in range(NC):
                                m = pe.matmul(ps[:, value_bank(c, pair), j * D:(j + 1) * D], ctxT[c % CTXT][:, dc, t * P:(t + 1) * P],
                                              wkv_sb[:, dc, D:2 * D], start=dc == 0, stop=dc == NC - 1)
                        m.then_inc(sem("v_proj"), 1)

                def max_product(H0, n, i, bank):
                    kc, qt = divmod(i % TASKS, NQ)
                    slot = (i // TASKS) % 4
                    pe.wait_ge(sem("max_read"), H0 * TASKS + (n + 1))
                    pe.matmul(ps[:, bank, :], qslot[slot][0:ROWS + 1, qt * P:(qt + 1) * P],
                              kslot[slot][0:ROWS + 1, kc * 512:(kc + 1) * 512], start=True, stop=True
                              ).then_inc(sem("s1_done"), 1)

                def first_tasks(lo, hi):
                    for n in range(lo, hi):
                        if n == 0:
                            pe.wait_ge(sem("slot_ones"), 9)
                            pe.wait_ge(sem("o_reduced"), b * H + 2)
                        if n in (0, 8):
                            pe.wait_ge(sem(f"k_first{n // 8}"), b * FIRST_LOADS + FIRST_LOADS)
                        if n == EARLY:
                            pe.wait_ge(sem("k_loaded0"), b * K_LOADED[0] + LOADS // 2)
                        max_product(b * H, n, FIRST[n], 6 + n % 2)

                turn(0)
                for c in range(NCH):
                    if c + 1 < NCH:
                        turn(c + 1)
                    project_keys(c)
                    if c:
                        project_values(c - 1)
                    first_tasks(*EARLY_TASKS.get(c, (0, 0)))
                project_values(NCH - 1)

                def max_task(H0, i, g0):
                    hh, k = divmod(i, TASKS)
                    slot, turns = hh % 4, hh // 4
                    if k == 0 or i == LEAD:
                        if slot >= 2:
                            pe.wait_ge(sem(f"k_first{slot}"), b * 16 + 16)
                        need = LOADS * turns + (LOADS // 2 if slot < 2 else LOADS)
                        pe.wait_ge(sem(f"k_loaded{slot}"), b * K_LOADED[slot] + (g0 * LOADS + need))
                    max_product(H0, i, i, 4 + i % 2)

                def turn_max(H0, hh):
                    pe.wait_ge(sem("mt_parts"), H0 * 4 + (4 * hh + 12))
                    pe.wait_ge(sem("o_reduced"), H0 + (hh + 1))
                    bank = ps[96:100, 6 + hh % 2, 0:P].bitcast(BF16)
                    for qt in range(NQ):
                        m = transpose(bank[:, qt * P:(qt + 1) * P], mt[:, hh % 2, qt, :], identb[:, :], tile_position=(0, 96))
                    m.then_inc(sem("mt_transposed"), 1)

                def steps(H0, g0, lo, hi, first=False, last=False):
                    for s in range(lo, hi):
                        hh, u = divmod(s, UNITS)
                        slot = hh % 4
                        live = not (last and s >= HPB * UNITS)
                        if live:
                            if u == 0:
                                pe.wait_ge(sem("qrow_ready"), H0 + (hh + 1))
                            pe.wait_ge(sem("exp_done"), H0 * UNITS + (s + 1))
                            for j in range(4):
                                kt = 4 * u + j
                                m = pe.matmul(ps[:, 2 * (s % 2) + j // 2, (j % 2) * T:(j % 2 + 1) * T],
                                              kslot[slot][:, kt * P:(kt + 1) * P], qslot[slot][:, :], start=True, stop=True)
                            m.then_inc(sem("s2_done"), 1)
                        tasks = [i for i in (LEAD + 2 * s, LEAD + 2 * s + 1) if not (last and i >= HPB * TASKS)]
                        if tasks:
                            max_task(H0, tasks[0], g0)
                        if not (first and s == 0) and s <= (HPB * UNITS if last else hi):
                            weigh(H0, g0, s - 1)
                        if tasks:
                            max_task(H0, tasks[1], g0)
                        if u == 2 and not (first and hh == 0):
                            pe.wait_ge(sem("acc_copied"), H0 + hh)
                            for qt in range(NQ):
                                m = transpose(ps[:, 6 + (hh - 1) % 2, T + qt * P:T + (qt + 1) * P], accS[:, qt * P:(qt + 1) * P], ident[:, :])
                            m.then_inc(sem("accT_done"), 1)
                        if u == 6 and live and not (last and hh == HPB - 1):
                            turn_max(H0, hh + 1)

                def weigh(H0, g0, s):
                    hh, u = divmod(s, UNITS)
                    pe.wait_ge(sem("exp_done"), H0 * UNITS + (s + 3))
                    if u == 0:
                        pe.wait_ge(sem("o_reduced"), H0 + (hh + 1))
                        pe.wait_ge(sem(f"v_loaded{hh % 2}"), b * (H * 8) + g0 * (HPB * 8) + 16 * (hh // 2 + 1))
                    for j in range(4):
                        m = pe.matmul(ps[32 * j:32 * j + HD + 1, 6 + hh % 2, 0:T], vslot[hh % 2][:, 4 * u + j, :],
                                      pT[s % 2][:, j, :], start=u == 0, stop=u == UNITS - 1, tile_position=(0, 32 * j))
                    m.then_inc(sem("pv_done"), 1)

                Hb = b * H
                first_tasks(EARLY, LEAD)
                pe.wait_ge(sem("v_evacuated"), b * NCK + NCK)
                pe.wait_ge(sem("k_rest"), b * NCK + NCK)
                turn_max(Hb, 0)
                steps(Hb, 0, 0, 4, first=True)
                with pe.Fori(0, H // HPB - 1) as g:
                    steps(Hb + g * HPB, g, 4, 36)
                steps(Hb + (H - HPB), H // HPB - 1, 4, 36, last=True)

            def token_products(name, left, right, ready):
                for t in range(NT):
                    if t % 4 == 0:
                        pe.wait_ge(sem(ready), 4)
                    for c in range(NC):
                        m = pe.matmul(ps[:, 4 + t // 2, (t % 2) * D:(t % 2 + 1) * D], left[:, c, t * P:(t + 1) * P], right[:, c, :],
                                      start=c == 0, stop=c == NC - 1)
                    if t % 2:
                        m.then_inc(sem(name), 1)

            transpose_all("on", on)
            token_products("x_proj", onT, wout_sb, "onT_ready")
            pe.wait_ge(sem("a_loaded"), 4 * 16)
            pe.wait_ge(sem("x1_ready"), 4)
            for i in range(4):
                for dc in range(NC):
                    for ec in range(NC):
                        m = transpose(ps[:, 4 + i, dc * D + ec * P:dc * D + (ec + 1) * P],
                                      araw[:, i, ec, dc * P:(dc + 1) * P], ident[:, :])
                m.then_inc(sem("a_turned"), 1)
            pe.wait_ge(sem("onT_ready"), 4)
            transpose_all("ln2", xn2)
            pe.wait_ge(sem("a_ready"), 4)
            token_products("rk_proj", xn2T, akT, "ln2T_ready")
            pe.wait_ge(sem("rho_ready"), 1)
            transpose(ps[:, 0, 0:P], sm["rho"][:, :], ident[:, :]).then_inc(sem("rho_turned"), 1)
            pe.wait_ge(sem("rhoT_ready"), 1)
            pe.wait_ge(sem("rk_ready"), 4)

            with pe.Fori(0, B // 2) as b2:
                for kb in range(2):
                    b = b2 * 2 + kb
                    for hg in range(4):
                        if hg == 0:
                            pe.wait_ge(sem("rec_q_ready"), b * 4 + 4)
                            pe.wait_ge(sem("weighted"), b * 8 + 6)
                        for i, w in enumerate((aqT, avT)):
                            for c in range(NC):
                                m = pe.matmul(ps[:, hg, i * T:(i + 1) * T],
                                              w[:, c, 4 * hg:4 * hg + 4, :].rearrange("p h e -> p (h e)"),
                                              xn2T[:, c, ds(b * T, T)], start=c == 0, stop=c == NC - 1)
                        m.then_inc(sem("qv_proj"), 1)

                    def affinity(hg):
                        o = 1 + 3 * (hg % 2)
                        if hg == 0:
                            pe.wait_ge(sem("rec_q_ready"), b * 4 + 8)
                        pe.wait_ge(sem("weighted"), b * 8 + (2 * hg + 6))
                        for a in range(2):
                            pe.matmul(ps[:, o + a, :], vT[hg][:, 0:P], qd[hg][:, 2 * a:2 * a + 2, :], start=True, stop=True)
                        pe.matmul(ps[:, o + 2, :], vT[hg][:, P:T], qd[hg][:, :, P:T], start=True, stop=True
                                  ).then_inc(sem("affinity"), 1)

                    def mix(hg):
                        pe.wait_ge(sem("weighted"), b * 8 + (2 * hg + 10))
                        if hg == 0:
                            pe.wait_ge(sem("kkb_ready"), b + 1)
                            pe.wait_ge(sem("y_ready"), b + 1)
                        w = dec[hg]
                        for h in range(4):
                            col = slice((4 * hg + h) * HD, (4 * hg + h + 1) * HD)
                            c1 = slice(D + col.start, D + col.stop)
                            pe.matmul(ps[:, 7, col], w[:, h, 0:P], kkb[kb][:, 0, col], start=True, stop=True)
                            pe.matmul(ps[:, 7, c1], w[:, h, P:T], kkb[kb][:, 0, col], start=True, stop=False)
                            m = pe.matmul(ps[:, 7, c1], w[:, h, T:T + P], kkb[kb][:, 1, col], start=False, stop=True)
                        m.then_inc(sem("mixed"), 1)

                    affinity(0)
                    affinity(1)
                    mix(0)
                    affinity(2)
                    mix(1)
                    affinity(3)
                    mix(2)
                    mix(3)
            pe.wait_ge(sem("y_ready"), B + 1)
            pe.wait_ge(sem("weighted"), 8 * B + 8)
            transpose_all("y", y_sb)
            token_products("y_proj", yT, aoT, "yT_ready")

            transpose_all("ln3", xn3)
            pe.wait_ge(sem("gate_loaded"), 16)
            for c in range(NC):
                m = transpose(ps[:, 4, c * E:(c + 1) * E], g_raw[:, c * P:(c + 1) * P], ident[0:E, 0:E])
            m.then_inc(sem("gate_turned"), 1)
            pe.wait_ge(sem("gate_ready"), 1)
            pe.wait_ge(sem("ln3T_ready"), 4)
            for t in range(NT):
                for c in range(NC):
                    m = pe.matmul(ps[:, 6, t * E:(t + 1) * E], xn3T[:, c, t * P:(t + 1) * P], gT[:, c, :],
                                  start=c == 0, stop=c == NC - 1)
            m.then_inc(sem("logits"), 1)

            def turn_weights(e, k, nth):
                pe.wait_ge(sem(f"w_loaded{k}"), nth)
                pe.wait_ge(sem("wT_ready"), e * 2 + 2)
                for i in range(2):
                    for c in range(NC):
                        transpose(ps[:, 0, (2 * i + c) * P:(2 * i + c + 1) * P], wraw[k][:, i, c * P:(c + 1) * P], ident[:, :])
                for c in range(NC):
                    m = transpose(ps[:, 1, c * P:(c + 1) * P], wraw[k][:, 2, c * P:(c + 1) * P], ident[:, :])
                m.then_inc(sem("w_transposed"), 1)

            def gate_up(e, k):
                pe.wait_ge(sem("wT_ready"), e * 2 + 4)
                for half in range(2):
                    pe.wait_ge(sem("h_ready"), e * 2 + (half + 1))
                    for i in range(2):
                        for c in range(NC):
                            m = pe.matmul(ps[:, 2 + 2 * half + i, :], wT[k][:, i, c * P:(c + 1) * P],
                                          xn3T[:, c, half * 512:(half + 1) * 512], start=c == 0, stop=c == NC - 1)
                    m.then_inc(sem("gu_done"), 1)

            def down(e, k):
                for t in range(NT):
                    pe.wait_ge(sem("h_ready"), e * 2 + (t // 4 + 3))
                    pe.wait_ge(sem("down_read"), e * NT + (t + 1))
                    pe.matmul(ps[:, 6 + t % 2, 0:D], hT[k][:, t * P:(t + 1) * P], wT[k][:, 2, :],
                              start=True, stop=True).then_inc(sem("down_done"), 1)

            turn_weights(0, 0, 48)
            with pe.Fori(0, E // 2) as e2:
                for k in range(2):
                    e = e2 * 2 + k
                    gate_up(e, k)
                    turn_weights(e + 1, 1 - k, e2 * 48 + 48 * (k + 1))
                    if k == 0:
                        pe.wait_ge(sem("logits_read"), 1)
                    down(e, k)
            gate_up(E, 0)
            down(E, 0)

        @block.scalar
        def _(act):
            def copy(dst, src):
                return act.activation(dst, src, ACT.Copy)

            act.sem_inc(sem("exp_done"), 2)
            act.sem_inc(sem("wT_ready"), 2)
            for i in range(4):
                act.wait_ge(sem("ln1_turned"), i + 1)
                copy(sxnT[:, i // 2, (i % 2) * 512:(i % 2 + 1) * 512], ps[:, i, :]).then_inc(sem("ln1T_ready"), 1)
            for i in range(4):
                g, half = divmod(i, 2)
                cols = slice(half * 512, (half + 1) * 512)
                act.wait_ge(sem("q_proj"), i + 1)
                act.activation(qp[:, g, 0, cols], ps[:, 4 + i, :], ACT.Identity, bias=bq_col[:, g:g + 1]).then_inc(sem("q_high"), 1)
                act.wait_ge(sem("q_rest"), i + 1)
                copy(qp[:, g, 1, cols], r1[i % 2][:, :]).then_inc(sem("q_mid"), 1)
            with act.Fori(0, B) as b:
                def evacuate(c):
                    act.wait_ge(sem("ctx_transposed"), b * NCH + (c + 3))
                    if c >= CTXT:
                        act.wait_ge(sem("v_proj"), b * NCK + 2 * (c - CTXT + 1))
                    copy(ctxT[c % CTXT][:, :, :], ps[:, 0:2, :]).then_inc(sem("ctxT_ready"), 1)

                evacuate(0)
                for c in range(NCH):
                    cols = slice(c * CH, (c + 1) * CH)
                    if c + 1 < NCH:
                        evacuate(c + 1)
                    for g in range(2):
                        act.wait_ge(sem("k_proj"), b * NCK + (2 * c + g + 1))
                        act.activation(kp[:, g, 0, cols], ps[:, 2 + g, :], ACT.Identity, bias=bk_col[:, g:g + 1]).then_inc(sem("k_high"), 1)
                    for g in range(2):
                        act.wait_ge(sem("k_rest"), b * NCK + (2 * c + g + 1))
                        copy(kp[:, g, 1, cols], r1[g][:, :]).then_inc(sem("k_mid"), 1)

                def qrow(H0, hh):
                    act.wait_ge(sem("mt_transposed"), H0 + (hh + 3))
                    copy(qslot[hh % 4][96:100, :], ps[96:100, 6 + hh % 2, 0:P].bitcast(BF16)).then_inc(sem("qrow_ready"), 1)

                def steps(H0, lo, hi, first=False, last=False):
                    for s in range(lo, hi):
                        hh, u = divmod(s, UNITS)
                        live = not (last and s >= HPB * UNITS)
                        if live:
                            act.wait_ge(sem("s2_done"), H0 * UNITS + (s + 1))
                            act.wait_ge(sem("pv_done"), H0 * UNITS + (s + 1))
                            act.activation(pT[s % 2][:, :, :], ps[:, 2 * (s % 2):2 * (s % 2) + 2, :].rearrange(
                                "p a (j t) -> p (a j) t", j=2), ACT.Exp, scale=SCALE).then_inc(sem("exp_done"), 1)
                        if u == 0 and not (first and hh == 0):
                            act.wait_ge(sem("pv_done"), H0 * UNITS + (s + 2))
                            act.wait_ge(sem("accT_done"), H0 + hh)
                            copy(accS[:, :], ps[:, 6 + (hh - 1) % 2, 0:T]).then_inc(sem("acc_copied"), 1)
                        if u == 6 and live and not (last and hh == HPB - 1):
                            qrow(H0, hh + 1)

                Hb = b * H
                qrow(Hb, 0)
                steps(Hb, 0, 4, first=True)
                with act.Fori(0, H // HPB - 1) as g:
                    steps(Hb + g * HPB, 4, 36)
                steps(Hb + (H - HPB), 4, 36, last=True)

            def turned(name, dst):
                for i in range(4):
                    act.wait_ge(sem(name + "_turned"), i + 1)
                    copy(dst[:, i // 2, (i % 2) * 512:(i % 2 + 1) * 512], ps[:, i, :]).then_inc(sem(name + "T_ready"), 1)

            turned("on", onT)
            for i, dst in enumerate((aqT, akT, avT, aoT)):
                act.wait_ge(sem("a_turned"), i + 1)
                if i % 2 == 0:
                    act.wait_ge(sem("a_zero"), 2)
                    for dc in range(NC):
                        m = copy(dst[:, dc, :, 0:HD], ps[:, 4 + i, dc * D:(dc + 1) * D].rearrange("p (h e) -> p h e", e=HD))
                else:
                    m = copy(dst[:, :, :], ps[:, 4 + i, :].rearrange("p (c e) -> p c e", c=NC))
                m.then_inc(sem("a_ready"), 1)
            turned("ln2", xn2T)
            for i in range(4):
                act.wait_ge(sem("rk_proj"), i + 1)
                copy(k_sb[:, 2 * i:2 * i + 2, :], ps[:, 4 + i, :].rearrange("p (q e) -> p q e", q=2)).then_inc(sem("rk_ready"), 1)
            act.wait_ge(sem("gates"), 2)
            act.activation(sm["eg"][:, :], sm["ug"][:, :], ACT.Exp, scale=-1.0).then_inc(sem("gate_exp"), 1)
            act.activation(sm["el"][:, :], sm["ul"][:, :], ACT.Exp).then_inc(sem("gate_exp"), 1)
            act.wait_ge(sem("rho_turned"), 1)
            copy(rhoT[:, :], ps[:, 0, 0:P]).then_inc(sem("rhoT_ready"), 1)
            act.sem_inc(sem("y_ready"), 1)
            act.sem_inc(sem("rec_q_ready"), 4)
            act.wait_ge(sem("q_zero"), 4)
            with act.Fori(0, B // 2) as b2:
                for kb in range(2):
                    b = b2 * 2 + kb
                    for hg in range(4):
                        act.wait_ge(sem("qv_proj"), b * 4 + (hg + 1))
                        act.wait_ge(sem("affinity"), b * 4 + (hg + 1))
                        for h in range(4):
                            r = slice(32 * h, 32 * h + 32)
                            copy(qd[hg][r, h, :], ps[r, hg, 0:T]).then_inc(sem("q_placed"), 1)
                        copy(vT[hg][:, :], ps[:, hg, T:2 * T]).then_inc(sem("rec_q_ready"), 1)
                        if hg == 0:
                            act.wait_ge(sem("kk_ready"), 1)
                            act.wait_ge(sem("mixed"), b * 4 + 1)
                            copy(kkb[kb][:, :, :], kk[:, ds(b * NQ, NQ), :]).then_inc(sem("kkb_ready"), 1)
                    act.wait_ge(sem("mixed"), b * 4 + 8)
                    copy(y_sb[:, ds(b * NQ, NQ), :], ps[:, 7, :].rearrange("p (q e) -> p q e", q=NQ)).then_inc(sem("y_ready"), 1)
            turned("y", yT)
            turned("ln3", xn3T)
            act.wait_ge(sem("gate_turned"), 1)
            copy(gT[:, :, :], ps[:, 4, 0:NC * E].rearrange("p (c e) -> p c e", c=NC)).then_inc(sem("gate_ready"), 1)

            def weights(e, k):
                act.wait_ge(sem("w_transposed"), e + 3)
                act.wait_ge(sem("down_done"), e * NT)
                copy(wT[k][:, 0:2, :], ps[:, 0, :].rearrange("p (i f) -> p i f", i=2)).then_inc(sem("wT_ready"), 1)
                copy(wT[k][:, 2, :], ps[:, 1, 0:D]).then_inc(sem("wT_ready"), 1)

            def gates(e):
                for half in range(2):
                    act.wait_ge(sem("gu_done"), e * 2 + (half + 1))
                    act.wait_ge(sem("h_ready"), e * 2 + (half + 1))
                    act.activation(silu[half][:, :], ps[:, 2 + 2 * half, :], ACT.Silu).then_inc(sem("silu_done"), 1)

            act.wait_ge(sem("w_transposed"), 3)
            copy(wT[0][:, 0:2, :], ps[:, 0, :].rearrange("p (i f) -> p i f", i=2)).then_inc(sem("wT_ready"), 1)
            copy(wT[0][:, 2, :], ps[:, 1, 0:D]).then_inc(sem("wT_ready"), 1)
            act.wait_ge(sem("lg_shifted"), 1)
            act.activation(pr[:, :, :], lg[:, :, :], ACT.Exp).then_inc(sem("lg_exp"), 1)
            with act.Fori(0, E // 2) as e2:
                for k in range(2):
                    gates(e2 * 2 + k)
                    weights(e2 * 2 + (k + 1), 1 - k)
            gates(E)

        @block.vector
        def _(dve):
            def normalise(name, n, src, dst, base, lane):
                for t in range(n):
                    dve.bn_stats(stats[:, t, :], src[:, t, :]).then_inc(sem(name + "_stats"), 1)
                dve.wait_ge(sem(name + "_stats"), base * n + n)
                dve.sem_inc(sem("dve_past"), 1)
                for t in range(n):
                    dve.bn_aggr(mv[:, t, :], stats[:, t, :]).then_inc(sem(name + "_aggr"), 1)
                dve.wait_ge(sem(name + "_aggr"), base * n + n)
                dve.tensor_scalar(veps[:, 0:n], mv[:, 0:n, 1], LN_EPS, None, ALU.add).then_inc(sem(name + "_var"), 1)
                refine(name, rstd[:, 0:n], veps[:, 0:n], newt[:, 0:n], base)
                for t in range(n):
                    dve.tensor_scalar(dst[:, t, :], src[:, t, :], mv[:, t, 0:1], rstd[:, t:t + 1], ALU.subtract,
                                      ALU.mult).then_inc(sem(name + "_normed"), 1)

            def refine(name, y, v, tmp, base):
                step = sem(name + "_newton")
                dve.wait_ge(sem(name + "_root"), base + 1)
                dve.tensor_tensor(tmp, y, y, ALU.mult).then_inc(step, 1)
                dve.wait_ge(step, base * 4 + 1)
                dve.tensor_tensor(tmp, tmp, v, ALU.mult).then_inc(step, 1)
                dve.wait_ge(step, base * 4 + 2)
                dve.tensor_scalar(tmp, tmp, -0.5, 1.5, ALU.mult, ALU.add).then_inc(step, 1)
                dve.wait_ge(step, base * 4 + 3)
                dve.tensor_tensor(y, y, tmp, ALU.mult).then_inc(step, 1)
                dve.wait_ge(step, base * 4 + 4)

            dve.sem_inc(sem("max_read"), 2)
            dve.sem_inc(sem("nm_ready"), 2)
            dve.sem_inc(sem("o_reduced"), 2)
            dve.sem_inc(sem("h_ready"), 2)
            dve.sem_inc(sem("down_read"), 2)
            dve.sem_inc(sem("weighted"), 8)
            dve.wait_ge(sem("x_loaded"), 16)
            normalise("ln1", NT, x_sb, sxn, 0, 0)
            dve.wait_ge(sem("weights_loaded"), WEIGHTS_LOADED)
            dve.wait_ge(sem("ln1_normed"), NT)
            dve.tensor_tensor(x_sb[:, :, :], x_sb[:, :, :], bout_bc[:, :].unsqueeze(1).broadcast_to([P, NT, D]),
                              ALU.add).then_inc(sem("xb_ready"), 1)
            dve.tensor_scalar(mrow[:, :, :], mask_u8[:, :, :], -3e38, 10.0, ALU.mult, ALU.mult).then_inc(sem("mask_ready"), 1)
            for i in range(4):
                g, half = divmod(i, 2)
                cols = slice(half * 512, (half + 1) * 512)
                dve.wait_ge(sem("q_high"), i + 1)
                dve.scalar_tensor_tensor(out=r1[i % 2][:, :], in0=ps[:, 4 + i, :], scalar=bq_col[:, g:g + 1],
                                         in1=qp[:, g, 0, cols], op0=ALU.add, op1=ALU.subtract).then_inc(sem("q_rest"), 1)
                dve.wait_ge(sem("q_mid"), i + 1)
                dve.wait_ge(sem("q_rest"), i + 1)
                dve.tensor_tensor(qp[:, g, 2, cols], r1[i % 2][:, :], qp[:, g, 1, cols], ALU.subtract).then_inc(sem("q_low"), 1)
            dve.wait_ge(sem("q_rest"), 4)
            dve.wait_ge(sem("q_low"), 4)
            dve.memset(ps[:, 6:8, :], 0.0).then_inc(sem("acc_zero"), 1)

            with dve.Fori(0, B) as b:
                dve.wait_ge(sem("slot_ones"), 9)

                def values(c, pair):
                    dve.wait_ge(sem("v_proj"), b * NCK + (2 * c + pair + 1))
                    kt = 4 * c + 2 * pair
                    dve.tensor_tensor(vall[:, :, kt:kt + 2, 0:HD].rearrange("p h k e -> p k h e"),
                                      ps[:, value_bank(c, pair), :].rearrange("p (k h e) -> p k h e", k=2, h=H),
                                      bv_bc[:, :].rearrange("p (h e) -> p h e", h=H).unsqueeze(1).broadcast_to([P, 2, H, HD]),
                                      ALU.add).then_inc(sem("v_evacuated"), 1)

                def max_read(H0, n, i, bank):
                    hh, k = divmod(i, TASKS)
                    kc, qt = divmod(k, NQ)
                    par = hh % 2
                    if k == 0:
                        dve.wait_ge(sem("nm_ready"), H0 + (hh + 1))
                    dve.wait_ge(sem("s1_done"), H0 * TASKS + (n + 1))
                    dve.tensor_reduce(pm[:, par, qt, kc:kc + 1], ps[:, bank, :], AX.X, ALU.max).then_inc(sem("max_read"), 1)
                    if k == TASKS - 1:
                        dve.wait_ge(sem("max_read"), H0 * TASKS + (n + 3))
                        dve.wait_ge(sem("mt_parts"), H0 * 4 + (hh * 4 + 4))
                        dve.tensor_reduce(nm[:, par, :], pm[:, par, :, :], AX.X, ALU.max, negate=True).then_inc(sem("nm_ready"), 1)

                def first_tasks(lo, hi):
                    for n in range(lo, hi):
                        max_read(b * H, n, FIRST[n], 6 + n % 2)

                for c in range(NCH):
                    cols = slice(c * CH, (c + 1) * CH)
                    for g in range(2):
                        dve.wait_ge(sem("k_high"), b * NCK + (2 * c + g + 1))
                        if c:
                            dve.wait_ge(sem("k_low"), b * NCK + (2 * c - 1 + g))
                        dve.scalar_tensor_tensor(out=r1[g][:, :], in0=ps[:, 2 + g, :], scalar=bk_col[:, g:g + 1],
                                                 in1=kp[:, g, 0, cols], op0=ALU.add, op1=ALU.subtract).then_inc(sem("k_rest"), 1)
                    if c:
                        values(c - 1, 0)
                    for g in range(2):
                        dve.wait_ge(sem("k_mid"), b * NCK + (2 * c + g + 1))
                        dve.wait_ge(sem("k_rest"), b * NCK + (2 * c + g + 1))
                        dve.tensor_tensor(kp[:, g, 2, cols], r1[g][:, :], kp[:, g, 1, cols], ALU.subtract).then_inc(sem("k_low"), 1)
                    if c:
                        values(c - 1, 1)
                    first_tasks(*EARLY_TASKS.get(c, (0, 0)))
                values(NCH - 1, 0)
                values(NCH - 1, 1)

                def steps(H0, g0, lo, hi, first=False, last=False):
                    for s in range(lo, hi):
                        hh, u = divmod(s, UNITS)
                        for i in (LEAD + 2 * s, LEAD + 2 * s + 1):
                            if not (last and i >= HPB * TASKS):
                                max_read(H0, i, i, 4 + i % 2)
                        if u == 3 and not (first and hh == 0):
                            dve.wait_ge(sem("accT_done"), H0 + (hh + 1))
                            dst = o_un[:, ds(g0 * (NQ * (HD + 1)) + (hh - 1) * NQ * (HD + 1), NQ * (HD + 1))]
                            dve.tensor_reduce(dst.rearrange("p (q c) -> p q c", q=NQ),
                                              ps[:, 6 + (hh - 1) % 2, T:2 * T].rearrange("p (q j c) -> p q c j", q=NQ, j=4)[:, :, 0:HD + 1, :],
                                              AX.X, ALU.add).then_inc(sem("o_reduced"), 1)

                Hb = b * H
                first_tasks(EARLY, LEAD)
                steps(Hb, 0, 0, 4, first=True)
                with dve.Fori(0, H // HPB - 1) as g:
                    steps(Hb + g * HPB, g * HPB, 4, 36)
                steps(Hb + (H - HPB), H - HPB, 4, 36, last=True)

                dve.wait_ge(sem("o_reduced"), b * H + (H + 2))
                dve.reciprocal(rden[:, :, :], o_un4[:, :, :, HD]).then_inc(sem("rden_ready"), 1)
                dve.wait_ge(sem("rden_ready"), b + 1)
                dve.tensor_tensor(on[:, ds(b * NQ, NQ), :].rearrange("p q (h e) -> p q h e", h=H), o_un4[:, :, :, 0:HD],
                                  rden[:, :, :].unsqueeze(3).broadcast_to([P, NQ, H, HD]), ALU.mult).then_inc(sem("on_ready"), 1)

            dve.wait_ge(sem("on_ready"), B)
            dve.sem_inc(sem("loop_done"), 1)
            for w in (aqT, avT):
                dve.memset(w[:, :, :, :], 0.0).then_inc(sem("a_zero"), 1)
            pairs = lambda t, i: t[:, 2 * i:2 * i + 2, :]
            bank2 = lambda i: ps[:, i, :].rearrange("p (q e) -> p q e", q=2)
            for i in range(4):
                dve.wait_ge(sem("x_proj"), i + 1)
                dve.tensor_tensor(pairs(x_sb, i), bank2(4 + i), pairs(x_sb, i), ALU.add).then_inc(sem("x1_ready"), 1)
            for m in qd:
                dve.memset(m[:, :, :], 0.0).then_inc(sem("q_zero"), 1)
            dve.wait_ge(sem("x1_ready"), 4)
            normalise("ln2", NT, x_sb, xn2, 0, 0)

            dve.wait_ge(sem("rk_ready"), 4)
            dve.wait_ge(sem("ln2_turned"), 4)
            n = [0]

            def chain(name, ins):
                n[0] += 1
                ins.then_inc(sem(name), 1)
                dve.wait_ge(sem(name), n[0])

            step = lambda ins: chain("key_stats", ins)
            hv = lambda t: t[:, :].rearrange("p (q h) -> p q h", q=NT)
            bc = lambda i: gl_bc[:, i, :].unsqueeze(1).broadcast_to([P, NT, H])
            heads = lambda t: t[:, :, :].rearrange("p q (h e) -> p (q h) e", h=H)
            step(dve.tensor_tensor(ksq[:, :, :], k_sb[:, :, :], k_sb[:, :, :], ALU.mult))
            step(dve.tensor_reduce(sm["ss"][:, :], heads(ksq), AX.X, ALU.add))
            step(dve.tensor_reduce(sm["ks"][:, :], heads(k_sb), AX.X, ALU.add))
            dve.tensor_scalar(sm["ss"][:, :], sm["ss"][:, :], NORM_EPS2, None, ALU.max).then_inc(sem("kn_var"), 1)
            refine("kn", sm["rn"][:, :], sm["ss"][:, :], sm["t"][:, :], 0)
            step(dve.scalar_tensor_tensor(out=sm["kbar"][:, :], in0=sm["ks"][:, :], scalar=1.0 / HD, in1=sm["rn"][:, :],
                                          op0=ALU.mult, op1=ALU.mult))
            step(dve.tensor_tensor(hv(sm["ug"]), hv(sm["kbar"]), bc(0), ALU.mult))
            step(dve.tensor_tensor(hv(sm["ul"]), hv(sm["kbar"]), bc(2), ALU.mult))
            dve.tensor_tensor(hv(sm["ug"]), hv(sm["ug"]), bc(1), ALU.add).then_inc(sem("gates"), 1)
            dve.tensor_tensor(hv(sm["ul"]), hv(sm["ul"]), bc(3), ALU.add).then_inc(sem("gates"), 1)
            dve.wait_ge(sem("gate_exp"), 2)
            step(dve.tensor_scalar(sm["den"][:, :], sm["eg"][:, :], 1.0, None, ALU.add))
            step(dve.scalar_tensor_tensor(out=sm["den"][:, :], in0=sm["el"][:, :], scalar=1.0, in1=sm["den"][:, :],
                                          op0=ALU.add, op1=ALU.mult))
            dve.reciprocal(sm["rho"][:, :], sm["den"][:, :]).then_inc(sem("rho_ready"), 1)
            dve.wait_ge(sem("rho_ready"), 1)
            step(dve.tensor_scalar(sm["t"][:, :], sm["rho"][:, :], -1.0, 1.0, ALU.mult, ALU.add))
            step(dve.tensor_tensor(sm["kscale"][:, :], sm["t"][:, :], sm["rn"][:, :], ALU.mult))
            dve.tensor_tensor(heads(kk), heads(k_sb), sm["kscale"][:, :].unsqueeze(2).broadcast_to([P, NT * H, HD]),
                              ALU.mult).then_inc(sem("kk_ready"), 1)

            dve.wait_ge(sem("starts_ready"), 2)
            flat = lambda t: t.rearrange("p h t -> p (h t)")
            with dve.Fori(0, B // 2) as b2:
                for kb in range(2):
                    b = b2 * 2 + kb

                    def scan(hg):
                        dve.wait_ge(sem(f"rows_loaded{hg}_{kb}"), b2 * 32 + 32)
                        dve.wait_ge(sem("mixed"), b * 4 + (hg + 1))
                        row = rows[kb][:, 4 * hg:4 * hg + 4, :]
                        dve.memset(row[:, :, 0:T + 1:T], 0.0).then_inc(sem("rows_cut"), 1)
                        dve.wait_ge(sem("rows_cut"), b * 4 + (hg + 1))
                        dve.tensor_tensor_scan(flat(dec[hg][:, :, :]), flat(row), flat(starts[:, :, :]), 0.0,
                                               ALU.mult, ALU.add).then_inc(sem("scan_done"), 1)

                    def weight(hg):
                        o = 1 + 3 * (hg % 2)
                        dve.wait_ge(sem("affinity"), b * 4 + (hg + 5))
                        dve.wait_ge(sem("scan_done"), b * 4 + (hg + 1))
                        w1, w2 = dec[hg][:, :, 0:T], dec[hg][:, :, T:T + P]
                        dve.tensor_tensor(w1, w1, ps[:, o:o + 2, :].rearrange("p a (h t) -> p (a h) t", h=2), ALU.mult).then_inc(sem("weighted"), 1)
                        dve.tensor_tensor(w2, w2, ps[:, o + 2, :].rearrange("p (h t) -> p h t", h=4), ALU.mult).then_inc(sem("weighted"), 1)

                    scan(0)
                    scan(1)
                    weight(0)
                    scan(2)
                    weight(1)
                    scan(3)
                    weight(2)
                    weight(3)
            for i in range(4):
                dve.wait_ge(sem("y_proj"), i + 1)
                dve.tensor_tensor(pairs(x_sb, i), bank2(4 + i), pairs(x_sb, i), ALU.add).then_inc(sem("x2_ready"), 1)

            dve.wait_ge(sem("x2_ready"), 4)
            normalise("ln3", NT, x_sb, xn3, 0, 0)
            n[0] = 0
            dve.wait_ge(sem("logits"), 1)
            dve.tensor_copy(lg[:, :, :], ps[:, 6, 0:NT * E].rearrange("p (t e) -> p t e", e=E)).then_inc(sem("logits_read"), 1)
            dve.wait_ge(sem("logits_read"), 1)
            over_e = lambda t: t[:, :].unsqueeze(2).broadcast_to([P, NT, E])
            chain("route", dve.tensor_reduce(mx8[:, :], lg[:, :, :], AX.X, ALU.max))
            dve.tensor_tensor(lg[:, :, :], lg[:, :, :], over_e(mx8), ALU.subtract).then_inc(sem("lg_shifted"), 1)
            dve.wait_ge(sem("lg_exp"), 1)
            chain("route", dve.tensor_reduce(sum8[:, :], pr[:, :, :], AX.X, ALU.add))
            chain("route", dve.reciprocal(sum8[:, :], sum8[:, :]))
            chain("route", dve.tensor_tensor(pr[:, :, :], pr[:, :, :], over_e(sum8), ALU.mult))
            other = lambda t: pr[:, t, :].unsqueeze(1).broadcast_to([P, E, E])
            own = lambda t: pr[:, t, :].unsqueeze(2).broadcast_to([P, E, E])
            dve.wait_ge(sem("lower_ready"), 1)
            for t in range(NT):
                dve.tensor_tensor(ahead[:, t, :, :], other(t), own(t), ALU.is_gt).then_inc(sem("ahead"), 1)
                dve.tensor_tensor(tie[:, t, :, :], other(t), own(t), ALU.is_equal).then_inc(sem("ahead"), 1)
            dve.wait_ge(sem("ahead"), 2 * NT)
            flat2 = lambda t: t[:, :, :, :].rearrange("p t e f -> p t (e f)")
            chain("route", dve.tensor_tensor(flat2(tie), flat2(tie), lower[:, :, :].rearrange("p e f -> p (e f)").unsqueeze(1).broadcast_to([P, NT, E * E]), ALU.mult))
            chain("route", dve.tensor_tensor(flat2(ahead), flat2(ahead), flat2(tie), ALU.add))
            chain("route", dve.tensor_reduce(rank[:, :, :], ahead[:, :, :, :], AX.X, ALU.add))
            chain("route", dve.scalar_tensor_tensor(out=cw[:, :, :].rearrange("p e t -> p t e"), in0=rank[:, :, :], scalar=1.5,
                                           in1=pr[:, :, :], op0=ALU.is_lt, op1=ALU.mult))

            def expert(e, k, shared=False):
                if not shared:
                    dve.wait_ge(sem("down_read"), e * NT + 2)
                    dve.tensor_copy(cwe[k][:, :], cw[:, ds(e, 1), :].rearrange("p o t -> p (o t)")).then_inc(sem("cwe_ready"), 1)
                for half in range(2):
                    dve.wait_ge(sem("silu_done"), e * 2 + (half + 1))
                    dve.wait_ge(sem("down_done"), e * NT + NT)
                    dve.tensor_tensor(hT[k][:, half * 512:(half + 1) * 512], silu[half][:, :], ps[:, 3 + 2 * half, :],
                                      ALU.mult).then_inc(sem("h_ready"), 1)
                for t in range(NT):
                    dve.wait_ge(sem("down_done"), e * NT + (NT + t + 1))
                    if not shared:
                        if t == 0:
                            dve.wait_ge(sem("cwe_ready"), e + 1)
                        dve.scalar_tensor_tensor(out=x_sb[:, t, :], in0=ps[:, 6 + t % 2, 0:D], scalar=cwe[k][:, t:t + 1],
                                                 in1=x_sb[:, t, :], op0=ALU.mult, op1=ALU.add).then_inc(sem("down_read"), 1)
                    else:
                        dve.tensor_tensor(x_sb[:, t, :], x_sb[:, t, :], ps[:, 6 + t % 2, 0:D], ALU.add).then_inc(sem("down_read"), 1)

            with dve.Fori(0, E // 2) as e2:
                for k in range(2):
                    expert(e2 * 2 + k, k)
            expert(E, 0, shared=True)


_INS = ['x', 'ctx_1024', 'mask_BxS2_bf0', 'L0_xattn_Wq', 'L0_xattn_bq', 'L0_xattn_Wkv', 'L0_xattn_bkv', 'L0_xattn_Wout',
        'L0_xattn_bout', 'L0_attn_Wq', 'L0_attn_Wk', 'L0_attn_Wv', 'L0_attn_Wo', 'L0_attn_W_gamma', 'L0_attn_b_gamma',
        'L0_attn_W_lambda', 'L0_attn_b_lambda', 'L0_ffn_gate_w', 'L0_ffn_wg', 'L0_ffn_wu', 'L0_ffn_wd', 'L0_ffn_sg',
        'L0_ffn_su', 'L0_ffn_sd']


def kernel(**inputs):
    import numpy as np
    import concourse.bacc as bacc
    from concourse.bass_utils import run_bass_kernel_spmd

    nc = bacc.Bacc("TRN2", target_bir_lowering=False, num_devices=1)
    arrays, args = {}, []
    for name in _INS:
        a = np.ascontiguousarray(inputs[name])
        arrays[f"in_{name}_dram"] = a
        args.append(nc.dram_tensor(f"in_{name}_dram", a.shape, mybir.dt.from_np(a.dtype), kind="ExternalInput").ap())
    o = nc.dram_tensor("out_0_dram", (B, T, D), F32, kind="ExternalOutput").ap()
    build(nc, *args, o)
    r = run_bass_kernel_spmd(nc, [arrays], core_ids=[0])
    return r.results[0]["out_0_dram"]
```

```python
from contextlib import ExitStack

import concourse.bass as bass
import concourse.mybir as mybir
from concourse.bass import ds

F32 = mybir.dt.float32
F32R = mybir.dt.float32r
BF16 = mybir.dt.bfloat16
U8 = mybir.dt.uint8
ALU = mybir.AluOpType
ACT = mybir.ActivationFunctionType
AX = mybir.AxisListType

P = 128
B, T, D = 4, 256, 256
S = 4096
H, HD = 16, 16
NC = D // P
NQ = T // P
NT = B * NQ
CH = 512
NCH = S // CH
KT = S // P
ROWS = 6 * HD
UNITS = 8
TASKS = 16
HPB = 4
LEAD = 22
SCALE = HD ** -0.5
LN_EPS = 1e-5
NORM_EPS2 = 1e-24
E, F = 8, 128
WEIGHTS_LOADED = 12 * 16
AHEAD = 27
K_PARTS = (0, 0, 0, 1, 1, 2)
Q_PARTS = (2, 1, 0, 1, 0, 0)
CTXT = 4
LAG = 3
HALF = S // 2
LAST = S - CH
FIRST = list(range(8)) + [16, 17] + list(range(8, 16)) + list(range(18, 22))
EARLY_TASKS = {5: [(), (), (0, 1), (1, 2), (2, 3)], 6: [(3, 4), (4, 5), (5, 6), (6, 7)],
               7: [(7, 8), (), (8, 9), (), (9, 10)], 9: [(), (10, 13), (13, 16)], 10: [(), (16, 18)]}
SECOND, THIRD, SPARE = 10, 16, 18
ROW_LOADS = (1 + 6) * 16
FIRST_LOADS = ROW_LOADS + 6 * 16
LOADS = 12 * 16


SPLIT_PASSES = [(w, t, c) for c in range(NC) for w, t in ((0, 0), (0, 1), (1, 0))]


def build(nc, x, ctx_, mask, Wq, bq, Wkv, bkv, Wout, bout, Aq, Ak, Av, Ao, W_g, b_g, W_l, b_l,
          gate_w, wg, wu, wd, sg, su, sd, out):
    with ExitStack() as top:
        sems = {}

        def sem(name):
            if name not in sems:
                sems[name] = top.enter_context(nc.semaphore(name))
            return sems[name]

        def sb(name, shape, dt=F32, scope=top):
            return scope.enter_context(nc.sbuf_tensor(name, shape, dt))

        ps = top.enter_context(nc.psum_tensor("ps", [P, 8, 512], F32))
        rho_dram = nc.dram_tensor("rho_scratch", [NT * H, P], F32)

        x_sb = sb("x_sb", [P, NT, D])
        on = sb("on", [P, NT, D])
        ident = sb("ident", [P, P])
        identb = sb("identb", [P, P], BF16)
        stats = sb("stats", [P, NT, 6])
        mv = sb("mv", [P, NT, 2])
        veps = sb("veps", [P, NT])
        rstd = sb("rstd", [P, NT])
        newt = sb("newt", [P, NT])
        mhalf = sb("mhalf", [P, NT])
        head_row = sb("head_row", [P, P // HD])
        gl_bc = sb("gl_bc", [P, 4, H])
        wout_sb = sb("wout_sb", [P, NC, D])

        loop = ExitStack()
        wq_sb = sb("wq_sb", [P, NC, D], scope=loop)
        wkv = [sb(f"wkv_{n}", [P, NC, 2 * D], F32R, scope=loop) for n in ("high", "low")]
        bq_col = sb("bq_col", [P, 2], scope=loop)
        bk_col = sb("bk_col", [P, 2], scope=loop)
        bv_bc = sb("bv_bc", [P, D], scope=loop)
        mrow = sb("mrow", [KT, B, P], BF16, scope=loop)
        qp = sb("qp", [P, 2, 3, B * T], BF16, scope=loop)
        kslot = [sb(f"kslot{i}", [100, S], BF16, scope=loop) for i in range(4)]
        qslot = [sb(f"qslot{i}", [100, T], BF16, scope=loop) for i in range(4)]
        projection = ExitStack()
        ctxT_low = [sb(f"ctxT_low{i}", [P, NC, CH], F32R, scope=projection) for i in range(3)]
        projection.close()
        pT = [sb(f"pT{i}", [P, 4, T], scope=loop) for i in range(2)]
        vslot = [sb(f"vslot{i}", [P, KT, HD + 1], scope=loop) for i in range(2)]
        accS = sb("accS", [P, T], scope=loop)
        o_un = sb("o_un", [P, H * NQ * (HD + 1)], scope=loop)
        rden = sb("rden", [P, NQ, H], scope=loop)
        pm = sb("pm", [P, 2, NQ, UNITS], scope=loop)
        nm = sb("nm", [P, 2, NQ], scope=loop)
        nmr = sb("nmr", [P, NQ], scope=loop)
        mt = sb("mt", [P, 2, NQ, 4], BF16, scope=loop)
        o_un4 = o_un[:, :].rearrange("p (h q c) -> p q h c", h=H, q=NQ)
        ctx_raw = [sb(f"ctx_raw{i}", [P, 4, D], scope=loop) for i in range(2)]
        ctxT = [sb(f"ctxT{i}", [P, NC, CH], F32R, scope=loop) for i in range(CTXT)]
        ctxT_low.insert(0, sb("ctxT_low3", [P, NC, CH], F32R, scope=loop))
        r1 = [sb(f"r1_{i}", [P, CH], scope=loop) for i in range(2)]
        setup = ExitStack()
        sxn = sb("sxn", [P, NT, D], scope=setup)
        sxnT = sb("sxnT", [P, NC, B * T], scope=setup)
        mask_u8 = sb("mask_u8", [KT, B, P], U8, scope=setup)
        bout_bc = sb("bout_bc", [P, D], scope=setup)
        wkv_sb = sb("wkv_sb", [P, NC, 2 * D], scope=setup)
        setup.close()
        kp = sb("kp", [P, 2, 3, S], BF16, scope=loop)
        vall = sb("vall", [P, H, KT, HD + 1], scope=loop)
        loop.close()

        rec = ExitStack()
        araw = sb("araw", [P, 4, NC, D], scope=rec)
        ao_pad = sb("ao_pad", [P, NC, H, 32], scope=rec)
        onT = sb("onT", [P, NC, B * T], scope=rec)
        aqT = sb("aqT", [P, NC, D], scope=rec)
        avT = sb("avT", [P, NC, D], scope=rec)
        akT = sb("akT", [P, NC, D], scope=rec)
        aoT = sb("aoT", [P, H // HPB, D], scope=rec)
        xn2 = sb("xn2", [P, NT, D], scope=rec)
        xn2T = sb("xn2T", [P, NC, B * T], scope=rec)
        k_sb = sb("k_sb", [P, NT, D], scope=rec)
        kk = sb("kk", [P, NT, D], scope=rec)
        kkb = [sb(f"kkb{i}", [P, NQ, D], scope=rec) for i in range(2)]
        ksq = xn2
        sm = {n: sb("sm_" + n, [P, NT * H], scope=rec)
              for n in ("ss", "ks", "rn", "t", "kbar", "ug", "ul", "eg", "el", "den", "rho", "kscale")}
        rhoT = sb("rhoT", [NT * H, P], scope=rec)
        starts = sb("starts", [P, HPB, T + P], scope=rec)
        rows = [sb(f"rows{i}", [P, H, T + P], scope=rec) for i in range(2)]
        dec = [sb(f"dec{i}", [P, HPB, T + P], scope=rec) for i in range(4)]
        qd = [sb(f"qd{i}", [P, HPB, T], scope=rec) for i in range(4)]
        vT = [sb(f"vT{i}", [P, T], scope=rec) for i in range(2)]
        yT = sb("yT", [P, H // HPB, B * T], scope=rec)
        rec.close()

        moe = ExitStack()
        wraw = [sb(f"wraw{i}", [P, 3, D], scope=moe) for i in range(2)]
        wT = [[sb(f"wT{i}_{n}", [P, 2, D], F32R, scope=moe) for n in ("high", "low")] for i in range(2)]
        wdT = [sb(f"wdT{i}", [P, D], scope=moe) for i in range(2)]
        g_raw = sb("g_raw", [E, D], scope=moe)
        gT = sb("gT", [P, NC, E], scope=moe)
        xn3 = sb("xn3", [P, NT, D], scope=moe)
        xn3T = sb("xn3T", [P, NC, B * T], scope=moe)
        xn3T_parts = [sb(f"xn3T_{n}", [P, NC, B * T], F32R, scope=moe) for n in ("high", "low")]
        lower = sb("lower", [P, E, E], scope=moe)
        lg = sb("lg", [P, NT, E], scope=moe)
        pr = sb("pr", [P, NT, E], scope=moe)
        mx8 = sb("mx8", [P, NT], scope=moe)
        sum8 = sb("sum8", [P, NT], scope=moe)
        ahead = sb("ahead", [P, NT, E, E], scope=moe)
        tie = sb("tie", [P, NT, E, E], scope=moe)
        rank = sb("rank", [P, NT, E], scope=moe)
        cw = sb("cw", [P, E, NT], scope=moe)
        cwe = [sb(f"cwe{i}", [P, NT], scope=moe) for i in range(2)]
        silu = [sb(f"silu{i}", [P, 512], scope=moe) for i in range(2)]
        hT = [sb(f"hT{i}", [P, B * T], scope=moe) for i in range(2)]
        moe.close()

        K_LOADED = 3 * LOADS + LOADS // 2

        def first_bank(n):
            return (4 if n >= SPARE else 6) + n % 2

        def early_range(c, place):
            at = EARLY_TASKS.get(c, [])
            return range(*at[place]) if place < len(at) and at[place] else range(0)

        def context_parts(c):
            return ctxT[c % CTXT], ctxT_low[c % CTXT]

        def context_bank(c):
            return 4 if c == 0 else 0

        def value_bank(c, pair):
            return (0 if c == NCH - 1 else 4) + pair

        block = top.enter_context(nc.Block())
        NCK = 2 * NCH

        @block.sync
        def _(sp):
            sp.dma_start(x_sb[:, :, :], x.rearrange("b (q p) d -> p (b q) d", p=P)).then_inc(sem("x_loaded"), 16)
            loads = [
                (wq_sb[:, :, :], Wq.rearrange("(c p) n -> p c n", p=P)),
                (wkv_sb[:, :, :], Wkv.rearrange("(c p) n -> p c n", p=P)),
                (wout_sb[:, :, :], Wout.rearrange("(c p) n -> p c n", p=P)),
                (bq_col[:, :], bq.rearrange("(g p) -> p g", p=P)),
                (bk_col[:, :], bkv[0:D].rearrange("(g p) -> p g", p=P)),
                (bv_bc[:, :], bkv[D:2 * D].partition_broadcast(P)),
                (bout_bc[:, :], bout.partition_broadcast(P)),
                (mask_u8[:, :, :], mask.rearrange("b (c k) -> c b k", k=P)),
            ] + [(gl_bc[:, i, :], w.partition_broadcast(P)) for i, w in enumerate((W_g, b_g, W_l, b_l))]
            for dst, src in loads:
                sp.dma_start(dst, src, allow_slow_non_contiguous=dst.shape[-1] == 2).then_inc(sem("weights_loaded"), 16)
            assert len(loads) * 16 == WEIGHTS_LOADED

            ctx_v = ctx_.rearrange("b (c t p) d -> p (b c) t d", p=P, t=4)
            with sp.Fori(0, B) as b:
                def key_rows(h, lo, hi, done):
                    slot, g, p0 = h % 4, h // 8, HD * (h % 8)
                    for r, part in enumerate(K_PARTS):
                        sp.dma_start(kslot[slot][r * HD:(r + 1) * HD, lo:hi], kp[p0:p0 + HD, g, part, lo:hi]).then_inc(done, 16)

                def query_rows(h, done):
                    slot, g, p0 = h % 4, h // 8, HD * (h % 8)
                    for r, part in enumerate(Q_PARTS):
                        sp.dma_start(qslot[slot][r * HD:(r + 1) * HD, :], qp[p0:p0 + HD, g, part, ds(b * T, T)]).then_inc(done, 16)

                def load_values(h):
                    if h < 2:
                        sp.wait_ge(sem("v_evacuated"), b * NCK + NCK)
                    else:
                        sp.wait_ge(sem("pv_done"), b * (H * UNITS) + (h - 1) * UNITS + 2)
                    sp.dma_start(vslot[h % 2][:, :, :], vall[:, h, :, :]).then_inc(sem(f"v_loaded{h % 2}"), 16)

                for c in range(NCH):
                    sp.wait_ge(sem("ctx_transposed"), b * NCH + (c + 1))
                    sp.dma_start(ctx_raw[c % 2][:, :, :], ctx_v[:, ds(b * NCH + c, 1), :, :].rearrange(
                        "p o t d -> p (o t) d")).then_inc(sem(f"ctx_loaded{c % 2}"), 16)
                    if 2 <= c < 6:
                        h = c - 2
                        sp.wait_ge(sem("mask_ready"), 1)
                        sp.wait_ge(sem("q_low"), 4)
                        sp.wait_ge(sem("slot_ones"), 9)
                        sp.dma_start(kslot[h][96:97, :].rearrange("o (c k) -> o c k", k=P),
                                     mrow[:, ds(b, 1), :].rearrange("c o k -> c (o k)")).then_inc(sem(f"k_first{h}"), 16)
                        query_rows(h, sem(f"k_first{h}"))
                    if c == 6:
                        sp.wait_ge(sem("k_low"), b * NCK + NCK // 2)
                        key_rows(0, 0, HALF, sem("k_first0"))
                key_rows(1, 0, HALF, sem("k_first1"))
                sp.wait_ge(sem("k_low"), b * NCK + (NCK - 2))
                key_rows(0, HALF, LAST, sem("k_second"))
                sp.wait_ge(sem("k_low"), b * NCK + NCK)
                key_rows(0, LAST, S, sem("k_loaded0"))
                key_rows(1, HALF, S, sem("k_loaded1"))
                load_values(0)
                load_values(1)
                for h in range(2, 4):
                    key_rows(h, 0, S, sem(f"k_loaded{h}"))
                for t in range(1, H - 1):
                    if t + 3 < H:
                        h = t + 3
                        sp.wait_ge(sem("s2_done"), b * (H * UNITS) + (h - 3) * UNITS)
                        key_rows(h, 0, S, sem(f"k_loaded{h % 4}"))
                        query_rows(h, sem(f"k_loaded{h % 4}"))
                    load_values(t + 1)

            sp.wait_ge(sem("loop_done"), 1)
            for i, w in enumerate((Aq, Ak, Av, Ao)):
                sp.dma_start(araw[:, i, :, :], w.rearrange("(c p) n -> p c n", p=P)).then_inc(sem("a_loaded"), 16)
            sp.wait_ge(sem("rhoT_ready"), 1)
            sp.dma_start(rho_dram[:, :], rhoT[:, :]).then_inc(sem("rho_stored"), 16)
            sp.wait_ge(sem("rho_stored"), 16)
            for b in range(B):
                if b >= 2:
                    sp.wait_ge(sem("scan_done"), 4 * (b - 1))
                for hg in range(4):
                    for n, q in enumerate((0, 1, 1)):
                        at = (b * NQ + q) * H + HPB * hg
                        sp.dma_start(rows[b % 2][:, HPB * hg:HPB * (hg + 1), n * P:(n + 1) * P],
                                     rho_dram[at:at + HPB, :].partition_broadcast(P)).then_inc(sem(f"rows_loaded{hg}_{b % 2}"), 16)

            sp.wait_ge(sem("aoT_ready"), 1)
            sp.dma_start(g_raw[:, :], gate_w).then_inc(sem("gate_loaded"), 16)

            def load_expert(i, buf, g3, u3, d3):
                sp.wait_ge(sem("w_transposed"), i + 1)
                done = sem(f"w_loaded{buf}")
                sp.dma_start(wraw[buf][:, 0, :], g3).then_inc(done, 16)
                sp.dma_start(wraw[buf][:, 1, :], u3).then_inc(done, 16)
                sp.dma_start(wraw[buf][:, 2, :].rearrange("p (c f) -> p c f", c=NC),
                             d3.rearrange("(c p) f -> p c f", p=P)).then_inc(done, 16)
            with sp.Fori(0, E // 2) as e2:
                for k in range(2):
                    e = e2 * 2 + k
                    load_expert(e, k, wg[ds(e, 1), :, :].rearrange("o f d -> (o f) d"),
                                wu[ds(e, 1), :, :].rearrange("o f d -> (o f) d"),
                                wd[ds(e, 1), :, :].rearrange("o d f -> (o d) f"))
            load_expert(E, 0, sg, su, sd)
            out_v = out.rearrange("b (q p) d -> p (b q) d", p=P)
            for q in range(4):
                sp.wait_ge(sem("down_read"), E * NT + 2 + (2 * q + 2))
                sp.dma_start(out_v[:, 2 * q:2 * q + 2, :], x_sb[:, 2 * q:2 * q + 2, :]).then_inc(sem("out_stored"), 16)
            sp.wait_ge(sem("out_stored"), 64)

        @block.gpsimd
        def _(pool):
            pool.sem_inc(sem("mt_parts"), 8)
            pool.memset(ident[:, :], 0.0).then_inc(sem("pool_const"), 1)
            pool.memset(identb[:, :], 0.0).then_inc(sem("pool_const"), 1)
            pool.memset(mhalf[:, :], -0.5).then_inc(sem("pool_const"), 1)
            pool.memset(mt[:, :, :, :], 1.0).then_inc(sem("pool_const"), 1)
            pool.wait_ge(sem("pool_const"), 4)
            for m in (ident, identb):
                pool.affine_select(out=m[:, :], in_=m[:, :], compare_op=ALU.not_equal, fill=1.0, base=0, pattern=[[-1, P]],
                                   channel_multiplier=1).then_inc(sem("ident_ready"), 1)
            pool.wait_ge(sem("ident_ready"), 2)
            def inverse_root(name):
                pool.wait_ge(sem(name + "_var"), 1)
                pool.tensor_tensor(rstd[:, :], veps[:, :], mhalf[:, :], ALU.pow).then_inc(sem(name + "_root"), 1)

            inverse_root("ln1")
            pool.memset(head_row[:, :], 1.0).then_inc(sem("head_row"), 1)
            for n, (sign, base) in enumerate(((1, 0), (-1, HD - 1))):
                pool.wait_ge(sem("head_row"), n + 1)
                pool.affine_select(out=head_row[:, :], in_=head_row[:, :], compare_op=ALU.is_ge, fill=0.0, base=base,
                                   pattern=[[-sign * HD, P // HD]], channel_multiplier=sign).then_inc(sem("head_row"), 1)
            pool.wait_ge(sem("head_row"), 3)
            for s in range(4):
                pool.memset(kslot[s][96:100, :], 1.0).then_inc(sem("slot_ones"), 1)
                pool.wait_ge(sem("slot_ones"), 2 * s + 1)
                pool.memset(qslot[s][96:100, :], 1.0).then_inc(sem("slot_ones"), 1)
                pool.wait_ge(sem("slot_ones"), 2 * s + 2)
            pool.memset(vall[:, :, :, HD], 1.0).then_inc(sem("slot_ones"), 1)

            with pool.Fori(0, B) as b:
                for c in range(NCH):
                    cols = slice(c * CH, (c + 1) * CH)
                    for g in range(2):
                        pool.wait_ge(sem("k_mid"), b * NCK + (2 * c + g + 1))
                        if c or g:
                            pool.wait_ge(sem("k_low"), b * NCK + (2 * c + g))
                        pool.tensor_tensor(kp[:, g, 2, cols], r1[g][:, :], kp[:, g, 1, cols], ALU.subtract).then_inc(sem("k_low"), 1)

                def split_max(Hn, par):
                    pool.wait_ge(sem("nm_ready"), Hn + 3)
                    pool.wait_ge(sem("mt_transposed"), Hn + 1)
                    pool.sem_inc(sem("pool_past"), 1)
                    part = sem("mt_parts")
                    pool.tensor_copy(mt[:, par, :, 1], nm[:, par, :]).then_inc(part, 1)
                    pool.wait_ge(part, Hn * 4 + 9)
                    pool.tensor_tensor(nmr[:, :], nm[:, par, :], mt[:, par, :, 1], ALU.subtract).then_inc(part, 1)
                    pool.wait_ge(part, Hn * 4 + 10)
                    pool.sem_inc(sem("pool_past"), 1)
                    pool.tensor_copy(mt[:, par, :, 2], nmr[:, :]).then_inc(part, 1)
                    pool.wait_ge(part, Hn * 4 + 11)
                    pool.tensor_tensor(mt[:, par, :, 3], nmr[:, :], mt[:, par, :, 2], ALU.subtract).then_inc(part, 1)
                with pool.Fori(0, H // 2) as g:
                    for k in range(2):
                        split_max(b * H + (g * 2 + k), k)
            pool.wait_ge(sem("loop_done"), 1)
            pool.memset(starts[:, :, :], 0.0).then_inc(sem("starts0"), 1)
            pool.wait_ge(sem("starts0"), 1)
            for part, w in ((starts[:, :, 0:T], T), (starts[:, :, T:T + P], P)):
                pool.affine_select(out=part, in_=part, compare_op=ALU.not_equal, fill=1.0, base=0,
                                   pattern=[[0, HPB], [-1, w]], channel_multiplier=1).then_inc(sem("starts_ready"), 1)
            inverse_root("ln2")
            inverse_root("ln3")
            pool.wait_ge(sem("x2_ready"), 4)
            pool.memset(lower[:, :, :], 1.0).then_inc(sem("lower0"), 1)
            pool.wait_ge(sem("lower0"), 1)
            pool.affine_select(out=lower[:, :, :], in_=lower[:, :, :], compare_op=ALU.is_gt, fill=0.0, base=0,
                               pattern=[[1, E], [-1, E]], channel_multiplier=0).then_inc(sem("lower_ready"), 1)
            pool.wait_ge(sem("ln3T_lows"), 4)
            pool.tensor_tensor(xn3T[:, :, :], xn3T_parts[0][:, :, :], xn3T_parts[1][:, :, :], ALU.add).then_inc(sem("xn3T_whole"), 1)

        @block.tensor
        def _(pe):
            def transpose(dst, src, idt, **k):
                return pe.matmul(dst, src, idt, start=True, stop=True, is_transpose=True, **k)

            def transpose_all(name, src):
                if name == "on":
                    pe.wait_ge(sem("on_ready"), B)
                for c in range(NC):
                    for half in range(2):
                        for i in range(4):
                            t = half * 4 + i
                            if name != "on":
                                pe.wait_ge(sem(name + "_normed"), t + 1)
                            m = transpose(ps[:, 2 * c + half, i * P:(i + 1) * P], src[:, t, c * P:(c + 1) * P], ident[:, :])
                        m.then_inc(sem(name + "_turned"), 1)

            pe.sem_inc(sem("ctx_transposed"), 2)
            pe.sem_inc(sem("affinity"), 4)
            pe.sem_inc(sem("mixed"), 4)
            pe.sem_inc(sem("pv_done"), 2)
            pe.sem_inc(sem("accT_done"), 1)
            pe.sem_inc(sem("mt_transposed"), 2)
            pe.sem_inc(sem("w_transposed"), 2)
            pe.sem_inc(sem("down_done"), NT)
            pe.sem_inc(sem("wT_lows"), 1)
            pe.wait_ge(sem("ident_ready"), 2)
            transpose_all("ln1", sxn)
            pe.wait_ge(sem("ln1T_ready"), 4)
            pe.wait_ge(sem("weights_loaded"), WEIGHTS_LOADED)
            for g in range(2):
                for half in range(2):
                    i = 2 * g + half
                    for c in range(NC):
                        m = pe.matmul(ps[:, 4 + i, :], wq_sb[:, c, g * P:(g + 1) * P],
                                      sxnT[:, c, half * 512:(half + 1) * 512], start=c == 0, stop=c == NC - 1)
                    m.then_inc(sem("q_proj"), 1)
            pe.wait_ge(sem("wkv_low"), 1)

            def turn(b, c):
                pe.wait_ge(sem(f"ctx_loaded{c % 2}"), b * (8 * NCH) + 16 * (c // 2 + 1))
                if c:
                    pe.wait_ge(sem("ctxT_lows"), b * NCH + c)
                else:
                    pe.wait_ge(sem("max_read"), b * (H * TASKS) + 2)
                for dc in range(NC):
                    for t in range(4):
                        m = transpose(ps[:, context_bank(c) + dc, t * P:(t + 1) * P], ctx_raw[c % 2][:, t, dc * P:(dc + 1) * P], ident[:, :])
                m.then_inc(sem("ctx_transposed"), 1)

            def project_keys(b, c, early=None):
                pe.wait_ge(sem("ctxT_lows"), b * NCH + (c + 1))
                for g in range(2):
                    if c:
                        pe.wait_ge(sem("k_rest"), b * NCK + (2 * c - 1 + g))
                    for n, (wi, ti, dc) in enumerate(SPLIT_PASSES):
                        m = pe.matmul(ps[:, 2 + g, :], wkv[wi][:, dc, g * P:(g + 1) * P], context_parts(c)[ti][:, dc, :],
                                      start=n == 0, stop=n == len(SPLIT_PASSES) - 1)
                    m.then_inc(sem("k_proj"), 1)
                    if early:
                        early(c, 3 + g)

            pe.wait_ge(sem("q_rest"), 4)
            turn(0, 0)
            turn(0, 1)
            project_keys(0, 0)

            def cross_attention(b, more=True):
                def project_values(c):
                    if c == NCH - 1:
                        pe.wait_ge(sem("ctxT_lows"), b * NCH + NCH)
                    for pair in range(2):
                        if c:
                            pe.wait_ge(sem("v_evacuated"), b * NCK + (2 * c - 1 + pair))
                        for j in range(2):
                            t = 2 * pair + j
                            for n, (wi, ti, dc) in enumerate(SPLIT_PASSES):
                                m = pe.matmul(ps[:, value_bank(c, pair), j * D:(j + 1) * D],
                                              context_parts(c)[ti][:, dc, t * P:(t + 1) * P], wkv[wi][:, dc, D:2 * D],
                                              start=n == 0, stop=n == len(SPLIT_PASSES) - 1)
                        m.then_inc(sem("v_proj"), 1)
                        early_tasks(c + LAG, 1 + pair)

                def max_product(H0, n, i, bank):
                    kc, qt = divmod(i % TASKS, NQ)
                    slot = (i // TASKS) % 4
                    pe.wait_ge(sem("max_read"), H0 * TASKS + (n + 1))
                    pe.matmul(ps[:, bank, :], qslot[slot][0:ROWS + 1, qt * P:(qt + 1) * P],
                              kslot[slot][0:ROWS + 1, kc * 512:(kc + 1) * 512], start=True, stop=True
                              ).then_inc(sem("s1_done"), 1)

                def first_tasks(lo, hi):
                    for n in range(lo, hi):
                        if n == 0:
                            pe.wait_ge(sem("slot_ones"), 9)
                            pe.wait_ge(sem("acc_zero"), 1)
                            pe.wait_ge(sem("o_reduced"), b * H + 2)
                        if n in (0, 8):
                            pe.wait_ge(sem(f"k_first{n // 8}"), b * FIRST_LOADS + FIRST_LOADS)
                        if n == SECOND:
                            pe.wait_ge(sem("k_second"), b * (6 * 16) + 6 * 16)
                        if n == THIRD:
                            pe.wait_ge(sem("k_loaded0"), b * K_LOADED + LOADS // 2)
                        max_product(b * H, n, FIRST[n], first_bank(n))

                def early_tasks(c, place):
                    for n in early_range(c, place):
                        first_tasks(n, n + 1)

                for c in range(1, NCH + LAG):
                    if c + 1 < NCH:
                        turn(b, c + 1)
                    early_tasks(c, 0)
                    if c >= LAG:
                        project_values(c - LAG)
                    if c < NCH:
                        project_keys(b, c, early_tasks)

                def max_task(H0, i, g0):
                    hh, k = divmod(i, TASKS)
                    slot, turns = hh % 4, hh // 4
                    if k == 0 or i == LEAD:
                        if slot >= 2:
                            pe.wait_ge(sem(f"k_first{slot}"), b * ROW_LOADS + ROW_LOADS)
                        pe.wait_ge(sem(f"k_loaded{slot}"), b * K_LOADED + (g0 * LOADS + LOADS * turns + LOADS // 2))
                    max_product(H0, i, i, 4 + i % 2)

                def turn_max(H0, hh):
                    pe.wait_ge(sem("mt_parts"), H0 * 4 + (4 * hh + 12))
                    pe.wait_ge(sem("o_reduced"), H0 + (hh + 1))
                    bank = ps[96:100, 6 + hh % 2, 0:P].bitcast(BF16)
                    for qt in range(NQ):
                        m = transpose(bank[:, qt * P:(qt + 1) * P], mt[:, hh % 2, qt, :], identb[:, :], tile_position=(0, 96))
                    m.then_inc(sem("mt_transposed"), 1)

                def steps(H0, g0, lo, hi, first=False, last=False):
                    for s in range(lo, hi):
                        hh, u = divmod(s, UNITS)
                        slot = hh % 4
                        live = not (last and s >= HPB * UNITS)
                        if live:
                            if u == 0:
                                pe.wait_ge(sem("qrow_ready"), H0 + (hh + 1))
                            pe.wait_ge(sem("exp_done"), H0 * UNITS + (s + 1))
                            for j in range(4):
                                kt = 4 * u + j
                                m = pe.matmul(ps[:, 2 * (s % 2) + j // 2, (j % 2) * T:(j % 2 + 1) * T],
                                              kslot[slot][:, kt * P:(kt + 1) * P], qslot[slot][:, :], start=True, stop=True)
                            m.then_inc(sem("s2_done"), 1)
                        tasks = [i for i in (LEAD + 2 * s, LEAD + 2 * s + 1) if not (last and i >= HPB * TASKS)]
                        if tasks:
                            max_task(H0, tasks[0], g0)
                        if not (first and s == 0) and s <= (HPB * UNITS if last else hi):
                            weigh(H0, g0, s - 1)
                        if tasks:
                            max_task(H0, tasks[1], g0)
                        if u == 2 and not (first and hh == 0):
                            pe.wait_ge(sem("acc_copied"), H0 + hh)
                            for qt in range(NQ):
                                m = transpose(ps[:, 6 + (hh - 1) % 2, T + qt * P:T + (qt + 1) * P], accS[:, qt * P:(qt + 1) * P], ident[:, :])
                            m.then_inc(sem("accT_done"), 1)
                        if u == 6 and live and not (last and hh == HPB - 1):
                            turn_max(H0, hh + 1)

                def weigh(H0, g0, s):
                    hh, u = divmod(s, UNITS)
                    pe.wait_ge(sem("exp_done"), H0 * UNITS + (s + 3))
                    if u == 0:
                        pe.wait_ge(sem("o_reduced"), H0 + (hh + 1))
                        pe.wait_ge(sem(f"v_loaded{hh % 2}"), b * (H * 8) + g0 * (HPB * 8) + 16 * (hh // 2 + 1))
                    for j in range(4):
                        m = pe.matmul(ps[32 * j:32 * j + HD + 1, 6 + hh % 2, 0:T], vslot[hh % 2][:, 4 * u + j, :],
                                      pT[s % 2][:, j, :], start=u == 0, stop=u == UNITS - 1, tile_position=(0, 32 * j))
                    m.then_inc(sem("pv_done"), 1)

                Hb = b * H
                pe.wait_ge(sem("v_evacuated"), b * NCK + NCK)
                pe.wait_ge(sem("k_rest"), b * NCK + NCK)
                first_tasks(SPARE, SPARE + 2)
                turn_max(Hb, 0)
                first_tasks(SPARE + 2, LEAD)
                steps(Hb, 0, 0, 4, first=True)
                with pe.Fori(0, H // HPB - 1) as g:
                    steps(Hb + g * HPB, g, 4, 36)
                last = (Hb + (H - HPB), H // HPB - 1)
                steps(*last, 4, AHEAD, last=True)
                if more:
                    turn(b + 1, 0)
                steps(*last, AHEAD, HPB * UNITS + 1, last=True)
                if more:
                    turn(b + 1, 1)
                    project_keys(b + 1, 0)
                steps(*last, HPB * UNITS + 1, 36, last=True)

            with pe.Fori(0, B - 1) as b:
                cross_attention(b)
            cross_attention(B - 1, more=False)

            def token_products(name, left, right, chunks):
                for t in range(NT):
                    for c in range(chunks):
                        m = pe.matmul(ps[:, 4 + t // 2, (t % 2) * D:(t % 2 + 1) * D], left[:, c, t * P:(t + 1) * P], right[:, c, :],
                                      start=c == 0, stop=c == chunks - 1)
                    if t % 2:
                        m.then_inc(sem(name), 1)

            transpose_all("on", on)
            pe.wait_ge(sem("onT_ready"), 4)
            token_products("x_proj", onT, wout_sb, NC)
            pe.wait_ge(sem("a_loaded"), 4 * 16)
            pe.wait_ge(sem("x1_ready"), 4)
            for i in range(3):
                for dc in range(NC):
                    for ec in range(NC):
                        m = transpose(ps[:, 4 + i, dc * D + ec * P:dc * D + (ec + 1) * P],
                                      araw[:, i, ec, dc * P:(dc + 1) * P], ident[:, :])
                m.then_inc(sem("a_turned"), 1)
            transpose_all("ln2", xn2)
            pe.wait_ge(sem("a_ready"), 3)
            pe.wait_ge(sem("ln2T_ready"), 4)
            token_products("rk_proj", xn2T, akT, NC)

            def project_queries(b, g, first=False):
                if not first:
                    pe.wait_ge(sem("rec_q_ready"), b * 2 + g)
                for i, w in enumerate((aqT, avT)):
                    for c in range(NC):
                        m = pe.matmul(ps[:, 0, i * T:(i + 1) * T], w[:, c, g * P:(g + 1) * P], xn2T[:, c, ds(b * T, T)],
                                      start=c == 0, stop=c == NC - 1)
                m.then_inc(sem("qv_proj"), 1)
            project_queries(0, 0, first=True)
            pe.wait_ge(sem("ao_padded"), 3)
            for hg in range(H // HPB):
                for oc in range(NC):
                    m = transpose(ps[:, 1 + hg // 2, (hg % 2) * D + oc * P:(hg % 2) * D + (oc + 1) * P],
                                  ao_pad[:, oc, HPB * hg:HPB * (hg + 1), :].rearrange("p h e -> p (h e)"), ident[:, :])
            m.then_inc(sem("ao_turned"), 1)
            project_queries(0, 1)
            pe.wait_ge(sem("rho_ready"), 1)
            pe.wait_ge(sem("rk_squared"), 4)
            transpose(ps[:, 3, 0:P], sm["rho"][:, :], ident[:, :]).then_inc(sem("rho_turned"), 1)
            pe.wait_ge(sem("rhoT_ready"), 1)
            pe.wait_ge(sem("rk_ready"), 4)
            pe.wait_ge(sem("aoT_ready"), 1)
            pe.wait_ge(sem("mix_zero"), 1)

            def affinity_of(b, hg):
                o = 1 + 3 * (hg % 2)
                pe.wait_ge(sem("rec_q_ready"), b * 2 + (hg // 2 + 1))
                pe.wait_ge(sem("weighted"), b * 8 + (2 * hg + 6))
                for a in range(2):
                    pe.matmul(ps[:, o + a, :], vT[hg // 2][:, 0:P], qd[hg][:, 2 * a:2 * a + 2, :], start=True, stop=True)
                pe.matmul(ps[:, o + 2, :], vT[hg // 2][:, P:T], qd[hg][:, :, P:T], start=True, stop=True
                          ).then_inc(sem("affinity"), 1)

            def batch(b, kb, more=True):
                def mix(hg):
                    pe.wait_ge(sem("weighted"), b * 8 + (2 * hg + 10))
                    pe.wait_ge(sem("y_ready"), b * 4 + (hg + 1))
                    if hg == 0:
                        pe.wait_ge(sem("kkb_ready"), b + 1)
                    w = dec[hg]
                    for h in range(HPB):
                        col = slice((HPB * hg + h) * HD, (HPB * hg + h + 1) * HD)
                        pe.matmul(ps[32 * h:32 * h + HD, 7, 0:T], kkb[kb][:, 0, col], w[:, h, 0:T],
                                  start=True, stop=False, tile_position=(0, 32 * h))
                        m = pe.matmul(ps[32 * h:32 * h + HD, 7, P:T], kkb[kb][:, 1, col], w[:, h, T:T + P],
                                      start=False, stop=True, tile_position=(0, 32 * h))
                    m.then_inc(sem("mixed"), 1)

                affinity_of(b, 2)
                mix(0)
                if more:
                    project_queries(b + 1, 0)
                affinity_of(b, 3)
                mix(1)
                if more:
                    affinity_of(b + 1, 0)
                mix(2)
                if more:
                    project_queries(b + 1, 1)
                    affinity_of(b + 1, 1)
                mix(3)

            affinity_of(0, 0)
            affinity_of(0, 1)
            with pe.Fori(0, B // 2 - 1) as b2:
                batch(b2 * 2, 0)
                batch(b2 * 2 + 1, 1)
            batch(B - 2, 0)
            batch(B - 1, 1, more=False)
            pe.wait_ge(sem("y_ready"), 4 * B + 1)
            pe.wait_ge(sem("weighted"), 8 * B + 8)
            token_products("y_proj", yT, aoT, H // HPB)

            def turn_weights(e, k, nth):
                pe.wait_ge(sem(f"w_loaded{k}"), nth)
                pe.wait_ge(sem("wT_ready"), e * 2 + 2)
                pe.wait_ge(sem("wT_lows"), e + 1)
                for i in range(2):
                    for c in range(NC):
                        transpose(ps[:, 0, (2 * i + c) * P:(2 * i + c + 1) * P], wraw[k][:, i, c * P:(c + 1) * P], ident[:, :])
                for c in range(NC):
                    m = transpose(ps[:, 1, c * P:(c + 1) * P], wraw[k][:, 2, c * P:(c + 1) * P], ident[:, :])
                m.then_inc(sem("w_transposed"), 1)

            def gate_up(e, k, half, i):
                if half == 0 and i == 0:
                    pe.wait_ge(sem("wT_lows"), e + 2)
                if i == 0:
                    pe.wait_ge(sem("h_ready"), e * 2 + (half + 1))
                for n, (wi, ti, c) in enumerate(SPLIT_PASSES):
                    m = pe.matmul(ps[:, 2 + 2 * half + i, :], wT[k][wi][:, i, c * P:(c + 1) * P],
                                  xn3T_parts[ti][:, c, half * 512:(half + 1) * 512],
                                  start=n == 0, stop=n == len(SPLIT_PASSES) - 1)
                if i == 1:
                    m.then_inc(sem("gu_done"), 1)

            def down(e, k, tiles):
                if 0 in tiles:
                    pe.wait_ge(sem("wT_ready"), e * 2 + 4)
                for t in tiles:
                    pe.wait_ge(sem("h_ready"), e * 2 + (t // 4 + 3))
                    pe.wait_ge(sem("down_read"), e * NT + (t + 1))
                    pe.matmul(ps[:, 6 + t % 2, 0:D], hT[k][:, t * P:(t + 1) * P], wdT[k][:, :],
                              start=True, stop=True).then_inc(sem("down_done"), 1)

            def expert(e, k, turns, more=True):
                for n, (half, i) in enumerate(((0, 0), (0, 1), (1, 0), (1, 1))):
                    gate_up(e + 1, 1 - k, half, i)
                    if n == 0 and more:
                        turn_weights(e + 2, k, turns * 48 + 96)
                    down(e, k, (2 * n, 2 * n + 1))

            turn_weights(0, 0, 48)
            pe.wait_ge(sem("gate_loaded"), 16)
            for c in range(NC):
                m = transpose(ps[:, 2, c * E:(c + 1) * E], g_raw[:, c * P:(c + 1) * P], ident[0:E, 0:E])
            m.then_inc(sem("gate_turned"), 1)
            pe.wait_ge(sem("gate_ready"), 1)
            pe.wait_ge(sem("wT_ready"), 4)
            pe.wait_ge(sem("wT_lows"), 2)
            transpose_all("ln3", xn3)
            pe.wait_ge(sem("ln3T_lows"), 4)
            for half, i in ((0, 0), (0, 1), (1, 0), (1, 1)):
                gate_up(0, 0, half, i)
            pe.wait_ge(sem("xn3T_whole"), 1)
            for t in range(NT):
                for c in range(NC):
                    m = pe.matmul(ps[:, 6, t * E:(t + 1) * E], xn3T[:, c, t * P:(t + 1) * P], gT[:, c, :],
                                  start=c == 0, stop=c == NC - 1)
            m.then_inc(sem("logits"), 1)
            turn_weights(1, 1, 48)
            pe.wait_ge(sem("logits_read"), 1)
            with pe.Fori(0, E // 2 - 1) as e2:
                for k in range(2):
                    expert(e2 * 2 + k, k, e2)
            expert(E - 2, 0, E // 2 - 1)
            expert(E - 1, 1, E // 2 - 1, more=False)
            down(E, 0, range(NT))

        @block.scalar
        def _(act):
            def copy(dst, src):
                return act.activation(dst, src, ACT.Copy)

            act.sem_inc(sem("exp_done"), 2)
            act.wait_ge(sem("weights_loaded"), WEIGHTS_LOADED)
            copy(wkv[0][:, :, :], wkv_sb[:, :, :]).then_inc(sem("wkv_high"), 1)
            act.sem_inc(sem("wT_ready"), 2)
            for i in range(4):
                act.wait_ge(sem("ln1_turned"), i + 1)
                copy(sxnT[:, i // 2, (i % 2) * 512:(i % 2 + 1) * 512], ps[:, i, :]).then_inc(sem("ln1T_ready"), 1)
            for i in range(4):
                g, half = divmod(i, 2)
                cols = slice(half * 512, (half + 1) * 512)
                act.wait_ge(sem("q_proj"), i + 1)
                act.activation(qp[:, g, 0, cols], ps[:, 4 + i, :], ACT.Identity, bias=bq_col[:, g:g + 1]).then_inc(sem("q_high"), 1)
                act.wait_ge(sem("q_rest"), i + 1)
                copy(qp[:, g, 1, cols], r1[i % 2][:, :]).then_inc(sem("q_mid"), 1)
            def evacuate(b, c):
                act.wait_ge(sem("ctx_transposed"), b * NCH + (c + 3))
                if c >= CTXT:
                    act.wait_ge(sem("v_proj"), b * NCK + 2 * (c - CTXT + 1))
                copy(ctxT[c % CTXT][:, :, :], ps[:, 0:2, :]).then_inc(sem("ctxT_ready"), 1)

            def key_parts(b, c):
                cols = slice(c * CH, (c + 1) * CH)
                for g in range(2):
                    act.wait_ge(sem("k_proj"), b * NCK + (2 * c + g + 1))
                    act.activation(kp[:, g, 0, cols], ps[:, 2 + g, :], ACT.Identity, bias=bk_col[:, g:g + 1]).then_inc(sem("k_high"), 1)
                for g in range(2):
                    act.wait_ge(sem("k_rest"), b * NCK + (2 * c + g + 1))
                    copy(kp[:, g, 1, cols], r1[g][:, :]).then_inc(sem("k_mid"), 1)

            evacuate(0, 1)
            key_parts(0, 0)

            def cross_attention(b, more=True):
                def values(c, pair):
                    act.wait_ge(sem("v_proj"), b * NCK + (2 * c + pair + 1))
                    kt = 4 * c + 2 * pair
                    copy(vall[:, :, kt:kt + 2, 0:HD].rearrange("p h k e -> p k h e"),
                         ps[:, value_bank(c, pair), :].rearrange("p (k h e) -> p k h e", k=2, h=H)).then_inc(sem("v_evacuated"), 1)

                for c in range(1, NCH + LAG):
                    if c + 1 < NCH:
                        evacuate(b, c + 1)
                    if c >= LAG:
                        values(c - LAG, 0)
                        values(c - LAG, 1)
                    if c < NCH:
                        key_parts(b, c)

                def qrow(H0, hh):
                    act.wait_ge(sem("mt_transposed"), H0 + (hh + 3))
                    copy(qslot[hh % 4][96:100, :], ps[96:100, 6 + hh % 2, 0:P].bitcast(BF16)).then_inc(sem("qrow_ready"), 1)

                def steps(H0, lo, hi, first=False, last=False):
                    for s in range(lo, hi):
                        hh, u = divmod(s, UNITS)
                        live = not (last and s >= HPB * UNITS)
                        if live:
                            act.wait_ge(sem("s2_done"), H0 * UNITS + (s + 1))
                            act.wait_ge(sem("pv_done"), H0 * UNITS + (s + 1))
                            act.activation(pT[s % 2][:, :, :], ps[:, 2 * (s % 2):2 * (s % 2) + 2, :].rearrange(
                                "p a (j t) -> p (a j) t", j=2), ACT.Exp, scale=SCALE).then_inc(sem("exp_done"), 1)
                        if u == 0 and not (first and hh == 0):
                            act.wait_ge(sem("pv_done"), H0 * UNITS + (s + 2))
                            act.wait_ge(sem("accT_done"), H0 + hh)
                            copy(accS[:, :], ps[:, 6 + (hh - 1) % 2, 0:T]).then_inc(sem("acc_copied"), 1)
                        if u == 6 and live and not (last and hh == HPB - 1):
                            qrow(H0, hh + 1)

                Hb = b * H
                qrow(Hb, 0)
                steps(Hb, 0, 4, first=True)
                with act.Fori(0, H // HPB - 1) as g:
                    steps(Hb + g * HPB, 4, 36)
                steps(Hb + (H - HPB), 4, 36, last=True)
                if more:
                    evacuate(b + 1, 1)
                    key_parts(b + 1, 0)

            with act.Fori(0, B - 1) as b:
                cross_attention(b)
            cross_attention(B - 1, more=False)

            def turned(name, dst):
                for i in range(4):
                    act.wait_ge(sem(name + "_turned"), i + 1)
                    copy(dst[:, i // 2, (i % 2) * 512:(i % 2 + 1) * 512], ps[:, i, :]).then_inc(sem(name + "T_ready"), 1)

            turned("on", onT)
            for i, dst in enumerate((aqT, akT, avT)):
                act.wait_ge(sem("a_turned"), i + 1)
                copy(dst[:, :, :], ps[:, 4 + i, :].rearrange("p (c e) -> p c e", c=NC)).then_inc(sem("a_ready"), 1)
            turned("ln2", xn2T)
            for i in range(4):
                act.wait_ge(sem("rk_proj"), i + 1)
                pair = ps[:, 4 + i, :].rearrange("p (q e) -> p q e", q=2)
                copy(k_sb[:, 2 * i:2 * i + 2, :], pair).then_inc(sem("rk_ready"), 1)
                act.activation(ksq[:, 2 * i:2 * i + 2, :], pair, ACT.Square).then_inc(sem("rk_squared"), 1)

            def place(b, g):
                act.wait_ge(sem("qv_proj"), b * 2 + (g + 1))
                act.wait_ge(sem("affinity"), b * 4 + (2 * g + 2))
                for hg in (2 * g, 2 * g + 1):
                    for h in range(HPB):
                        r = HPB * (hg % 2) + h
                        act.activation(qd[hg][:, h, :], ps[:, 0, 0:T], ACT.Copy, scale=head_row[:, r:r + 1]).then_inc(sem("q_placed"), 1)
                copy(vT[g][:, :], ps[:, 0, T:2 * T]).then_inc(sem("rec_q_ready"), 1)

            def key_batch(b, kb):
                act.wait_ge(sem("mixed"), b * 4 + 1)
                copy(kkb[kb][:, :, :], kk[:, ds(b * NQ, NQ), :]).then_inc(sem("kkb_ready"), 1)

            def mixed(b, hg):
                act.wait_ge(sem("mixed"), b * 4 + (hg + 5))
                copy(yT[:, hg, ds(b * T, T)], ps[:, 7, 0:T]).then_inc(sem("y_ready"), 1)

            def batch(b, kb, more=True):
                mixed(b, 0)
                if more:
                    place(b + 1, 0)
                mixed(b, 1)
                mixed(b, 2)
                if more:
                    place(b + 1, 1)
                    key_batch(b + 1, 1 - kb)
                mixed(b, 3)

            act.wait_ge(sem("head_row"), 3)
            place(0, 0)
            act.wait_ge(sem("kn_var"), 1)
            act.activation(sm["t"][:, :], sm["ss"][:, :], ACT.Sqrt).then_inc(sem("kn_sqrt"), 1)
            act.wait_ge(sem("gates"), 2)
            act.activation(sm["eg"][:, :], sm["ug"][:, :], ACT.Exp, scale=-1.0).then_inc(sem("gate_exp"), 1)
            act.activation(sm["el"][:, :], sm["ul"][:, :], ACT.Exp).then_inc(sem("gate_exp"), 1)
            act.wait_ge(sem("rho_turned"), 1)
            copy(rhoT[:, :], ps[:, 3, 0:P]).then_inc(sem("rhoT_ready"), 1)
            place(0, 1)
            act.wait_ge(sem("ao_turned"), 1)
            copy(aoT[:, :, :], ps[:, 1:3, :].rearrange("p b (c e) -> p (b c) e", c=2)).then_inc(sem("aoT_ready"), 1)
            act.sem_inc(sem("y_ready"), 1)
            act.wait_ge(sem("kk_ready"), 1)
            key_batch(0, 0)
            with act.Fori(0, B // 2 - 1) as b2:
                batch(b2 * 2, 0)
                batch(b2 * 2 + 1, 1)
            batch(B - 2, 0)
            batch(B - 1, 1, more=False)

            def gate_up_weights(e, k, reused=True):
                act.wait_ge(sem("w_transposed"), e + 3)
                if reused:
                    act.wait_ge(sem("gu_done"), e * 2 - 2)
                copy(wT[k][0][:, :, :], ps[:, 0, :].rearrange("p (i f) -> p i f", i=2)).then_inc(sem("wT_ready"), 1)

            def down_weights(e, k, reused=True):
                if reused:
                    act.wait_ge(sem("down_done"), e * NT)
                copy(wdT[k][:, :], ps[:, 1, 0:D]).then_inc(sem("wT_ready"), 1)

            def gates(e):
                for half in range(2):
                    act.wait_ge(sem("gu_done"), e * 2 + (half + 1))
                    act.wait_ge(sem("h_ready"), e * 2 + (half + 1))
                    act.activation(silu[half][:, :], ps[:, 2 + 2 * half, :], ACT.Silu).then_inc(sem("silu_done"), 1)

            gate_up_weights(0, 0, reused=False)
            down_weights(0, 0, reused=False)
            act.wait_ge(sem("gate_turned"), 1)
            copy(gT[:, :, :], ps[:, 2, 0:NC * E].rearrange("p (c e) -> p c e", c=NC)).then_inc(sem("gate_ready"), 1)
            turned("ln3", xn3T_parts[0])
            gates(0)
            gate_up_weights(1, 1, reused=False)
            down_weights(1, 1, reused=False)
            act.wait_ge(sem("lg_shifted"), 1)
            act.activation(pr[:, :, :], lg[:, :, :], ACT.Exp).then_inc(sem("lg_exp"), 1)
            with act.Fori(0, E // 2 - 1) as e2:
                for k in range(2):
                    gate_up_weights(e2 * 2 + (k + 2), k)
                    gates(e2 * 2 + (k + 1))
                    down_weights(e2 * 2 + (k + 2), k)
            gate_up_weights(E, 0)
            gates(E - 1)
            down_weights(E, 0)
            gates(E)

        @block.vector
        def _(dve):
            def statistics(name, src, tiles):
                for t in tiles:
                    dve.bn_stats(stats[:, t, :], src[:, t, :]).then_inc(sem(name + "_stats"), 1)

            def normalise(name, n, src, dst, base):
                dve.wait_ge(sem(name + "_stats"), base * n + n)
                dve.sem_inc(sem("dve_past"), 1)
                for t in range(n):
                    dve.bn_aggr(mv[:, t, :], stats[:, t, :]).then_inc(sem(name + "_aggr"), 1)
                dve.wait_ge(sem(name + "_aggr"), base * n + n)
                dve.tensor_scalar(veps[:, 0:n], mv[:, 0:n, 1], LN_EPS, None, ALU.add).then_inc(sem(name + "_var"), 1)
                refine(name, rstd[:, 0:n], veps[:, 0:n], newt[:, 0:n], base)
                for t in range(n):
                    dve.tensor_scalar(dst[:, t, :], src[:, t, :], mv[:, t, 0:1], rstd[:, t:t + 1], ALU.subtract,
                                      ALU.mult).then_inc(sem(name + "_normed"), 1)

            def refine(name, y, v, tmp, base):
                step = sem(name + "_newton")
                dve.wait_ge(sem(name + "_root"), base + 1)
                dve.tensor_tensor(tmp, y, y, ALU.mult).then_inc(step, 1)
                dve.wait_ge(step, base * 4 + 1)
                dve.tensor_tensor(tmp, tmp, v, ALU.mult).then_inc(step, 1)
                dve.wait_ge(step, base * 4 + 2)
                dve.tensor_scalar(tmp, tmp, -0.5, 1.5, ALU.mult, ALU.add).then_inc(step, 1)
                dve.wait_ge(step, base * 4 + 3)
                dve.tensor_tensor(y, y, tmp, ALU.mult).then_inc(step, 1)
                dve.wait_ge(step, base * 4 + 4)

            dve.sem_inc(sem("max_read"), 2)
            dve.sem_inc(sem("nm_ready"), 2)
            dve.sem_inc(sem("o_reduced"), 2)
            dve.sem_inc(sem("h_ready"), 2)
            dve.sem_inc(sem("down_read"), 2)
            dve.sem_inc(sem("weighted"), 8)
            dve.wait_ge(sem("x_loaded"), 16)
            statistics("ln1", x_sb, range(NT))
            normalise("ln1", NT, x_sb, sxn, 0)
            dve.wait_ge(sem("weights_loaded"), WEIGHTS_LOADED)
            dve.wait_ge(sem("wkv_high"), 1)
            dve.tensor_tensor(wkv[1][:, :, :], wkv_sb[:, :, :], wkv[0][:, :, :], ALU.subtract).then_inc(sem("wkv_low"), 1)
            dve.wait_ge(sem("ln1_normed"), NT)
            dve.tensor_tensor(x_sb[:, :, :], x_sb[:, :, :], bout_bc[:, :].unsqueeze(1).broadcast_to([P, NT, D]),
                              ALU.add).then_inc(sem("xb_ready"), 1)
            dve.tensor_scalar(mrow[:, :, :], mask_u8[:, :, :], -3e38, 10.0, ALU.mult, ALU.mult).then_inc(sem("mask_ready"), 1)
            for i in range(4):
                g, half = divmod(i, 2)
                cols = slice(half * 512, (half + 1) * 512)
                dve.wait_ge(sem("q_high"), i + 1)
                dve.scalar_tensor_tensor(out=r1[i % 2][:, :], in0=ps[:, 4 + i, :], scalar=bq_col[:, g:g + 1],
                                         in1=qp[:, g, 0, cols], op0=ALU.add, op1=ALU.subtract).then_inc(sem("q_rest"), 1)
                dve.wait_ge(sem("q_mid"), i + 1)
                dve.wait_ge(sem("q_rest"), i + 1)
                dve.tensor_tensor(qp[:, g, 2, cols], r1[i % 2][:, :], qp[:, g, 1, cols], ALU.subtract).then_inc(sem("q_low"), 1)
            dve.wait_ge(sem("q_rest"), 4)
            dve.wait_ge(sem("q_low"), 4)
            dve.memset(ps[:, 6:8, :], 0.0).then_inc(sem("acc_zero"), 1)

            def context_low(b, c):
                high, low = context_parts(c)
                turned = ps[:, context_bank(c):context_bank(c) + 2, :]
                if c == 0:
                    dve.wait_ge(sem("ctx_transposed"), b * NCH + 3)
                    dve.tensor_copy(high[:, :, :], turned).then_inc(sem("ctxT_ready"), 1)
                dve.wait_ge(sem("ctxT_ready"), b * NCH + (c + 1))
                dve.tensor_tensor(low[:, :, :], turned, high[:, :, :], ALU.subtract).then_inc(sem("ctxT_lows"), 1)

            def key_rest(b, c, g):
                cols = slice(c * CH, (c + 1) * CH)
                dve.wait_ge(sem("k_high"), b * NCK + (2 * c + g + 1))
                if c:
                    dve.wait_ge(sem("k_low"), b * NCK + (2 * c - 1 + g))
                dve.scalar_tensor_tensor(out=r1[g][:, :], in0=ps[:, 2 + g, :], scalar=bk_col[:, g:g + 1],
                                         in1=kp[:, g, 0, cols], op0=ALU.add, op1=ALU.subtract).then_inc(sem("k_rest"), 1)

            def first_chunk(b):
                context_low(b, 1)
                key_rest(b, 0, 0)
                key_rest(b, 0, 1)

            context_low(0, 0)
            first_chunk(0)

            def cross_attention(b, more=True):
                def max_read(H0, n, i, bank):
                    hh, k = divmod(i, TASKS)
                    kc, qt = divmod(k, NQ)
                    par = hh % 2
                    if k == 0:
                        dve.wait_ge(sem("nm_ready"), H0 + (hh + 1))
                    dve.wait_ge(sem("s1_done"), H0 * TASKS + (n + 1))
                    dve.tensor_reduce(pm[:, par, qt, kc:kc + 1], ps[:, bank, :], AX.X, ALU.max).then_inc(sem("max_read"), 1)
                    if k == TASKS - 1:
                        dve.wait_ge(sem("max_read"), H0 * TASKS + (n + 3))
                        dve.wait_ge(sem("mt_parts"), H0 * 4 + (hh * 4 + 4))
                        dve.tensor_reduce(nm[:, par, :], pm[:, par, :, :], AX.X, ALU.max, negate=True).then_inc(sem("nm_ready"), 1)

                def first_tasks(lo, hi):
                    for n in range(lo, hi):
                        max_read(b * H, n, FIRST[n], first_bank(n))

                def early_tasks(c, place):
                    for n in early_range(c, place):
                        first_tasks(n, n + 1)

                for c in range(1, NCH):
                    early_tasks(c, 0)
                    if c + 1 < NCH:
                        context_low(b, c + 1)
                    early_tasks(c, 1)
                    early_tasks(c, 2)
                    key_rest(b, c, 0)
                    early_tasks(c, 3)
                    key_rest(b, c, 1)
                    early_tasks(c, 4)
                for c in range(NCH, NCH + LAG):
                    for place in range(3):
                        early_tasks(c, place)

                def steps(H0, g0, lo, hi, first=False, last=False):
                    for s in range(lo, hi):
                        hh, u = divmod(s, UNITS)
                        for i in (LEAD + 2 * s, LEAD + 2 * s + 1):
                            if not (last and i >= HPB * TASKS):
                                max_read(H0, i, i, 4 + i % 2)
                        if u == 3 and not (first and hh == 0):
                            dve.wait_ge(sem("accT_done"), H0 + (hh + 1))
                            dst = o_un[:, ds(g0 * (NQ * (HD + 1)) + (hh - 1) * NQ * (HD + 1), NQ * (HD + 1))]
                            dve.tensor_reduce(dst.rearrange("p (q c) -> p q c", q=NQ),
                                              ps[:, 6 + (hh - 1) % 2, T:2 * T].rearrange("p (q j c) -> p q c j", q=NQ, j=4)[:, :, 0:HD + 1, :],
                                              AX.X, ALU.add).then_inc(sem("o_reduced"), 1)

                Hb = b * H
                first_tasks(SPARE, LEAD)
                steps(Hb, 0, 0, 4, first=True)
                with dve.Fori(0, H // HPB - 1) as g:
                    steps(Hb + g * HPB, g * HPB, 4, 36)
                last = (Hb + (H - HPB), H - HPB)
                steps(*last, 4, AHEAD + 1, last=True)
                if more:
                    context_low(b + 1, 0)
                    first_chunk(b + 1)
                steps(*last, AHEAD + 1, 36, last=True)

                dve.wait_ge(sem("o_reduced"), b * H + (H + 2))
                dve.reciprocal(rden[:, :, :], o_un4[:, :, :, HD]).then_inc(sem("rden_ready"), 1)
                dve.wait_ge(sem("rden_ready"), b + 1)
                dve.tensor_tensor(on[:, ds(b * NQ, NQ), :].rearrange("p q (h e) -> p q h e", h=H), o_un4[:, :, :, 0:HD],
                                  rden[:, :, :].unsqueeze(3).broadcast_to([P, NQ, H, HD]), ALU.mult).then_inc(sem("on_mean"), 1)
                dve.wait_ge(sem("on_mean"), b + 1)
                mean = on[:, ds(b * NQ, NQ), :]
                dve.tensor_tensor(mean, mean, bv_bc[:, :].unsqueeze(1).broadcast_to([P, NQ, D]), ALU.add).then_inc(sem("on_ready"), 1)

            with dve.Fori(0, B - 1) as b:
                cross_attention(b)
            cross_attention(B - 1, more=False)

            dve.wait_ge(sem("on_ready"), B)
            dve.sem_inc(sem("loop_done"), 1)
            dve.memset(ao_pad[:, :, :, :], 0.0).then_inc(sem("ao_padded"), 1)
            dve.wait_ge(sem("ao_padded"), 1)
            dve.wait_ge(sem("a_loaded"), 4 * 16)
            for c in range(NC):
                dve.tensor_copy(ao_pad[:, c, :, 0:HD], araw[:, 3, c, :].rearrange("p (h e) -> p h e", h=H)).then_inc(sem("ao_padded"), 1)
            pairs = lambda t, i: t[:, 2 * i:2 * i + 2, :]
            bank2 = lambda i: ps[:, i, :].rearrange("p (q e) -> p q e", q=2)
            for i in range(4):
                dve.wait_ge(sem("x_proj"), i + 1)
                dve.tensor_tensor(pairs(x_sb, i), bank2(4 + i), pairs(x_sb, i), ALU.add).then_inc(sem("x1_ready"), 1)
                dve.wait_ge(sem("x1_ready"), i + 1)
                statistics("ln2", x_sb, (2 * i, 2 * i + 1))
            normalise("ln2", NT, x_sb, xn2, 0)

            n = [0]

            def chain(name, ins):
                n[0] += 1
                ins.then_inc(sem(name), 1)
                dve.wait_ge(sem(name), n[0])

            step = lambda ins: chain("key_stats", ins)
            hv = lambda t: t[:, :].rearrange("p (q h) -> p q h", q=NT)
            bc = lambda i: gl_bc[:, i, :].unsqueeze(1).broadcast_to([P, NT, H])
            heads = lambda t: t.rearrange("p q (h e) -> p (q h) e", h=H)
            for i in range(4):
                cols = slice(2 * H * i, 2 * H * (i + 1))
                dve.wait_ge(sem("rk_ready"), i + 1)
                dve.tensor_reduce(sm["ks"][:, cols], heads(k_sb[:, 2 * i:2 * i + 2, :]), AX.X, ALU.add).then_inc(sem("k_sums"), 1)
                dve.wait_ge(sem("rk_squared"), i + 1)
                dve.tensor_reduce(sm["ss"][:, cols], heads(ksq[:, 2 * i:2 * i + 2, :]), AX.X, ALU.add).then_inc(sem("k_sums"), 1)
            dve.wait_ge(sem("k_sums"), 8)
            dve.tensor_scalar(sm["ss"][:, :], sm["ss"][:, :], NORM_EPS2, None, ALU.max).then_inc(sem("kn_var"), 1)
            dve.wait_ge(sem("kn_sqrt"), 1)
            dve.reciprocal(sm["rn"][:, :], sm["t"][:, :]).then_inc(sem("kn_root"), 1)
            refine("kn", sm["rn"][:, :], sm["ss"][:, :], sm["t"][:, :], 0)
            step(dve.scalar_tensor_tensor(out=sm["kbar"][:, :], in0=sm["ks"][:, :], scalar=1.0 / HD, in1=sm["rn"][:, :],
                                          op0=ALU.mult, op1=ALU.mult))
            step(dve.tensor_tensor(hv(sm["ug"]), hv(sm["kbar"]), bc(0), ALU.mult))
            step(dve.tensor_tensor(hv(sm["ul"]), hv(sm["kbar"]), bc(2), ALU.mult))
            dve.tensor_tensor(hv(sm["ug"]), hv(sm["ug"]), bc(1), ALU.add).then_inc(sem("gates"), 1)
            dve.tensor_tensor(hv(sm["ul"]), hv(sm["ul"]), bc(3), ALU.add).then_inc(sem("gates"), 1)
            dve.wait_ge(sem("gate_exp"), 2)
            step(dve.tensor_scalar(sm["den"][:, :], sm["eg"][:, :], 1.0, None, ALU.add))
            step(dve.scalar_tensor_tensor(out=sm["den"][:, :], in0=sm["el"][:, :], scalar=1.0, in1=sm["den"][:, :],
                                          op0=ALU.add, op1=ALU.mult))
            dve.reciprocal(sm["rho"][:, :], sm["den"][:, :]).then_inc(sem("rho_ready"), 1)
            dve.wait_ge(sem("rho_ready"), 1)
            step(dve.tensor_scalar(sm["t"][:, :], sm["rho"][:, :], -1.0, 1.0, ALU.mult, ALU.add))
            step(dve.tensor_tensor(sm["kscale"][:, :], sm["t"][:, :], sm["rn"][:, :], ALU.mult))
            dve.tensor_tensor(heads(kk[:, :, :]), heads(k_sb[:, :, :]), sm["kscale"][:, :].unsqueeze(2).broadcast_to([P, NT * H, HD]),
                              ALU.mult).then_inc(sem("kk_ready"), 1)

            dve.wait_ge(sem("starts_ready"), 2)
            flat = lambda t: t.rearrange("p h t -> p (h t)")

            def scan(b, kb, turns, hg):
                dve.wait_ge(sem(f"rows_loaded{hg}_{kb}"), turns * 48 + 48)
                dve.wait_ge(sem("mixed"), b * 4 + (hg + 1))
                row = rows[kb][:, 4 * hg:4 * hg + 4, :]
                dve.memset(row[:, :, 0:T + 1:T], 0.0).then_inc(sem("rows_cut"), 1)
                dve.wait_ge(sem("rows_cut"), b * 4 + (hg + 1))
                dve.tensor_tensor_scan(flat(dec[hg][:, :, :]), flat(row), flat(starts[:, :, :]), 0.0,
                                       ALU.mult, ALU.add).then_inc(sem("scan_done"), 1)

            def weight(b, hg):
                o = 1 + 3 * (hg % 2)
                dve.wait_ge(sem("affinity"), b * 4 + (hg + 5))
                dve.wait_ge(sem("scan_done"), b * 4 + (hg + 1))
                w1, w2 = dec[hg][:, :, 0:T], dec[hg][:, :, T:T + P]
                dve.tensor_tensor(w1, w1, ps[:, o:o + 2, :].rearrange("p a (h t) -> p (a h) t", h=2), ALU.mult).then_inc(sem("weighted"), 1)
                dve.tensor_tensor(w2, w2, ps[:, o + 2, :].rearrange("p (h t) -> p h t", h=4), ALU.mult).then_inc(sem("weighted"), 1)

            def batch(b, kb, turns, more=True):
                for hg in range(4):
                    weight(b, hg)
                    if hg < 3:
                        scan(b, kb, turns, hg + 1)
                    elif more:
                        scan(b + 1, 1 - kb, turns + kb, 0)

            dve.memset(ps[:, 7, :], 0.0).then_inc(sem("mix_zero"), 1)
            scan(0, 0, 0, 0)
            with dve.Fori(0, B // 2 - 1) as b2:
                batch(b2 * 2, 0, b2)
                batch(b2 * 2 + 1, 1, b2)
            batch(B - 2, 0, B // 2 - 1)
            batch(B - 1, 1, B // 2 - 1, more=False)
            for i in range(4):
                dve.wait_ge(sem("y_proj"), i + 1)
                dve.tensor_tensor(pairs(x_sb, i), bank2(4 + i), pairs(x_sb, i), ALU.add).then_inc(sem("x2_ready"), 1)
                dve.wait_ge(sem("x2_ready"), i + 1)
                statistics("ln3", x_sb, (2 * i, 2 * i + 1))

            def weights_low(e, k):
                dve.wait_ge(sem("wT_ready"), e * 2 + 3)
                dve.tensor_tensor(wT[k][1][:, :, :], ps[:, 0, :].rearrange("p (i f) -> p i f", i=2), wT[k][0][:, :, :],
                                  ALU.subtract).then_inc(sem("wT_lows"), 1)

            weights_low(0, 0)
            normalise("ln3", NT, x_sb, xn3, 0)
            for i in range(4):
                part = (slice(None), i // 2, slice((i % 2) * 512, (i % 2 + 1) * 512))
                dve.wait_ge(sem("ln3T_ready"), i + 1)
                dve.tensor_tensor(xn3T_parts[1][part], ps[:, i, :], xn3T_parts[0][part], ALU.subtract).then_inc(sem("ln3T_lows"), 1)
            def values_of(e, k, halves, first=False):
                for half in halves:
                    dve.wait_ge(sem("silu_done"), e * 2 + (half + 1))
                    if not first:
                        dve.wait_ge(sem("down_done"), e * NT)
                    dve.tensor_tensor(hT[k][:, half * 512:(half + 1) * 512], silu[half][:, :], ps[:, 3 + 2 * half, :],
                                      ALU.mult).then_inc(sem("h_ready"), 1)

            values_of(0, 0, range(2), first=True)
            n[0] = 0
            dve.wait_ge(sem("logits"), 1)
            dve.tensor_copy(lg[:, :, :], ps[:, 6, 0:NT * E].rearrange("p (t e) -> p t e", e=E)).then_inc(sem("logits_read"), 1)
            dve.wait_ge(sem("logits_read"), 1)
            over_e = lambda t: t[:, :].unsqueeze(2).broadcast_to([P, NT, E])
            chain("route", dve.tensor_reduce(mx8[:, :], lg[:, :, :], AX.X, ALU.max))
            dve.tensor_tensor(lg[:, :, :], lg[:, :, :], over_e(mx8), ALU.subtract).then_inc(sem("lg_shifted"), 1)
            weights_low(1, 1)
            dve.wait_ge(sem("lg_exp"), 1)
            chain("route", dve.tensor_reduce(sum8[:, :], pr[:, :, :], AX.X, ALU.add))
            chain("route", dve.reciprocal(sum8[:, :], sum8[:, :]))
            chain("route", dve.tensor_tensor(pr[:, :, :], pr[:, :, :], over_e(sum8), ALU.mult))
            other = lambda t: pr[:, t, :].unsqueeze(1).broadcast_to([P, E, E])
            own = lambda t: pr[:, t, :].unsqueeze(2).broadcast_to([P, E, E])
            dve.wait_ge(sem("lower_ready"), 1)
            for t in range(NT):
                dve.tensor_tensor(ahead[:, t, :, :], other(t), own(t), ALU.is_gt).then_inc(sem("ahead"), 1)
                dve.tensor_tensor(tie[:, t, :, :], other(t), own(t), ALU.is_equal).then_inc(sem("ahead"), 1)
            dve.wait_ge(sem("ahead"), 2 * NT)
            flat2 = lambda t: t[:, :, :, :].rearrange("p t e f -> p t (e f)")
            chain("route", dve.tensor_tensor(flat2(tie), flat2(tie), lower[:, :, :].rearrange("p e f -> p (e f)").unsqueeze(1).broadcast_to([P, NT, E * E]), ALU.mult))
            chain("route", dve.tensor_tensor(flat2(ahead), flat2(ahead), flat2(tie), ALU.add))
            chain("route", dve.tensor_reduce(rank[:, :, :], ahead[:, :, :, :], AX.X, ALU.add))
            chain("route", dve.scalar_tensor_tensor(out=cw[:, :, :].rearrange("p e t -> p t e"), in0=rank[:, :, :], scalar=1.5,
                                           in1=pr[:, :, :], op0=ALU.is_lt, op1=ALU.mult))

            def add(e, k, tiles, shared=False):
                if not shared and 0 in tiles:
                    dve.wait_ge(sem("down_read"), e * NT + 2)
                    dve.tensor_copy(cwe[k][:, :], cw[:, ds(e, 1), :].rearrange("p o t -> p (o t)")).then_inc(sem("cwe_ready"), 1)
                for t in tiles:
                    dve.wait_ge(sem("down_done"), e * NT + (NT + t + 1))
                    if not shared:
                        if t == 0:
                            dve.wait_ge(sem("cwe_ready"), e + 1)
                        dve.scalar_tensor_tensor(out=x_sb[:, t, :], in0=ps[:, 6 + t % 2, 0:D], scalar=cwe[k][:, t:t + 1],
                                                 in1=x_sb[:, t, :], op0=ALU.mult, op1=ALU.add).then_inc(sem("down_read"), 1)
                    else:
                        dve.tensor_tensor(x_sb[:, t, :], x_sb[:, t, :], ps[:, 6 + t % 2, 0:D], ALU.add).then_inc(sem("down_read"), 1)

            def expert(e, k, more=True):
                add(e, k, (0, 1))
                if more:
                    weights_low(e + 2, k)
                add(e, k, (2, 3))
                values_of(e + 1, 1 - k, (0,))
                add(e, k, (4, 5, 6, 7))
                values_of(e + 1, 1 - k, (1,))

            with dve.Fori(0, E // 2 - 1) as e2:
                for k in range(2):
                    expert(e2 * 2 + k, k)
            expert(E - 2, 0)
            expert(E - 1, 1, more=False)
            add(E, 0, range(NT), shared=True)


_INS = ['x', 'ctx_1024', 'mask_BxS2_bf0', 'L0_xattn_Wq', 'L0_xattn_bq', 'L0_xattn_Wkv', 'L0_xattn_bkv', 'L0_xattn_Wout',
        'L0_xattn_bout', 'L0_attn_Wq', 'L0_attn_Wk', 'L0_attn_Wv', 'L0_attn_Wo', 'L0_attn_W_gamma', 'L0_attn_b_gamma',
        'L0_attn_W_lambda', 'L0_attn_b_lambda', 'L0_ffn_gate_w', 'L0_ffn_wg', 'L0_ffn_wu', 'L0_ffn_wd', 'L0_ffn_sg',
        'L0_ffn_su', 'L0_ffn_sd']


def kernel(**inputs):
    import numpy as np
    import concourse.bacc as bacc
    from concourse.bass_utils import run_bass_kernel_spmd

    nc = bacc.Bacc("TRN2", target_bir_lowering=False, num_devices=1)
    arrays, args = {}, []
    for name in _INS:
        a = np.ascontiguousarray(inputs[name])
        arrays[f"in_{name}_dram"] = a
        args.append(nc.dram_tensor(f"in_{name}_dram", a.shape, mybir.dt.from_np(a.dtype), kind="ExternalInput").ap())
    o = nc.dram_tensor("out_0_dram", (B, T, D), F32, kind="ExternalOutput").ap()
    build(nc, *args, o)
    r = run_bass_kernel_spmd(nc, [arrays], core_ids=[0])
    return r.results[0]["out_0_dram"]
```
